# Optimizing a Trainium2 kernel written in Bass

```python
import numpy as np
import jax
import jax.numpy as jnp

def _softmax(x, axis=-1):
    return jax.nn.softmax(x, axis=axis)

def _gelu(x):
    return jax.nn.gelu(x, approximate=True)

def _silu(x):
    return jax.nn.silu(x)

def _sigmoid(x):
    return jax.nn.sigmoid(x)

def _layernorm(x, axis=-1, eps=1e-05):
    m = jnp.mean(x, axis=axis, keepdims=True)
    v = jnp.var(x, axis=axis, keepdims=True)
    return (x - m) / jnp.sqrt(v + eps)

def _scatter_add(tgt, idx, src, axis=0):
    return tgt.at[idx].add(src)

def _segment_sum(src, seg, n):
    return jax.ops.segment_sum(src, seg, n)
kernel_name = 'mk_macaron_d1_jaxref_r2_805341'

def setup_inputs(seed: int=0):
    np.random.seed(seed)
    _w = jnp.asarray

    def _L0_attn_setup():
        import jax, jax.numpy as jnp
        import numpy as np
        LN_EPS = 1e-05

        def _layernorm(x, w, b):
            mu = jnp.mean(x, axis=-1, keepdims=True)
            var = jnp.mean(jnp.square(x - mu), axis=-1, keepdims=True)
            return (x - mu) * jax.lax.rsqrt(var + LN_EPS) * w + b

        def _s4d(u, log_tau, log_dt, mix, D):
            B, C, T = u.shape
            tau = jax.nn.softplus(log_tau)
            dt = jax.nn.softplus(log_dt)
            t = jnp.arange(T, dtype=jnp.float32)
            E = jnp.exp(-(tau * dt)[:, None] * t[None, :])
            E = jax.lax.stop_gradient(E)
            K = mix @ E
            n = 2 * T
            Uf = jnp.fft.rfft(u, n=n, axis=-1)
            Kf = jnp.fft.rfft(K, n=n, axis=-1)
            y = jnp.fft.irfft(Uf * Kf[None], n=n, axis=-1)[..., :T]
            return y + D[None, :, None] * u
        key = jax.random.key(seed)
        ks = jax.random.split(key, 8)
        B, T, C, N = (4, 2048, 512, 64)
        H = 4 * C
        x = jax.random.normal(ks[0], (B, T, C), dtype=jnp.float32)
        log_tau = jnp.zeros((N,), dtype=jnp.float32)
        log_dt = jnp.zeros((), dtype=jnp.float32)
        mix = jax.random.normal(ks[1], (C, N), dtype=jnp.float32) * 0.02
        D = jnp.ones((C,), dtype=jnp.float32)
        norm1_w = jnp.ones((C,), dtype=jnp.float32)
        norm1_b = jnp.zeros((C,), dtype=jnp.float32)
        norm2_w = jnp.ones((C,), dtype=jnp.float32)
        norm2_b = jnp.zeros((C,), dtype=jnp.float32)
        fc1_w = jax.random.normal(ks[2], (H, C), dtype=jnp.float32) * 0.02
        fc1_b = jnp.zeros((H,), dtype=jnp.float32)
        fc2_w = jax.random.normal(ks[3], (C, H), dtype=jnp.float32) * 0.02
        fc2_b = jnp.zeros((C,), dtype=jnp.float32)
        return {'x': x, 'log_tau': log_tau, 'log_dt': log_dt, 'mix': mix, 'D': D, 'norm1_w': norm1_w, 'norm1_b': norm1_b, 'norm2_w': norm2_w, 'norm2_b': norm2_b, 'fc1_w': fc1_w, 'fc1_b': fc1_b, 'fc2_w': fc2_w, 'fc2_b': fc2_b}
    _L0_attn_in = _L0_attn_setup()

    def _L0_ffn_setup():
        import jax, jax.numpy as jnp
        import numpy as np
        B, N, D = (4, 1024, 512)
        SPARSITY = 0.01
        key = jax.random.key(seed)
        k1, k2, k3 = jax.random.split(key, 3)
        x = jax.random.normal(k1, (B, N, D), dtype=jnp.float32)
        spatial = jax.random.normal(k2, (D, D), dtype=jnp.float32) * 0.02
        freq = jnp.fft.fft(spatial, axis=-1)
        k = int(D * SPARSITY)
        mag = jnp.abs(freq)
        kth = jax.lax.top_k(mag, k)[0][:, -1:]
        w_sparse = jnp.where(mag >= kth, freq, 0.0 + 0j)
        bias = jax.random.normal(k3, (D,), dtype=jnp.float32) * 0.01
        return {'x': x, 'w_freq_real': jnp.real(w_sparse).astype(jnp.float32), 'w_freq_imag': jnp.imag(w_sparse).astype(jnp.float32), 'bias': bias}
    _L0_ffn_in = _L0_ffn_setup()
    _d = {'L0_attn_x': _L0_attn_in['x'], 'L0_attn_log_tau': _L0_attn_in['log_tau'], 'L0_attn_log_dt': _L0_attn_in['log_dt'], 'L0_attn_mix': _L0_attn_in['mix'], 'L0_attn_D': _L0_attn_in['D'], 'L0_attn_norm1_w': _L0_attn_in['norm1_w'], 'L0_attn_norm1_b': _L0_attn_in['norm1_b'], 'L0_attn_norm2_w': _L0_attn_in['norm2_w'], 'L0_attn_norm2_b': _L0_attn_in['norm2_b'], 'L0_attn_fc1_w': _L0_attn_in['fc1_w'], 'L0_attn_fc1_b': _L0_attn_in['fc1_b'], 'L0_attn_fc2_w': _L0_attn_in['fc2_w'], 'L0_attn_fc2_b': _L0_attn_in['fc2_b'], 'L0_ffn_w_freq_real': _L0_ffn_in['w_freq_real'], 'L0_ffn_w_freq_imag': _L0_ffn_in['w_freq_imag'], 'L0_ffn_bias': _L0_ffn_in['bias']}
    _x0 = _d['L0_attn_x']
    _d['L0_attn_x'] = jax.random.normal(jax.random.fold_in(jax.random.key(seed), 1), (4, 2048, 512), dtype=_x0.dtype)
    del _x0
    return _d

def reference(L0_attn_x, L0_attn_log_tau, L0_attn_log_dt, L0_attn_mix, L0_attn_D, L0_attn_norm1_w, L0_attn_norm1_b, L0_attn_norm2_w, L0_attn_norm2_b, L0_attn_fc1_w, L0_attn_fc1_b, L0_attn_fc2_w, L0_attn_fc2_b, L0_ffn_w_freq_real, L0_ffn_w_freq_imag, L0_ffn_bias):

    def _L0_attn_ref(x, log_tau, log_dt, mix, D, norm1_w, norm1_b, norm2_w, norm2_b, fc1_w, fc1_b, fc2_w, fc2_b):
        import jax, jax.numpy as jnp
        import numpy as np
        LN_EPS = 1e-05

        def _layernorm(x, w, b):
            mu = jnp.mean(x, axis=-1, keepdims=True)
            var = jnp.mean(jnp.square(x - mu), axis=-1, keepdims=True)
            return (x - mu) * jax.lax.rsqrt(var + LN_EPS) * w + b

        def _s4d(u, log_tau, log_dt, mix, D):
            B, C, T = u.shape
            tau = jax.nn.softplus(log_tau)
            dt = jax.nn.softplus(log_dt)
            t = jnp.arange(T, dtype=jnp.float32)
            E = jnp.exp(-(tau * dt)[:, None] * t[None, :])
            E = jax.lax.stop_gradient(E)
            K = mix @ E
            n = 2 * T
            Uf = jnp.fft.rfft(u, n=n, axis=-1)
            Kf = jnp.fft.rfft(K, n=n, axis=-1)
            y = jnp.fft.irfft(Uf * Kf[None], n=n, axis=-1)[..., :T]
            return y + D[None, :, None] * u
        h = _layernorm(x, norm1_w, norm1_b)
        h2 = _s4d(jnp.swapaxes(h, 1, 2), log_tau, log_dt, mix, D)
        x = x + jnp.swapaxes(h2, 1, 2)
        g = _layernorm(x, norm2_w, norm2_b)
        g = jax.nn.gelu(g @ fc1_w.T + fc1_b, approximate=False)
        g = g @ fc2_w.T + fc2_b
        return x + g

    def _L0_ffn_ref(x, w_freq_real, w_freq_imag, bias):
        import jax, jax.numpy as jnp
        import numpy as np
        B, N, D = (4, 1024, 512)
        SPARSITY = 0.01
        w = jax.lax.complex(w_freq_real, w_freq_imag)
        x_freq = jnp.fft.fft(x, axis=-1)
        y_freq = jnp.einsum('bnd,do->bno', x_freq, w)
        y = jnp.real(jnp.fft.ifft(y_freq, axis=-1))
        return y + bias
    x = L0_attn_x
    x = x + 0.5 * _L0_ffn_ref(_layernorm(x, axis=-1), L0_ffn_w_freq_real, L0_ffn_w_freq_imag, L0_ffn_bias)
    x = x + _L0_attn_ref(_layernorm(x, axis=-1), L0_attn_log_tau, L0_attn_log_dt, L0_attn_mix, L0_attn_D, L0_attn_norm1_w, L0_attn_norm1_b, L0_attn_norm2_w, L0_attn_norm2_b, L0_attn_fc1_w, L0_attn_fc1_b, L0_attn_fc2_w, L0_attn_fc2_b)
    x = x + 0.5 * _L0_ffn_ref(_layernorm(x, axis=-1), L0_ffn_w_freq_real, L0_ffn_w_freq_imag, L0_ffn_bias)
    return x

_drawn_inputs = setup_inputs


def setup_inputs(seed=0):
    import zlib

    import numpy as np

    out = dict(_drawn_inputs(seed))
    spreads = {'L0_attn_log_tau': (0.0, 0.8),
     'L0_attn_D': (1.0, 0.2),
     'L0_attn_norm1_w': (1.0, 0.2),
     'L0_attn_norm1_b': (0.0, 0.274),
     'L0_attn_norm2_w': (1.0, 0.6),
     'L0_attn_norm2_b': (0.0, 0.8),
     'L0_attn_fc1_b': (0.0, 0.602),
     'L0_attn_fc2_b': (0.0, 0.301)}
    factors = {'L0_ffn_bias': 8.0}
    for name, (base, spread) in spreads.items():
        noise = np.random.default_rng([zlib.crc32(name.encode()), seed]).standard_normal(out[name].shape)
        drawn = base * np.exp(spread * noise) if base else spread * noise
        out[name] = jnp.asarray(drawn.astype(out[name].dtype))
    for name, factor in factors.items():
        out[name] = (out[name] * factor).astype(out[name].dtype)
    return out
```

```python
from contextlib import ExitStack

import numpy as np

import concourse.bass as bass
from concourse import mybir

ALU = mybir.AluOpType
ACT = mybir.ActivationFunctionType
F32 = mybir.dt.float32
F16 = mybir.dt.float16
I32 = mybir.dt.int32
AX_X = mybir.AxisListType.X
RMAX = bass.bass_isa.ReduceOp.max

P = 128
BATCH, TIME, C, HID, NST = 4, 2048, 512, 2048, 64
KC = C // P
HC = HID // P
TILES = BATCH * TIME // P
PER_BATCH = TIME // P
GT = 4
GROUPS = TILES // GT
PAIRS = GROUPS // 2
CB = 16
CBLOCKS = C // CB
OC = 8
BLK = 128
BLOCKS = C // BLK
TAPROWS = 2 * P - 1
COPIES = 16
EPS = 1e-5
REG = 8192


def broadcast_rows(ap, n, parts=P):
    return bass.AP(tensor=ap.tensor, offset=0, ap=[[0, parts], [1, n]])


def build(nc, x, wr, wi, ffn_bias, fc1t, fc2t, fc1b, fc2b, n1w, n1b, n2w, n2b, dskip, mixt, log_tau, log_dt,
          cos_t, sin_t, ncos_t, out):
    x1_dram = nc.dram_tensor("x1_scratch", (TILES * P, C), F32, kind="Internal").ap()
    y_dram = nc.dram_tensor("y_scratch", (TILES, P, C), F32, kind="Internal").ap()
    taps_one = nc.dram_tensor("taps_scratch", (CBLOCKS, TAPROWS, 2 * CB), F16, kind="Internal").ap()
    taps_dram = nc.dram_tensor("taps_copies", (COPIES, CBLOCKS * TAPROWS * 2 * CB), F16, kind="Internal").ap()
    w1_dram = nc.dram_tensor("w1_scratch", (P, 2 * KC * HID), F16, kind="Internal").ap()
    w2_dram = nc.dram_tensor("w2_scratch", (P, 2 * KC * HID), F16, kind="Internal").ap()

    with ExitStack() as ctx:
        def sb(name, shape, dt):
            return ctx.enter_context(nc.sbuf_tensor(name, shape, dt))

        def sem(name):
            return ctx.enter_context(nc.semaphore(name))

        arena = sb("arena", [P, 5 * REG], F32)

        def area(start, cols):
            return arena[:, start:start + cols]

        ident = sb("ident", [P, P], F32)
        m_parts = sb("m_parts", [P, 2, KC, C], F16)
        ring = sb("ring", [P, 4, C], F32)
        taps_a = sb("taps_a", [P, P, 2, CB], F16)
        taps_b = sb("taps_b", [P, P, 2, CB], F16)
        half_bias = sb("half_bias", [P, C], F32)
        w1s = sb("w1s", [P, C], F32)
        b1s = sb("b1s", [P, C], F32)
        to_state = sb("to_state", [P, 2, P], F16)
        from_state = sb("from_state", [P, 2, P], F16)
        carry = sb("carry", [P, C], F32)
        mix_s = sb("mix_s", [P, C], F32)
        state_parts = sb("state_parts", [P, 2, C], F16)
        alpha1 = sb("alpha1", [P, TILES], F32)
        beta1 = sb("beta1", [P, TILES], F32)
        mv = sb("mv", [P, 2, GT, 2], F32)
        bn = sb("bn", [P, 2, GT, 6], F32)
        va = sb("va", [P, 8, GT], F32)
        mhalf = sb("mhalf", [P, GT], F32)
        peak = sb("peak", [P, 8], F32)
        peak_all = sb("peak_all", [P, 8], F32)
        sc = sb("sc", [P, 24], F32)
        bounds = sb("bounds", [P, 8], F32)
        ubias = sb("ubias", [P, GT], F32)
        b1p = sb("b1p", [P, HC], F32)
        colsb = sb("colsb", [P, HC + 2 * KC], F32)
        psum = ctx.enter_context(nc.psum_tensor("psum", [P, 8, 512], F32))

        xbuf = [area(i * GT * C, GT * C).rearrange("p (j c) -> p j c", j=GT) for i in range(2)]
        x1buf = [area((2 + i) * GT * C, GT * C).rearrange("p (j c) -> p j c", j=GT) for i in range(2)]
        odd = taps_b[:, :, :, :].rearrange("p a b c -> p (a b c)")
        zt = odd[:, 0:2048].rearrange("p (r s k t) -> p r s k t", r=2, s=2, k=KC)
        uring = odd[:, 2048:4096].bitcast(F32).rearrange("p (r c) -> p r c", r=2)
        u_all = area(REG, 4 * REG).bitcast(F16).rearrange("p (b s c t) -> p b s c t", b=BLOCKS, s=2, c=BLK)
        u_flat = area(REG, 4 * REG).bitcast(F16)

        def table(i):
            return area(REG + i * KC * C, KC * C).rearrange("p (k n) -> p k n", k=KC)

        cos_sb, sin_sb, ncos_sb, wr_sb, wi_sb, at_re, at_im, m_full = [table(i) for i in range(8)]
        wfull = area(3 * REG, REG)
        wfull1 = wfull.rearrange("p (k h) -> p k h", k=KC)
        wsplit = area(4 * REG, REG).bitcast(F16)
        flat_ring = ring[:, :, :].rearrange("p a b -> p (a b)")
        logs = flat_ring[:, 0:66]
        tmp_a = flat_ring[:, 66:132]
        tmp_b = flat_ring[:, 132:198]
        neg_a = flat_ring[:, 198:264]
        steps = flat_ring[:, 264:392]
        left = flat_ring[:, 392:393]
        onehot = flat_ring[0:1, 400:528]
        e_taps = flat_ring[:, 528:656]
        e_out = flat_ring[:, 656:784]
        e_in = flat_ring[:, 784:848]
        e_tile = flat_ring[:, 848:849]
        drow = flat_ring[0:1, 1024:1536]
        taps_a_flat = taps_a[:, :, :, :].rearrange("p a b c -> p (a b c)")
        taps_out = taps_a_flat[:, 0:1024]
        taps_zero = taps_a_flat[:, 1024:2048]

        scan_out = [ring[:, i, :] for i in range(2)]
        weighted = [ring[:, 2 + i, :] for i in range(2)]
        taps = [taps_a, taps_b]

        w1_sb = area(0, REG).bitcast(F16).rearrange("p (s k h) -> p s k h", s=2, k=KC)
        w2_sb = area(REG, REG).bitcast(F16).rearrange("p (s h n) -> p s h n", s=2, h=HC)
        hid = area(2 * REG, REG).bitcast(F16).rearrange("p (s h t) -> p s h t", s=2, h=HC)
        at3 = 3 * REG
        rbuf = [area(at3 + i * GT * C, GT * C).rearrange("p (j c) -> p j c", j=GT) for i in range(2)]
        x2buf = [area(at3 + (2 + i) * GT * C, GT * C).rearrange("p (j c) -> p j c", j=GT) for i in range(2)]
        at4 = 4 * REG
        ybuf = area(at4, 2048).rearrange("p (j c) -> p j c", j=GT)
        gt = area(at4 + 2048, 2048).bitcast(F16).rearrange("p (s k t) -> p s k t", s=2, k=KC)
        z3t = area(at4 + 4096, 2048).bitcast(F16).rearrange("p (j s k t) -> p j s k t", j=GT, s=2, k=KC)
        h32 = area(at4 + 6144, 2048).rearrange("p (r t) -> p r t", r=4)
        fc2_bias = b1s[:, :]
        z3 = ring

        def bank(i):
            return psum[:, i, :]

        def scale(i):
            return sc[:, i:i + 1]

        S_U, S_K, S_W1, S_W2, S_H, S_M = range(6)
        C_Y, C_W1, C_2, C_M, C_MIX = range(8, 13)
        C_H = 16

        smalls_loaded = sem("smalls_loaded")
        tables_loaded = sem("tables_loaded")
        fc1_loaded, fc2_loaded = sem("fc1_loaded"), sem("fc2_loaded")
        fc1_stored, fc2_stored = sem("fc1_stored"), sem("fc2_stored")
        taps_stored, taps_copied = sem("taps_stored"), sem("taps_copied")
        pool_set = sem("pool_set")
        peaks_reduced = sem("peaks_reduced")
        prep_v = sem("prep_v")
        prep_a = sem("prep_a")
        prep_pe = sem("prep_pe")
        bounds_ready, gate = sem("bounds_ready"), sem("gate")

        x_loaded = [sem("x_loaded0"), sem("x_loaded1")]
        x1_stored = [sem("x1_stored0"), sem("x1_stored1")]
        x_bn, x_aggr, x_var, x_rstd, x_coef = [sem(n) for n in ("x_bn", "x_aggr", "x_var", "x_rstd", "x_coef")]
        z_ready, zt_psum, zt_high, zt_low = [sem(n) for n in ("z_ready", "zt_psum", "zt_high", "zt_low")]
        ffn_psum, xb_ready, x1_ready = sem("ffn_psum"), sem("xb_ready"), sem("x1_ready")
        x1_bn, x1_aggr, x1_var, x1_rstd = [sem(n) for n in ("x1_bn", "x1_aggr", "x1_var", "x1_rstd")]
        v_var0, v_var, v_rstd, u_coef = sem("v_var0"), sem("v_var"), sem("v_rstd"), sem("u_coef")
        u_norm, u_weighted, u_done, u_high, u_low = [sem(n) for n in
                                                     ("u_norm", "u_weighted", "u_done", "u_high", "u_low")]

        taps_loaded = [sem("taps_loaded0"), sem("taps_loaded1")]
        state_psum, state_scanned, state_mixed = sem("state_psum"), sem("state_scanned"), sem("state_mixed")
        state_high, state_low, state_zero = sem("state_high"), sem("state_low"), sem("state_zero")
        y_psum, y_staged = sem("y_psum"), sem("y_staged")
        y_stored = [sem(f"y_stored{b}") for b in range(BLOCKS)]

        w1_loaded, w2_loaded, fc2b_loaded = sem("w1_loaded"), sem("w2_loaded"), sem("fc2b_loaded")
        yg_loaded = sem("yg_loaded")
        r_loaded = [sem("r_loaded0"), sem("r_loaded1")]
        out_stored = [sem("out_stored0"), sem("out_stored1")]
        xm_sum, xm_bn, xm_aggr, xm_var, xm_rstd, xm_coef = [sem(n) for n in
                                                            ("xm_sum", "xm_bn", "xm_aggr", "xm_var", "xm_rstd",
                                                             "xm_coef")]
        r_sum, r_ready, z2_ready = sem("r_sum"), sem("r_ready"), sem("z2_ready")
        gt_psum, gt_high, gt_low = sem("gt_psum"), sem("gt_high"), sem("gt_low")
        fc1_psum, h_ready, h_high, h_low = sem("fc1_psum"), sem("h_ready"), sem("h_high"), sem("h_low")
        fc2_psum, x2_ready = sem("fc2_psum"), sem("x2_ready")
        x2_bn, x2_aggr, x2_var, x2_rstd, x2_coef = [sem(n) for n in
                                                    ("x2_bn", "x2_aggr", "x2_var", "x2_rstd", "x2_coef")]
        z3_ready, z3t_psum, z3t_high, z3t_low = [sem(n) for n in ("z3_ready", "z3t_psum", "z3t_high", "z3t_low")]
        x2b_ready, ffn2_psum, x3_ready = sem("x2b_ready"), sem("ffn2_psum"), sem("x3_ready")

        def each_group(eng, step):
            step(0, 0, 0)
            step(1, 0, 1)
            with eng.Fori(1, PAIRS - 1) as pair:
                step(2 * pair, pair, 0)
                step(2 * pair + 1, pair, 1)
            step(GROUPS - 2, PAIRS - 1, 0)
            step(GROUPS - 1, PAIRS - 1, 1)

        def is_first(g):
            return isinstance(g, int) and g == 0

        def is_last(g):
            return isinstance(g, int) and g == GROUPS - 1

        def rows(dram, g):
            return dram[bass.ds(g * (GT * P), GT * P), :].rearrange("(j p) c -> p j c", j=GT)

        N_SMALLS = 13
        V_STEPS = ("nx sp dt q_high q_low p_high p_low carry peaks0 bound0 e0 r0 scales0 vecs k_high k_low mixw "
                   "fc1bias fc1w peaks1 bound1 e1 r1 scales1 fc1high fc1low peaks2 e2 r2 scales2 fc2high fc2low "
                   "peaks3 e3 r3 scales3 mhigh mlow").split()
        V = {name: i + 1 for i, name in enumerate(V_STEPS)}
        A_STEPS = "exp ln e_taps e_out e_in e_tile at0 at1 at2 at3 at4 at5 at6 at7 m0 m1 m2 m3".split()
        A = {name: i + 1 for i, name in enumerate(A_STEPS)}
        E_STEPS = "taps at0 at1 at2 at3 at4 at5 at6 at7 fc1bias m0 m1 m2 m3".split()
        E = {name: i + 1 for i, name in enumerate(E_STEPS)}

        block = ctx.enter_context(nc.Block())

        @block.sync
        def _(sp):
            for half in range(2):
                sp.dma_start(mix_s[half * NST:(half + 1) * NST, :], mixt).then_inc(smalls_loaded, 16)
                sp.dma_start(logs[half * NST:(half + 1) * NST, 64:65], log_tau).then_inc(smalls_loaded, 16)
            sp.dma_start(logs[:, 0:64], broadcast_rows(log_tau, NST)).then_inc(smalls_loaded, 16)
            sp.dma_start(logs[:, 65:66], broadcast_rows(log_dt, 1)).then_inc(smalls_loaded, 16)
            sp.dma_start(drow, dskip).then_inc(smalls_loaded, 16)
            sp.dma_start(colsb[:, 0:HC], fc1b).then_inc(smalls_loaded, 16)
            sp.dma_start(colsb[:, HC:HC + KC], n2w).then_inc(smalls_loaded, 16)
            sp.dma_start(colsb[:, HC + KC:HC + 2 * KC], n2b).then_inc(smalls_loaded, 16)
            sp.dma_start(half_bias[:, :], broadcast_rows(ffn_bias, C)).then_inc(smalls_loaded, 16)
            sp.dma_start(w1s[:, :], broadcast_rows(n1w, C)).then_inc(smalls_loaded, 16)
            sp.dma_start(b1s[:, :], broadcast_rows(n1b, C)).then_inc(smalls_loaded, 16)
            for dst, src in ((wr_sb, wr), (wi_sb, wi), (cos_sb, cos_t), (sin_sb, sin_t), (ncos_sb, ncos_t)):
                sp.dma_start(dst, src.rearrange("(k p) n -> p k n", p=P)).then_inc(tables_loaded, 16)
            sp.dma_start(wfull1, fc1t.rearrange("(k p) h -> p k h", p=P)).then_inc(fc1_loaded, 16)
            for i in range(2):
                sp.dma_start(xbuf[i], rows(x, i)).then_inc(x_loaded[i], 16)
            sp.wait_ge(pool_set, 2)
            sp.dma_start(taps_one[:, 0:P - 1, :].rearrange("b j n -> j b n"),
                         taps_zero[0:P - 1, :].rearrange("p (b n) -> p b n", b=CBLOCKS)).then_inc(taps_stored, 16)
            sp.wait_ge(prep_v, V["k_low"])
            sp.dma_start(taps_one[:, P - 1:TAPROWS, :].rearrange("b j n -> j b n"),
                         taps_out.rearrange("p (b n) -> p b n", b=CBLOCKS)).then_inc(taps_stored, 16)
            sp.wait_ge(taps_stored, 32)
            sp.dma_start(taps_dram, bass.AP(tensor=taps_one.tensor, offset=0,
                                            ap=[[0, COPIES], [1, CBLOCKS * TAPROWS * 2 * CB]]))\
              .then_inc(taps_copied, 16)
            sp.wait_ge(prep_v, V["fc1low"])
            sp.dma_start(w1_dram, wsplit).then_inc(fc1_stored, 16)
            sp.dma_start(wfull, fc2t.rearrange("(h p) n -> p h n", p=P)).then_inc(fc2_loaded, 16)
            sp.wait_ge(prep_v, V["fc2low"])
            sp.dma_start(w2_dram, wsplit).then_inc(fc2_stored, 16)

            def step(g, pair, par):
                sp.wait_ge(x1_ready, 4 * g + 4)
                if not (isinstance(g, int) and g >= GROUPS - 2):
                    sp.dma_start(xbuf[par], rows(x, g + 2)).then_inc(x_loaded[par], 16)
                sp.dma_start(rows(x1_dram, g), x1buf[par]).then_inc(x1_stored[par], 16)
            each_group(sp, step)

            def load_taps(cb, par):
                dst = taps[par][:, :, :, :].rearrange("p a b c -> p (a b c)")
                copy, row, per = CBLOCKS * TAPROWS * 2 * CB, 2 * CB, P // COPIES
                src = bass.AP(tensor=taps_dram.tensor, offset=(cb * TAPROWS + P - 1) * row,
                              ap=[[copy - per * row, COPIES], [-row, per], [1, P * row]])
                sp.dma_start(dst, src).then_inc(taps_loaded[par], 16)

            sp.wait_ge(taps_copied, 16)
            load_taps(0, 0)
            sp.wait_ge(ffn_psum, TILES)
            sp.wait_ge(u_high, TILES)
            sp.wait_ge(u_low, TILES)
            load_taps(1, 1)
            for blk in range(BLOCKS):
                last = blk == BLOCKS - 1
                for cb in range(8 * blk, 8 * blk + (6 if last else 8)):
                    sp.wait_ge(y_psum, 2 * cb + 2)
                    load_taps(cb + 2, cb % 2)
                sp.wait_ge(y_staged, (blk + 1) * BLK // OC)
                stage = area(blk * REG, REG).rearrange("p (t c) -> p t c", t=TILES)
                sp.dma_start(y_dram[:, :, blk * BLK:(blk + 1) * BLK].rearrange("t p c -> p t c"), stage)\
                  .then_inc(y_stored[blk], 16)
                if blk == 1:
                    sp.wait_ge(fc1_stored, 16)
                    sp.wait_ge(y_stored[0], 16)
                    sp.dma_start(area(0, REG).bitcast(F16), w1_dram).then_inc(w1_loaded, 16)
                if blk == 2:
                    sp.wait_ge(fc2_stored, 16)
                    sp.wait_ge(y_stored[1], 16)
                    sp.dma_start(area(REG, REG).bitcast(F16), w2_dram).then_inc(w2_loaded, 16)

            for b in range(BLOCKS):
                sp.wait_ge(y_stored[b], 16)
            for i in range(2):
                sp.wait_ge(x1_stored[i], 16 * PAIRS)

            def load_y(g):
                sp.dma_start(ybuf, y_dram[bass.ds(g * GT, GT), :, :].rearrange("j p c -> p j c"))\
                  .then_inc(yg_loaded, 16)

            def load_r(g, par):
                sp.dma_start(rbuf[par], rows(x1_dram, g)).then_inc(r_loaded[par], 16)

            load_y(0)
            load_r(0, 0)
            sp.dma_start(fc2_bias, broadcast_rows(fc2b, C)).then_inc(fc2b_loaded, 16)

            def step(g, pair, par):
                if not is_last(g):
                    sp.wait_ge(gt_psum, 4 * g + 4)
                    load_y(g + 1)
                    if not is_first(g):
                        sp.wait_ge(x2_ready, 4 * g)
                    load_r(g + 1, 1 - par)
                if not is_first(g):
                    sp.wait_ge(x3_ready, 4 * g)
                    sp.dma_start(rows(out, g - 1), x2buf[1 - par]).then_inc(out_stored[1 - par], 16)
            each_group(sp, step)
            sp.wait_ge(x3_ready, TILES)
            sp.dma_start(rows(out, GROUPS - 1), x2buf[1]).then_inc(out_stored[1], 16)
            for i in range(2):
                sp.wait_ge(out_stored[i], 16 * PAIRS)

        @block.gpsimd
        def _(pool):
            pool.memset(peak[:, :], 0.0).then_inc(pool_set, 1)
            pool.memset(taps_zero, 0.0).then_inc(pool_set, 1)
            pool.memset(mhalf[:, :], -0.5).then_inc(pool_set, 1)
            pool.memset(onehot, 0.0).then_inc(pool_set, 1)
            pool.memset(ident[:, :], 0.0).then_inc(pool_set, 1)
            pool.memset(carry[:, :], 1.0).then_inc(pool_set, 1)
            pool.memset(from_state[:, :, :], 0.0).then_inc(pool_set, 1)
            pool.iota(steps, [[1, P]], base=0, channel_multiplier=0, allow_small_or_imprecise_dtypes=True)\
                .then_inc(pool_set, 1)
            pool.iota(left, [[0, 1]], base=P - 1, channel_multiplier=-1, allow_small_or_imprecise_dtypes=True)\
                .then_inc(pool_set, 1)
            pool.wait_ge(pool_set, 7)
            pool.memset(flat_ring[0:1, 400:401], 1.0).then_inc(pool_set, 1)
            pool.affine_select(out=ident[:, :], in_=ident[:, :], compare_op=ALU.not_equal, fill=1.0, base=0,
                               pattern=[[-1, P]], channel_multiplier=1).then_inc(pool_set, 1)
            pool.memset(carry[:, 0:C:PER_BATCH], 0.0).then_inc(pool_set, 1)

            for i in range(4):
                pool.wait_ge(prep_v, V[f"peaks{i}"])
                a, b = ((0, 4), (4, 6), (6, 7), (7, 8))[i]
                pool.partition_all_reduce(peak_all[:, a:b], peak[:, a:b], P, RMAX).then_inc(peaks_reduced, 1)

            def power(dst, src, done, **_):
                pool.tensor_tensor(dst, src, mhalf[:, :], ALU.pow).then_inc(done, 1)

            pool.wait_ge(x_var, 1)
            power(va[:, 1, :], va[:, 0, :], x_rstd)

            def weigh(g, par):
                for j in range(GT):
                    pool.wait_ge(u_norm, 4 * g + j + 1)
                    pool.tensor_tensor(uring[:, j % 2, :], uring[:, j % 2, :], w1s[:, :], ALU.mult)\
                        .then_inc(u_weighted, 1)

            def step(g, pair, par):
                if not is_last(g):
                    pool.wait_ge(x_var, g + 2)
                    pool.wait_ge(z_ready, 4 * g + 4)
                    power(va[:, 1, :], va[:, 0, :], x_rstd)
                if not is_first(g):
                    pool.wait_ge(v_var, g)
                    power(va[:, 6, :], va[:, 5, :], v_rstd)
                pool.wait_ge(z_ready, 4 * g + 4)
                for j in range(GT):
                    pool.tensor_tensor(xbuf[par][:, j, :], xbuf[par][:, j, :], half_bias[:, :], ALU.add)\
                        .then_inc(xb_ready, 1)
                if not is_first(g):
                    weigh(g - 1, 1 - par)
                pool.wait_ge(x1_var, g + 1)
                power(va[:, 4, :], va[:, 3, :], x1_rstd)
            pool.wait_ge(prep_v, V["vecs"])
            each_group(pool, step)
            pool.wait_ge(v_var, GROUPS)
            power(va[:, 6, :], va[:, 5, :], v_rstd)
            weigh(GROUPS - 1, 1)

            def mix(o, i):
                pool.wait_ge(state_scanned, o + 1)
                if not (isinstance(o, int) and o < 2):
                    pool.wait_ge(state_low, o - 1)
                pool.tensor_tensor(weighted[i].rearrange("p (c t) -> p c t", c=OC),
                                   scan_out[i].rearrange("p (c t) -> p c t", c=OC),
                                   mix_s[:, bass.ds(o * OC, OC)].unsqueeze(2).to_broadcast([P, OC, TILES]),
                                   ALU.mult).then_inc(state_mixed, 1)

            mix(0, 0)
            mix(1, 1)
            with pool.Fori(1, C // OC // 2) as h:
                mix(2 * h, 0)
                mix(2 * h + 1, 1)

            def residual(g, par):
                pool.wait_ge(xm_var, g + 1)
                power(va[:, 1, :], va[:, 0, :], xm_rstd)
                for j in range(GT):
                    pool.wait_ge(r_sum, 4 * g + j + 1)
                    pool.tensor_tensor(rbuf[par][:, j, :], rbuf[par][:, j, :], fc2_bias, ALU.add)\
                        .then_inc(r_ready, 1)

            pool.wait_ge(fc2b_loaded, 16)
            residual(0, 0)

            def step(g, pair, par):
                if not is_first(g):
                    for j in range(GT):
                        pool.wait_ge(z3_ready, 4 * (g - 1) + j + 1)
                        pool.tensor_tensor(x2buf[1 - par][:, j, :], x2buf[1 - par][:, j, :], half_bias[:, :],
                                           ALU.add).then_inc(x2b_ready, 1)
                if not is_last(g):
                    pool.wait_ge(z2_ready, 4 * g + 4)
                    residual(g + 1, 1 - par)
                pool.wait_ge(x2_var, g + 1)
                power(va[:, 4, :], va[:, 3, :], x2_rstd)
            each_group(pool, step)
            for j in range(GT):
                pool.wait_ge(z3_ready, 4 * (GROUPS - 1) + j + 1)
                pool.tensor_tensor(x2buf[1][:, j, :], x2buf[1][:, j, :], half_bias[:, :], ALU.add)\
                    .then_inc(x2b_ready, 1)

        @block.scalar
        def _(act):
            act.wait_ge(prep_v, V["nx"])
            act.activation(tmp_b, tmp_a, ACT.Exp).then_inc(prep_a, 1)
            act.wait_ge(prep_a, A["exp"])
            act.activation(tmp_b, tmp_b, ACT.Ln, bias=1.0).then_inc(prep_a, 1)
            act.wait_ge(prep_v, V["dt"])
            act.wait_ge(pool_set, 9)
            act.activation(e_taps, steps, ACT.Exp, scale=neg_a[:, 64:65]).then_inc(prep_a, 1)
            act.activation(e_out, steps, ACT.Exp, scale=neg_a[:, 64:65], bias=neg_a[:, 64:65]).then_inc(prep_a, 1)
            act.activation(e_in, neg_a[:, 0:64], ACT.Exp, scale=left).then_inc(prep_a, 1)
            act.activation(e_tile, neg_a[:, 64:65], ACT.Exp, scale=float(P)).then_inc(prep_a, 1)
            for i in range(8):
                act.wait_ge(prep_pe, E[f"at{i}"])
                act.activation((at_re if i < 4 else at_im)[:, i % 4, :], bank(i), ACT.Copy).then_inc(prep_a, 1)
            for i in range(4):
                act.wait_ge(prep_pe, E[f"m{i}"])
                act.activation(m_full[:, i, :], bank(i), ACT.Copy).then_inc(prep_a, 1)

            def normalise(g, par):
                act.wait_ge(x_coef, g + 1)
                for j in range(GT):
                    if not is_first(g):
                        act.wait_ge(zt_psum, 4 * g + j - 3)
                    act.activation(ring[:, j, :], xbuf[par][:, j, :], ACT.Identity,
                                   scale=va[:, 1, j:j + 1], bias=va[:, 2, j:j + 1]).then_inc(z_ready, 1)

            def normalise_u(g, par):
                act.wait_ge(u_coef, g + 1)
                def high(j):
                    act.wait_ge(u_done, 4 * g + j + 1)
                    act.activation(u_all[:, :, 0, :, bass.ds(4 * g + j, 1)],
                                   uring[:, j % 2, :].rearrange("p (b c o) -> p b c o", b=BLOCKS, o=1), ACT.Copy)\
                        .then_inc(u_high, 1)
                for j in range(GT):
                    if not (is_first(g) and j < 2):
                        act.wait_ge(u_low, 4 * g + j - 1)
                    act.activation(uring[:, j % 2, :], x1buf[par][:, j, :], ACT.Identity,
                                   scale=va[:, 7, j:j + 1], bias=ubias[:, j:j + 1]).then_inc(u_norm, 1)
                    if j >= 1:
                        high(j - 1)
                high(GT - 1)

            normalise(0, 0)
            act.wait_ge(fc2_stored, 16)

            def step(g, pair, par):
                for j in range(GT):
                    act.wait_ge(zt_psum, 4 * g + j + 1)
                    if not (is_first(g) and j < 2):
                        act.wait_ge(ffn_psum, 4 * g + j - 1)
                    act.activation(zt[:, j % 2, 0, :, :].rearrange("p k t -> p (k t)"), bank(j % 2), ACT.Copy)\
                       .then_inc(zt_high, 1)
                if not is_first(g):
                    normalise_u(g - 1, 1 - par)
                if not is_last(g):
                    normalise(g + 1, 1 - par)
            each_group(act, step)
            normalise_u(GROUPS - 1, 1)

            def state_part(o, i):
                act.wait_ge(state_mixed, o + 1)
                if not (isinstance(o, int) and o < 2):
                    act.wait_ge(y_psum, o - 1)
                src = weighted[i].rearrange("p (c t) -> p c t", t=PER_BATCH)[:, :, 0:PER_BATCH - 1]
                dst = state_parts[:, i, :].rearrange("p (c t) -> p c t", t=PER_BATCH)[:, :, 1:PER_BATCH]
                act.activation(dst, src, ACT.Copy).then_inc(state_high, 1)

            def stage_y(blk, o, i):
                act.wait_ge(y_psum, o + 1)
                stage = area(blk * REG, REG).rearrange("p (t c) -> p c t", c=BLK)
                act.activation(stage[:, bass.ds((o - blk * (BLK // OC)) * OC, OC), :],
                               bank(4 + i).rearrange("p (c t) -> p c t", c=OC), ACT.Copy, scale=scale(C_Y))\
                   .then_inc(y_staged, 1)

            for i in range(2):
                act.wait_ge(x1_stored[i], 16 * PAIRS)
            def two(blk, h):
                for i in range(2):
                    o = 2 * h + (blk * (BLK // OC) + i)
                    state_part(o + 1, 1 - i)
                    stage_y(blk, o, i)

            state_part(0, 0)
            for blk in range(BLOCKS):
                if blk == 0:
                    two(0, 0)
                with act.Fori(1 if blk == 0 else 0, BLK // OC // 2 - (1 if blk == BLOCKS - 1 else 0)) as h:
                    two(blk, h)
            act_last = C // OC - 2
            state_part(act_last + 1, 1)
            stage_y(BLOCKS - 1, act_last, 0)
            stage_y(BLOCKS - 1, act_last + 1, 1)

            def z2(g, j):
                act.wait_ge(xm_coef, g + 1)
                act.wait_ge(r_sum, 4 * g + j + 1)
                act.activation(ybuf[:, j, :], ybuf[:, j, :], ACT.Identity,
                               scale=va[:, 1, j:j + 1], bias=va[:, 2, j:j + 1]).then_inc(z2_ready, 1)

            def g_high(g, j):
                act.wait_ge(gt_psum, 4 * g + j + 1)
                act.activation(gt[:, 0, :, j * P:(j + 1) * P], bank(2 + j % 2).rearrange("p (k t) -> p k t", k=KC),
                               ACT.Copy).then_inc(gt_high, 1)

            def z3_norm(g, par):
                act.wait_ge(x2_coef, g + 1)
                for j in range(GT):
                    act.activation(z3[:, j, :], x2buf[par][:, j, :], ACT.Identity,
                                   scale=va[:, 4, j:j + 1], bias=va[:, 5, j:j + 1]).then_inc(z3_ready, 1)

            def z3_high(g, j):
                act.wait_ge(z3t_psum, 4 * g + j + 1)
                act.activation(z3t[:, j, 0, :, :].rearrange("p k t -> p (k t)"), bank(2 + j % 2), ACT.Copy)\
                   .then_inc(z3t_high, 1)

            for j in range(GT):
                z2(0, j)
            for j in range(GT):
                g_high(0, j)

            def step(g, pair, par):
                if not is_first(g):
                    z3_norm(g - 1, 1 - par)
                for hc in range(HC):
                    act.wait_ge(fc1_psum, HC * g + hc + 1)
                    if not (is_first(g) and hc < 4):
                        act.wait_ge(h_low, HC * g + hc - 3)
                    act.activation(h32[:, hc % 4, :],
                                   bank(hc % 2), ACT.Gelu, scale=scale(C_W1), bias=b1p[:, hc:hc + 1])\
                       .then_inc(h_ready, 1)
                    if hc in (3, 5, 7, 9) and not is_first(g):
                        z3_high(g - 1, (hc - 3) // 2)
                    if 10 <= hc < 14 and not is_last(g):
                        z2(g + 1, hc - 10)
                if not is_last(g):
                    for j in range(GT):
                        g_high(g + 1, j)
            each_group(act, step)
            z3_norm(GROUPS - 1, 1)
            for j in range(GT):
                z3_high(GROUPS - 1, j)

        @block.vector
        def _(dve):
            count = [0]

            def done(ins, name):
                count[0] += 1
                assert V[name] == count[0], name
                ins.then_inc(prep_v, 1)
                return ins

            def own(name):
                dve.wait_ge(prep_v, V[name])

            dve.wait_ge(smalls_loaded, 16 * N_SMALLS)
            done(dve.scalar_tensor_tensor(out=tmp_a, in0=logs, scalar=-1.0, in1=logs, op0=ALU.mult, op1=ALU.min),
                 "nx")
            dve.wait_ge(prep_a, A["ln"])
            done(dve.scalar_tensor_tensor(out=tmp_a, in0=logs, scalar=0.0, in1=tmp_b, op0=ALU.max, op1=ALU.add),
                 "sp")
            own("sp")
            done(dve.tensor_scalar(neg_a[:, 0:65], tmp_a[:, 0:65], tmp_a[:, 65:66], -1.0, ALU.mult, ALU.mult), "dt")
            dve.wait_ge(prep_a, A["e_tile"])
            dve.wait_ge(pool_set, 12)
            big = 32768.0
            done(dve.tensor_scalar(from_state[:, 0, :], e_out, big, None, ALU.mult), "q_high")
            own("q_high")
            done(dve.scalar_tensor_tensor(out=from_state[0:NST, 1, :], in0=e_out[0:NST, :], scalar=big,
                                          in1=from_state[0:NST, 0, :], op0=ALU.mult, op1=ALU.subtract), "q_low")
            for half in range(2):
                ins = dve.tensor_scalar(to_state[:, 0, half * NST:(half + 1) * NST], e_in, big, None, ALU.mult)
            done(ins, "p_high")
            own("p_high")
            for half in range(2):
                ins = dve.scalar_tensor_tensor(out=to_state[:, 1, half * NST:(half + 1) * NST], in0=e_in,
                                               scalar=big, in1=to_state[:, 0, half * NST:(half + 1) * NST],
                                               op0=ALU.mult, op1=ALU.subtract)
            done(ins, "p_low")
            done(dve.tensor_scalar(carry[:, :], carry[:, :], e_tile, None, ALU.mult), "carry")

            def peak_of(col, ap, parts=P, axis=AX_X):
                return dve.tensor_reduce(peak[0:parts, col:col + 1], ap, axis, ALU.max, apply_absolute_value=True)

            peak_of(0, mix_s[:, :])
            peak_of(1, drow, 1)
            peak_of(2, w1s[:, :])
            ins = peak_of(3, b1s[:, :])
            done(ins, "peaks0")
            dve.wait_ge(peaks_reduced, 1)
            dve.scalar_tensor_tensor(out=bounds[:, 0:1], in0=peak_all[:, 2:3], scalar=23.0, in1=peak_all[:, 3:4],
                                     op0=ALU.mult, op1=ALU.add)
            done(dve.scalar_tensor_tensor(out=bounds[:, 1:2], in0=peak_all[:, 0:1], scalar=1024.0,
                                          in1=peak_all[:, 1:2], op0=ALU.mult, op1=ALU.add), "bound0")

            def exponents(n, src, name):
                dve.tensor_scalar(bounds[:, 0:n], src, 2.0 ** -100, None, ALU.max).then_inc(bounds_ready, 1)
                dve.wait_ge(bounds_ready, name + 1)
                done(dve.tensor_scalar(bounds[:, 0:n].bitcast(I32), bounds[:, 0:n].bitcast(I32), 0x7F800000, None,
                                       ALU.bitwise_and), f"e{name}")
                own(f"e{name}")
                done(dve.reciprocal(bounds[:, 4:4 + n], bounds[:, 0:n]), f"r{name}")
                own(f"r{name}")

            own("bound0")
            exponents(2, bounds[:, 0:2], 0)
            dve.tensor_scalar(scale(S_U), bounds[:, 4:5], 2.0 ** 14, None, ALU.mult)
            dve.tensor_scalar(scale(S_K), bounds[:, 5:6], 2.0 ** 14, None, ALU.mult)
            dve.tensor_scalar(scale(C_MIX), bounds[:, 5:6], 2.0 ** -16, None, ALU.mult)
            done(dve.tensor_scalar(scale(C_Y), bounds[:, 0:1], bounds[:, 1:2], 2.0 ** -28, ALU.mult, ALU.mult),
                 "scales0")
            own("scales0")
            dve.tensor_scalar(half_bias[:, :], half_bias[:, :], 0.5, None, ALU.mult)
            dve.tensor_scalar(w1s[:, :], w1s[:, :], scale(S_U), None, ALU.mult)
            done(dve.tensor_scalar(b1s[:, :], b1s[:, :], scale(S_U), None, ALU.mult), "vecs")
            dve.wait_ge(prep_pe, E["taps"])
            k_psum = bank(7).rearrange("p (b c) -> p b c", c=CB)
            k_out = taps_out.rearrange("p (b s c) -> p b s c", s=2, c=CB)
            done(dve.tensor_scalar(k_out[:, :, 0, :], k_psum, scale(S_K), None, ALU.mult), "k_high")
            own("k_high")
            done(dve.scalar_tensor_tensor(out=k_out[:, :, 1, :], in0=k_psum, scalar=scale(S_K),
                                          in1=k_out[:, :, 0, :], op0=ALU.mult, op1=ALU.subtract), "k_low")
            done(dve.tensor_scalar(mix_s[:, :], mix_s[:, :], scale(C_MIX), None, ALU.mult), "mixw")

            dve.wait_ge(prep_pe, E["fc1bias"])
            done(dve.tensor_tensor(b1p[:, :], bank(4)[:, 0:HC], colsb[:, 0:HC], ALU.add), "fc1bias")
            for k in range(KC):
                ins = dve.tensor_scalar(wfull1[:, k, :], wfull1[:, k, :], colsb[:, HC + k:HC + k + 1], None,
                                        ALU.mult)
            done(ins, "fc1w")
            own("fc1w")
            peak_of(4, wfull)
            done(peak_of(5, b1p[:, :]), "peaks1")
            dve.wait_ge(peaks_reduced, 2)
            dve.tensor_copy(bounds[:, 0:1], peak_all[:, 4:5])
            done(dve.scalar_tensor_tensor(out=bounds[:, 1:2], in0=peak_all[:, 4:5], scalar=float(C),
                                          in1=peak_all[:, 5:6], op0=ALU.mult, op1=ALU.add), "bound1")
            own("bound1")
            exponents(2, bounds[:, 0:2], 1)
            dve.tensor_scalar(scale(S_W1), bounds[:, 4:5], 2.0 ** 14, None, ALU.mult)
            dve.tensor_scalar(scale(C_W1), bounds[:, 0:1], 2.0 ** -14, None, ALU.mult)
            dve.tensor_scalar(scale(C_H), bounds[:, 1:2], 2.0 ** -14, None, ALU.mult)
            done(dve.tensor_scalar(scale(S_H), bounds[:, 5:6], 2.0 ** 14, None, ALU.mult), "scales1")
            own("scales1")
            half_w = REG
            done(dve.tensor_scalar(wsplit[:, 0:half_w], wfull, scale(S_W1), None, ALU.mult), "fc1high")
            own("fc1high")
            done(dve.scalar_tensor_tensor(out=wsplit[:, half_w:], in0=wfull, scalar=scale(S_W1),
                                          in1=wsplit[:, 0:half_w], op0=ALU.mult, op1=ALU.subtract), "fc1low")
            dve.wait_ge(fc2_loaded, 16)
            done(peak_of(6, wfull), "peaks2")
            dve.wait_ge(peaks_reduced, 3)
            exponents(1, peak_all[:, 6:7], 2)
            dve.tensor_scalar(scale(S_W2), bounds[:, 4:5], 2.0 ** 14, None, ALU.mult)
            done(dve.tensor_scalar(scale(C_2), bounds[:, 0:1], scale(C_H), 2.0 ** -14, ALU.mult, ALU.mult),
                 "scales2")
            own("scales2")
            dve.wait_ge(fc1_stored, 16)
            done(dve.tensor_scalar(wsplit[:, 0:half_w], wfull, scale(S_W2), None, ALU.mult), "fc2high")
            own("fc2high")
            done(dve.scalar_tensor_tensor(out=wsplit[:, half_w:], in0=wfull, scalar=scale(S_W2),
                                          in1=wsplit[:, 0:half_w], op0=ALU.mult, op1=ALU.subtract), "fc2low")
            dve.wait_ge(prep_a, A["m3"])
            done(peak_of(7, m_full.rearrange("p k n -> p (k n)")), "peaks3")
            dve.wait_ge(peaks_reduced, 4)
            exponents(1, peak_all[:, 7:8], 3)
            dve.tensor_scalar(scale(S_M), bounds[:, 4:5], 2.0 ** 14, None, ALU.mult)
            done(dve.tensor_scalar(scale(C_M), bounds[:, 0:1], 2.0 ** -14 * 0.5 / C, None, ALU.mult), "scales3")
            own("scales3")
            m_flat = m_parts[:, :, :, :].rearrange("p s k n -> p s (k n)")
            m_src = m_full.rearrange("p k n -> p (k n)")
            done(dve.tensor_scalar(m_flat[:, 0, :], m_src, scale(S_M), None, ALU.mult), "mhigh")
            own("mhigh")
            ins = dve.scalar_tensor_tensor(out=m_flat[:, 1, :], in0=m_src, scalar=scale(S_M), in1=m_flat[:, 0, :],
                                           op0=ALU.mult, op1=ALU.subtract)
            done(ins, "mlow")

            def moments(tiles, chain, bn_done, aggr_done, var_done, var_out, g, waits):
                for j in range(GT):
                    waits(j)
                    ins = dve.bn_stats(bn[:, chain, j, :], tiles[:, j, :])
                ins.then_inc(bn_done, 1)
                dve.wait_ge(bn_done, g + 1)
                dve.sem_inc(gate, 1)
                for j in range(GT):
                    ins = dve.bn_aggr(mv[:, chain, j, :], bn[:, chain, j, :])
                ins.then_inc(aggr_done, 1)
                dve.wait_ge(aggr_done, g + 1)
                dve.tensor_scalar(var_out, mv[:, chain, :, 1], EPS, None, ALU.add).then_inc(var_done, 1)

            def x_moments(g, pair, par):
                dve.wait_ge(x_loaded[par], 16 * pair + 16)
                if not is_first(g):
                    dve.wait_ge(x_rstd, g)
                moments(xbuf[par], 0, x_bn, x_aggr, x_var, va[:, 0, :], g, lambda j: None)

            def x_shift(g):
                dve.wait_ge(x_rstd, g + 1)
                dve.scalar_tensor_tensor(out=va[:, 2, :], in0=mv[:, 0, :, 0], scalar=-1.0, in1=va[:, 1, :],
                                         op0=ALU.mult, op1=ALU.mult).then_inc(x_coef, 1)

            def v_variance(g):
                dve.wait_ge(x1_rstd, g + 1)
                dve.tensor_tensor(va[:, 5, :], mv[:, 1, :, 1], va[:, 4, :], ALU.mult).then_inc(v_var0, 1)
                dve.wait_ge(v_var0, 3 * g + 1)
                dve.tensor_tensor(va[:, 5, :], va[:, 5, :], va[:, 4, :], ALU.mult).then_inc(v_var0, 1)
                dve.wait_ge(v_var0, 3 * g + 2)
                dve.tensor_scalar(va[:, 5, :], va[:, 5, :], EPS, None, ALU.add).then_inc(v_var, 1)
                at = bass.ds(4 * g, GT)
                dve.tensor_copy(alpha1[:, at], va[:, 4, :])
                dve.scalar_tensor_tensor(out=beta1[:, at], in0=mv[:, 1, :, 0], scalar=-1.0, in1=va[:, 4, :],
                                         op0=ALU.mult, op1=ALU.mult).then_inc(v_var0, 1)

            def u_coefs(g):
                dve.wait_ge(v_rstd, g + 1)
                dve.wait_ge(v_var0, 3 * g + 3)
                dve.tensor_tensor(va[:, 7, :], va[:, 4, :], va[:, 6, :], ALU.mult)
                dve.tensor_tensor(ubias[:, :], beta1[:, bass.ds(4 * g, GT)], va[:, 6, :], ALU.mult)\
                   .then_inc(u_coef, 1)

            def u_finish(g):
                def low(j):
                    dve.wait_ge(u_high, 4 * g + j + 1)
                    at = bass.ds(4 * g + j, 1)
                    dve.tensor_tensor(u_all[:, :, 1, :, at],
                                      uring[:, j % 2, :].rearrange("p (b c o) -> p b c o", b=BLOCKS, o=1),
                                      u_all[:, :, 0, :, at], ALU.subtract).then_inc(u_low, 1)
                for j in range(GT):
                    dve.wait_ge(u_weighted, 4 * g + j + 1)
                    dve.tensor_tensor(uring[:, j % 2, :], uring[:, j % 2, :], b1s[:, :], ALU.add)\
                       .then_inc(u_done, 1)
                    if j >= 1:
                        low(j - 1)
                low(GT - 1)

            x_moments(0, 0, 0)
            x_shift(0)
            dve.wait_ge(fc2_stored, 16)

            def step(g, pair, par):
                if not is_last(g):
                    x_moments(g + 1, pair + par, 1 - par)
                if not is_first(g):
                    v_variance(g - 1)
                for j in range(GT):
                    dve.wait_ge(zt_high, 4 * g + j + 1)
                    dve.tensor_tensor(zt[:, j % 2, 1, :, :].rearrange("p k t -> p (k t)"), bank(j % 2),
                                      zt[:, j % 2, 0, :, :].rearrange("p k t -> p (k t)"), ALU.subtract)\
                       .then_inc(zt_low, 1)
                if not is_first(g):
                    u_coefs(g - 1)
                if not is_last(g):
                    x_shift(g + 1)
                if not is_first(g):
                    u_finish(g - 1)

                def x1(j):
                    if j == 0 and not (isinstance(g, int) and g < 2):
                        dve.wait_ge(x1_stored[par], 16 * pair)
                    dve.wait_ge(ffn_psum, 4 * g + j + 1)
                    dve.wait_ge(xb_ready, 4 * g + j + 1)
                    dve.scalar_tensor_tensor(out=x1buf[par][:, j, :], in0=bank(2 + j % 2), scalar=scale(C_M),
                                             in1=xbuf[par][:, j, :], op0=ALU.mult, op1=ALU.add)\
                       .then_inc(x1_ready, 1)
                    dve.wait_ge(x1_ready, 4 * g + j + 1)
                moments(x1buf[par], 1, x1_bn, x1_aggr, x1_var, va[:, 3, :], g, x1)
            each_group(dve, step)
            v_variance(GROUPS - 1)
            u_coefs(GROUPS - 1)
            u_finish(GROUPS - 1)

            firsts = state_parts[:, :, :].rearrange("p i (c t) -> p i c t", t=PER_BATCH)[:, :, :, 0:1]
            dve.memset(firsts, 0.0).then_inc(state_zero, 1)

            def scan(o, i):
                dve.wait_ge(state_psum, o + 1)
                if not (isinstance(o, int) and o < 2):
                    dve.wait_ge(state_mixed, o - 1)
                dve.tensor_tensor_scan(scan_out[i], carry[:, :], bank(i), 0.0, ALU.mult, ALU.add)\
                   .then_inc(state_scanned, 1)

            def low_part(o, i):
                dve.wait_ge(state_high, o + 1)
                src = weighted[i].rearrange("p (c t) -> p c t", t=PER_BATCH)[NST:P, :, 0:PER_BATCH - 1]
                dst = state_parts[:, i, :].rearrange("p (c t) -> p c t", t=PER_BATCH)[NST:P, :, 1:PER_BATCH]
                dve.tensor_tensor(dst, src, dst, ALU.subtract).then_inc(state_low, 1)

            scan(0, 0)
            scan(1, 1)
            low_part(0, 0)
            with dve.Fori(1, C // OC // 2) as h:
                scan(2 * h, 0)
                low_part(2 * h - 1, 1)
                scan(2 * h + 1, 1)
                low_part(2 * h, 0)
            low_part(C // OC - 1, 1)

            def mixed(g, j, pair, par):
                if j == 0:
                    dve.wait_ge(yg_loaded, 16 * g + 16)
                    dve.wait_ge(r_loaded[par], 16 * pair + 16)
                dve.scalar_tensor_tensor(out=ybuf[:, j, :], in0=rbuf[par][:, j, :],
                                         scalar=alpha1[:, bass.ds(4 * g + j, 1)], in1=ybuf[:, j, :],
                                         op0=ALU.mult, op1=ALU.add).then_inc(xm_sum, 1)
                dve.wait_ge(xm_sum, 4 * g + j + 1)
                ins = dve.bn_stats(bn[:, 0, j, :], ybuf[:, j, :])
                if j == GT - 1:
                    ins.then_inc(xm_bn, 1)
                    dve.wait_ge(xm_bn, g + 1)
                    dve.sem_inc(gate, 1)
                    for i in range(GT):
                        ins = dve.bn_aggr(mv[:, 0, i, :], bn[:, 0, i, :])
                    ins.then_inc(xm_aggr, 1)
                    dve.wait_ge(xm_aggr, g + 1)
                    dve.tensor_scalar(va[:, 0, :], mv[:, 0, :, 1], EPS, None, ALU.add).then_inc(xm_var, 1)

            def mixed_shift(g):
                dve.wait_ge(xm_rstd, g + 1)
                if not is_first(g):
                    dve.wait_ge(z2_ready, 4 * g)
                dve.scalar_tensor_tensor(out=va[:, 2, :], in0=mv[:, 0, :, 0], scalar=-1.0, in1=va[:, 1, :],
                                         op0=ALU.mult, op1=ALU.mult).then_inc(xm_coef, 1)

            def residual(g, j, par):
                dve.scalar_tensor_tensor(out=rbuf[par][:, j, :], in0=ybuf[:, j, :],
                                         scalar=beta1[:, bass.ds(4 * g + j, 1)], in1=rbuf[par][:, j, :],
                                         op0=ALU.add, op1=ALU.add).then_inc(r_sum, 1)

            def g_low(g, j):
                dve.wait_ge(gt_high, 4 * g + j + 1)
                dve.tensor_tensor(gt[:, 1, :, j * P:(j + 1) * P], bank(2 + j % 2).rearrange("p (k t) -> p k t", k=KC),
                                  gt[:, 0, :, j * P:(j + 1) * P], ALU.subtract).then_inc(gt_low, 1)

            def z3_low(g, j):
                dve.wait_ge(z3t_high, 4 * g + j + 1)
                dve.tensor_tensor(z3t[:, j, 1, :, :].rearrange("p k t -> p (k t)"), bank(2 + j % 2),
                                  z3t[:, j, 0, :, :].rearrange("p k t -> p (k t)"), ALU.subtract)\
                   .then_inc(z3t_low, 1)

            def x2_shift(g):
                dve.wait_ge(x2_rstd, g + 1)
                dve.scalar_tensor_tensor(out=va[:, 5, :], in0=mv[:, 1, :, 0], scalar=-1.0, in1=va[:, 4, :],
                                         op0=ALU.mult, op1=ALU.mult).then_inc(x2_coef, 1)

            def x3(g, j, par):
                dve.wait_ge(ffn2_psum, 4 * g + j + 1)
                dve.wait_ge(x2b_ready, 4 * g + j + 1)
                dve.scalar_tensor_tensor(out=x2buf[par][:, j, :], in0=bank(6 + j % 2), scalar=scale(C_M),
                                         in1=x2buf[par][:, j, :], op0=ALU.mult, op1=ALU.add)\
                   .then_inc(x3_ready, 1)

            for j in range(GT):
                mixed(0, j, 0, 0)
            mixed_shift(0)
            for j in range(GT):
                residual(0, j, 0)
            for j in range(GT):
                g_low(0, j)

            def step(g, pair, par):
                if not is_first(g):
                    x2_shift(g - 1)
                for hc in range(HC):
                    dve.wait_ge(h_ready, HC * g + hc + 1)
                    dve.tensor_scalar(hid[:, 0, hc, :], h32[:, hc % 4, :], scale(S_H), None, ALU.mult)\
                       .then_inc(h_high, 1)
                    dve.wait_ge(h_high, HC * g + hc + 1)
                    dve.scalar_tensor_tensor(out=hid[:, 1, hc, :], in0=h32[:, hc % 4, :], scalar=scale(S_H),
                                             in1=hid[:, 0, hc, :], op0=ALU.mult, op1=ALU.subtract)\
                       .then_inc(h_low, 1)
                    if hc in (3, 5, 7, 9) and not is_first(g):
                        z3_low(g - 1, (hc - 3) // 2)
                    if not is_last(g):
                        if 1 <= hc < 5:
                            mixed(g + 1, hc - 1, pair + par, 1 - par)
                        if hc == 6:
                            mixed_shift(g + 1)
                        if 6 <= hc < 10:
                            residual(g + 1, hc - 6, 1 - par)
                for j in range(GT):
                    if not is_last(g):
                        g_low(g + 1, j)
                    if not is_first(g):
                        x3(g - 1, j, 1 - par)

                def x2(j):
                    if j == 0 and not (isinstance(g, int) and g < 2):
                        dve.wait_ge(out_stored[par], 16 * pair)
                    dve.wait_ge(fc2_psum, 4 * g + j + 1)
                    dve.wait_ge(r_ready, 4 * g + j + 1)
                    dve.scalar_tensor_tensor(out=x2buf[par][:, j, :], in0=bank(4 + j % 2), scalar=scale(C_2),
                                             in1=rbuf[par][:, j, :], op0=ALU.mult, op1=ALU.add)\
                       .then_inc(x2_ready, 1)
                    dve.wait_ge(x2_ready, 4 * g + j + 1)
                moments(x2buf[par], 1, x2_bn, x2_aggr, x2_var, va[:, 3, :], g, x2)
            each_group(dve, step)
            x2_shift(GROUPS - 1)
            for j in range(GT):
                z3_low(GROUPS - 1, j)
            for j in range(GT):
                x3(GROUPS - 1, j, 1)

        @block.tensor
        def _(pe):
            pe.wait_ge(smalls_loaded, 16 * N_SMALLS)
            pe.wait_ge(prep_a, A["e_taps"])
            pe.wait_ge(pool_set, 12)
            pe.matmul(bank(7), e_taps[0:NST, :], mix_s[0:NST, :], start=True, stop=False)
            pe.matmul(bank(7), onehot, drow, start=False, stop=True).then_inc(prep_pe, 1)
            pe.wait_ge(tables_loaded, 16 * 5)
            for i in range(8):
                if i == 7:
                    pe.wait_ge(prep_v, V["k_low"])
                oc = i % 4
                pairs = ((wr_sb, cos_sb), (wi_sb, sin_sb)) if i < 4 else ((wr_sb, sin_sb), (wi_sb, ncos_sb))
                for s, (w, f) in enumerate(pairs):
                    for k in range(KC):
                        last = pe.matmul(bank(i), w[:, k, oc * P:(oc + 1) * P], f[:, k, :],
                                         start=(s == 0 and k == 0), stop=(s == 1 and k == KC - 1))
                last.then_inc(prep_pe, 1)
            pe.wait_ge(fc1_loaded, 16)
            pe.wait_ge(prep_a, A["at4"])
            for hc in range(HC):
                for k in range(KC):
                    last = pe.matmul(bank(4)[:, hc:hc + 1], wfull1[:, k, hc * P:(hc + 1) * P],
                                     colsb[:, HC + KC + k:HC + KC + k + 1], start=(k == 0), stop=(k == KC - 1))
            last.then_inc(prep_pe, 1)
            pe.wait_ge(prep_a, A["at7"])
            for i in range(4):
                for s, (a, f) in enumerate(((at_re, cos_sb), (at_im, sin_sb))):
                    for k in range(KC):
                        last = pe.matmul(bank(i), a[:, k, i * P:(i + 1) * P], f[:, k, :],
                                         start=(s == 0 and k == 0), stop=(s == 1 and k == KC - 1))
                last.then_inc(prep_pe, 1)

            PASSES = ((0, 0), (0, 1), (1, 0))

            def transposes(dst, src, done):
                for k in range(KC):
                    last = pe.transpose(dst[:, k * P:(k + 1) * P], src[:, k * P:(k + 1) * P], ident[:, :])
                last.then_inc(done, 1)

            def ffn(dst, act_parts, done):
                n = 0
                for k in range(KC):
                    for a, b in PASSES:
                        last = pe.matmul(dst, act_parts[:, a, k, :], m_parts[:, b, k, :], start=(n == 0),
                                         stop=(n == 3 * KC - 1))
                        n += 1
                last.then_inc(done, 1)

            def turn(g, j, first):
                pe.wait_ge(z_ready, 4 * g + j + 1)
                if not (first and j < 2):
                    pe.wait_ge(zt_low, 4 * g + j - 1)
                transposes(bank(j % 2), ring[:, j, :], zt_psum)

            pe.wait_ge(prep_a, A["m3"])
            turn(0, 0, True)
            pe.wait_ge(prep_v, V["mlow"])

            def step(g, pair, par):
                for j in range(GT):
                    if j < GT - 1:
                        turn(g, j + 1, is_first(g))
                    elif not is_last(g):
                        turn(g + 1, 0, False)
                    pe.wait_ge(zt_high, 4 * g + j + 1)
                    pe.wait_ge(zt_low, 4 * g + j + 1)
                    if not (is_first(g) and j < 2):
                        pe.wait_ge(x1_ready, 4 * g + j - 1)
                    ffn(bank(2 + j % 2), zt[:, j % 2, :, :, :], ffn_psum)
            each_group(pe, step)

            def states(blk, o, i):
                oo = o + blk * (BLK // OC)
                if not (isinstance(oo, int) and oo < 2):
                    pe.wait_ge(state_scanned, oo - 1)
                for n, (a, b) in enumerate(PASSES):
                    off = (blk * 2 + b) * BLK * TILES
                    last = pe.matmul(bank(i), to_state[:, a, :],
                                     u_flat[:, bass.ds(o * (OC * TILES) + off, OC * TILES)],
                                     start=(n == 0), stop=(n == 2))
                last.then_inc(state_psum, 1)

            def inside(blk, o, i, par, half):
                oo = o + blk * (BLK // OC)
                if not (isinstance(oo, int) and oo < 2):
                    pe.wait_ge(y_staged, oo - 1)
                for c in range(OC):
                    for n, (a, b) in enumerate(PASSES):
                        off = (blk * 2 + b) * BLK * TILES + c * TILES
                        pe.matmul(bank(4 + i)[:, c * TILES:(c + 1) * TILES],
                                  taps[par][:, :, a, half * OC + c],
                                  u_flat[:, bass.ds(o * (OC * TILES) + off, TILES)],
                                  start=(c == 0 and n == 0), stop=False, skip_group_check=True)

            def between(oo, i):
                pe.wait_ge(state_high, oo + 1)
                pe.wait_ge(state_low, oo + 1)
                pe.matmul(bank(4 + i), from_state[:, 0, :], state_parts[:, i, :], start=False, stop=False,
                          skip_group_check=True)
                pe.matmul(bank(4 + i), from_state[:, 1, :], state_parts[:, i, :], start=False, stop=True,
                          skip_group_check=True).then_inc(y_psum, 1)

            pe.wait_ge(u_high, TILES)
            pe.wait_ge(u_low, TILES)
            pe.wait_ge(state_zero, 1)
            states(0, 0, 0)
            states(0, 1, 1)

            def four(blk, q, n_ahead):
                for par in range(2):
                    pe.wait_ge(taps_loaded[par], 16 * (q + 4 * blk) + 16)
                    for half in range(2):
                        o = 4 * q + (2 * par + half)
                        inside(blk, o, half, par, half)
                        if 2 * par + half < n_ahead:
                            states(blk, 4 * q + (2 * par + half + 2), half)
                        elif blk < BLOCKS - 1:
                            states(blk + 1, half, half)
                        between(o + blk * (BLK // OC), half)

            for blk in range(BLOCKS):
                if blk == 0:
                    four(0, 0, 4)
                with pe.Fori(1 if blk == 0 else 0, 3) as q:
                    four(blk, q, 4)
                four(blk, 3, 2)

            def turn_z2(g, j):
                pe.wait_ge(z2_ready, 4 * g + j + 1)
                if is_first(g):
                    if j >= 2:
                        pe.wait_ge(gt_low, 4 * g + j - 1)
                elif j < 2:
                    if isinstance(g, int) and g == 1:
                        pe.wait_ge(gt_low, j + 3)
                    else:
                        pe.wait_ge(z3t_low, 4 * (g - 2) + j + 3)
                else:
                    pe.wait_ge(gt_low, 4 * g + j - 1)
                transposes(bank(2 + j % 2), ybuf[:, j, :], gt_psum)

            def turn_z3(g, j):
                pe.wait_ge(z3_ready, 4 * g + j + 1)
                if j < 2 and is_last(g):
                    pe.wait_ge(z3t_low, 4 * (g - 1) + j + 3)
                elif j < 2:
                    pe.wait_ge(gt_low, 4 * g + j + 7)
                else:
                    pe.wait_ge(z3t_low, 4 * g + j - 1)
                transposes(bank(2 + j % 2), z3[:, j, :], z3t_psum)

            def second_ffn(g, j):
                pe.wait_ge(z3t_high, 4 * g + j + 1)
                pe.wait_ge(z3t_low, 4 * g + j + 1)
                if not (is_first(g) and j < 2):
                    pe.wait_ge(x3_ready, 4 * g + j - 1)
                ffn(bank(6 + j % 2), z3t[:, j, :, :, :], ffn2_psum)

            for j in range(GT):
                turn_z2(0, j)
            pe.wait_ge(w1_loaded, 16)

            def step(g, pair, par):
                pe.wait_ge(gt_high, 4 * g + 4)
                pe.wait_ge(gt_low, 4 * g + 4)
                for hc in range(HC):
                    if not (is_first(g) and hc < 2):
                        pe.wait_ge(h_ready, HC * g + hc - 1)
                    n = 0
                    for k in range(KC):
                        for a, b in PASSES:
                            last = pe.matmul(bank(hc % 2), w1_sb[:, a, k, hc * P:(hc + 1) * P], gt[:, b, k, :],
                                             start=(n == 0), stop=(n == 3 * KC - 1))
                            n += 1
                    last.then_inc(fc1_psum, 1)
                    if hc in (3, 5, 7, 9) and not is_first(g):
                        turn_z3(g - 1, (hc - 3) // 2)
                for j in range(GT):
                    if not is_last(g):
                        turn_z2(g + 1, j)
                    if not is_first(g):
                        second_ffn(g - 1, j)
                if is_first(g):
                    pe.wait_ge(w2_loaded, 16)
                for j in range(GT):
                    if not (is_first(g) and j < 2):
                        pe.wait_ge(x2_ready, 4 * g + j - 1)
                    n = 0
                    for hc in range(HC):
                        if j == 0:
                            pe.wait_ge(h_low, HC * g + hc + 1)
                        for a, b in PASSES:
                            last = pe.matmul(bank(4 + j % 2), hid[:, a, hc, j * P:(j + 1) * P],
                                             w2_sb[:, b, hc, :], start=(n == 0), stop=(n == 3 * HC - 1))
                            n += 1
                    last.then_inc(fc2_psum, 1)
            each_group(pe, step)
            for j in range(GT):
                turn_z3(GROUPS - 1, j)
                if j >= 1:
                    second_ffn(GROUPS - 1, j - 1)
            second_ffn(GROUPS - 1, GT - 1)


def kernel(**inputs):
    import concourse.bacc as bacc
    from concourse.bass_utils import run_bass_kernel_spmd

    def get(name):
        return np.asarray(inputs["L0_" + name])

    def by_partition(v, n):
        return np.ascontiguousarray(v.reshape(n, P).T)

    turn = np.outer(np.arange(C), np.arange(C)) % C * (2 * np.pi / C)
    arrays = {
        "x": get("attn_x").reshape(TILES * P, C),
        "wr": get("ffn_w_freq_real"), "wi": get("ffn_w_freq_imag"), "ffn_bias": get("ffn_bias"),
        "fc1t": get("attn_fc1_w").T, "fc2t": get("attn_fc2_w").T,
        "fc1b": by_partition(get("attn_fc1_b"), HC), "fc2b": get("attn_fc2_b"),
        "n1w": get("attn_norm1_w"), "n1b": get("attn_norm1_b"),
        "n2w": by_partition(get("attn_norm2_w"), KC), "n2b": by_partition(get("attn_norm2_b"), KC),
        "dskip": get("attn_D").reshape(1, C), "mixt": get("attn_mix").T,
        "log_tau": get("attn_log_tau").reshape(NST, 1), "log_dt": get("attn_log_dt").reshape(1, 1),
        "cos_t": np.cos(turn).astype(np.float32), "sin_t": np.sin(turn).astype(np.float32),
        "ncos_t": (-np.cos(turn)).astype(np.float32),
    }
    nc = bacc.Bacc("TRN2", target_bir_lowering=False, num_devices=1)
    feed, aps = {}, {}
    for name, a in arrays.items():
        feed["in_" + name] = a = np.ascontiguousarray(a)
        aps[name] = nc.dram_tensor("in_" + name, a.shape, mybir.dt.from_np(a.dtype), kind="ExternalInput").ap()
    out = nc.dram_tensor("out", (TILES * P, C), F32, kind="ExternalOutput").ap()
    build(nc, out=out, **aps)
    r = run_bass_kernel_spmd(nc, [feed], core_ids=[0])
    return r.results[0]["out"].reshape(BATCH, TIME, C)
```

```python
from contextlib import ExitStack

import numpy as np

import concourse.bass as bass
from concourse import mybir

ALU = mybir.AluOpType
ACT = mybir.ActivationFunctionType
F32 = mybir.dt.float32
F16 = mybir.dt.float16
I32 = mybir.dt.int32
AX_X = mybir.AxisListType.X
RMAX = bass.bass_isa.ReduceOp.max

P = 128
BATCH, TIME, C, HID, NST = 4, 2048, 512, 2048, 64
KC = C // P
HC = HID // P
TILES = BATCH * TIME // P
PER_BATCH = TIME // P
GT = 4
GROUPS = TILES // GT
PAIRS = GROUPS // 2
HALF = C // 2 + 1
OC = 8
OBLOCKS = C // OC
QUADS = GROUPS // 4
LAG = 2
BLK = 128
BLOCKS = C // BLK
TAPROWS = 2 * P - 1
COPIES = 16
EPS = 1e-5
REG = 8192


def broadcast_rows(ap, n, parts=P):
    return bass.AP(tensor=ap.tensor, offset=0, ap=[[0, parts], [1, n]])


def build(nc, x, wr, wi, ffn_bias, fc1t, fc2t, fc1b, fc2b, n1w, n1b, n2w, n2b, dskip, mixt, log_tau, log_dt,
          cos_t, sin_t, out):
    x1_dram = nc.dram_tensor("x1_scratch", (TILES * P, C), F32, kind="Internal").ap()
    y_dram = nc.dram_tensor("y_scratch", (TILES, P, C), F32, kind="Internal").ap()
    taps_one = nc.dram_tensor("taps_scratch", (OBLOCKS, TAPROWS, 2 * OC), F16, kind="Internal").ap()
    taps_dram = nc.dram_tensor("taps_copies", (COPIES, OBLOCKS * TAPROWS * 2 * OC), F16, kind="Internal").ap()
    w1_dram = nc.dram_tensor("w1_scratch", (P, 2 * KC * HID), F16, kind="Internal").ap()
    w2_dram = nc.dram_tensor("w2_scratch", (P, 2 * KC * HID), F16, kind="Internal").ap()

    with ExitStack() as ctx:
        def sb(name, shape, dt):
            return ctx.enter_context(nc.sbuf_tensor(name, shape, dt))

        def sem(name):
            return ctx.enter_context(nc.semaphore(name))

        arena = sb("arena", [P, 5 * REG], F32)

        def area(start, cols):
            return arena[:, start:start + cols]

        ident = sb("ident", [P, P], F32)
        m_parts = sb("m_parts", [P, 2, KC, C], F16)
        ring = sb("ring", [P, 4, C], F32)
        taps = sb("taps", [P, 4, P, 2, OC], F16)
        half_bias = sb("half_bias", [P, C], F32)
        w1s = sb("w1s", [P, C], F32)
        b1s = sb("b1s", [P, C], F32)
        to_state = sb("to_state", [P, 2, P], F16)
        from_state = sb("from_state", [P, 2, P], F16)
        carry = sb("carry", [P, C], F32)
        mix_s = sb("mix_s", [P, C], F32)
        state_parts = sb("state_parts", [P, 2, C], F16)
        alpha1 = sb("alpha1", [P, TILES], F32)
        beta1 = sb("beta1", [P, TILES], F32)
        mv = sb("mv", [P, 2, GT, 2], F32)
        bn = sb("bn", [P, 2, GT, 6], F32)
        va = sb("va", [P, 8, GT], F32)
        mhalf = sb("mhalf", [P, GT], F32)
        peak = sb("peak", [P, 16], F32)
        peak_all = sb("peak_all", [P, 16], F32)
        peak_k = sb("peak_k", [P, KC], F32)
        n2ws = sb("n2ws", [P, KC], F32)
        sc = sb("sc", [P, 24], F32)
        bounds = sb("bounds", [P, 8], F32)
        ubias = sb("ubias", [P, GT], F32)
        b1p = sb("b1p", [P, HC], F32)
        colsb = sb("colsb", [P, HC + 2 * KC], F32)
        psum = ctx.enter_context(nc.psum_tensor("psum", [P, 8, 512], F32))

        xbuf = [area(i * GT * C, GT * C).rearrange("p (j c) -> p j c", j=GT) for i in range(4)]
        taps_flat = taps[:, :, :, :, :].rearrange("p r t s c -> p (r t s c)")
        one_block = P * 2 * OC
        zt = taps_flat[:, one_block:2 * one_block].rearrange("p (r s k t) -> p r s k t", r=2, s=2, k=KC)
        uring = taps_flat[:, 2 * one_block:4 * one_block].bitcast(F32).rearrange("p (r c) -> p r c", r=GT)
        u_all = area(REG, 4 * REG).bitcast(F16).rearrange("p (b s c t) -> p b s c t", b=BLOCKS, s=2, c=BLK)
        u_flat = area(REG, 4 * REG).bitcast(F16)

        taken = [REG]

        def table(*dims):
            cols = int(np.prod(dims))
            at, taken[0] = taken[0], taken[0] + cols
            return area(at, cols).rearrange("p (k n) -> p k n", k=dims[0])

        wr_sb, wi_sb, at_re, at_im, m_full = [table(KC, C) for _ in range(5)]
        cos_sb, sin_sb = table(KC, HALF), table(KC, HALF)
        first_sb = table(4, HALF)
        even_sb = table(2, HALF)
        taps_out = table(1, OBLOCKS * OC)[:, 0, :].bitcast(F16)
        taps_zero = table(1, OBLOCKS * OC)[:, 0, :].bitcast(F16)
        wfull = area(3 * REG, REG)
        wfull1 = wfull.rearrange("p (k h) -> p k h", k=KC)
        wsplit = area(4 * REG, REG).bitcast(F16)
        wsplit_k = wsplit.rearrange("p (s k h) -> p s k h", s=2, k=KC)
        flat_ring = ring[:, :, :].rearrange("p a b -> p (a b)")
        logs = flat_ring[:, 0:66]
        tmp_a = flat_ring[:, 66:132]
        tmp_b = flat_ring[:, 132:198]
        neg_a = flat_ring[:, 198:264]
        steps = flat_ring[:, 264:392]
        left = flat_ring[:, 392:393]
        onehot = flat_ring[0:1, 400:528]
        e_taps = flat_ring[:, 528:656]
        e_out = flat_ring[:, 656:784]
        e_in = flat_ring[:, 784:848]
        e_tile = flat_ring[:, 848:849]
        drow = flat_ring[0:1, 1024:1536]

        scan_out = [ring[:, i, :] for i in range(2)]
        weighted = [ring[:, 2 + i, :] for i in range(2)]

        w1_sb = area(0, REG).bitcast(F16).rearrange("p (s k h) -> p s k h", s=2, k=KC)
        w2_sb = area(REG, REG).bitcast(F16).rearrange("p (s h n) -> p s h n", s=2, h=HC)
        hid = area(2 * REG, REG).bitcast(F16).rearrange("p (s h t) -> p s h t", s=2, h=HC)
        def buffer(at):
            return area(at, GT * C).rearrange("p (j c) -> p j c", j=GT)

        at3, at4, size = 3 * REG, 4 * REG, GT * C
        rbuf = [buffer(at4), buffer(at3)]
        x2buf = [buffer(at3 + size), buffer(at3 + 2 * size)]
        ybuf = buffer(at4 + size)
        gt = area(at4 + 2 * size, size).bitcast(F16).rearrange("p (s k t) -> p s k t", s=2, k=KC)
        h32 = area(at4 + 3 * size, size).rearrange("p (r t) -> p r t", r=4)
        z3t = area(at3 + 3 * size, size).bitcast(F16).rearrange("p (j s k t) -> p j s k t", j=GT, s=2, k=KC)
        fc2_bias = b1s[:, :]
        z3 = ring

        def bank(i):
            return psum[:, i, :]

        def scale(i):
            return sc[:, i:i + 1]

        M_BANKS = (0, 4, 6, 0)
        S_U, S_K, S_W1, S_W2, S_H, S_M = range(6)
        C_Y, C_W1, C_2, C_M, C_MIX = range(8, 13)
        C_H = 16

        smalls_loaded = sem("smalls_loaded")
        tables_loaded = sem("tables_loaded")
        fc1_loaded, fc2_loaded = sem("fc1_loaded"), sem("fc2_loaded")
        fc1_stored, fc2_stored = sem("fc1_stored"), sem("fc2_stored")
        taps_stored, taps_copied = sem("taps_stored"), sem("taps_copied")
        pool_set = sem("pool_set")
        peaks_reduced = sem("peaks_reduced")
        prep_v = sem("prep_v")
        prep_a = sem("prep_a")
        prep_pe = sem("prep_pe")
        m_written, w2_peaks = sem("m_written"), sem("w2_peaks")
        bounds_ready, gate, sp_gate = sem("bounds_ready"), sem("gate"), sem("sp_gate")

        x_loaded = [sem(f"x_loaded{i}") for i in range(4)]
        x1_stored = [sem(f"x1_stored{i}") for i in range(4)]
        x_bn, x_aggr, x_var, x_rstd, x_coef = [sem(n) for n in ("x_bn", "x_aggr", "x_var", "x_rstd", "x_coef")]
        z_ready, zt_psum, zt_high, zt_low = [sem(n) for n in ("z_ready", "zt_psum", "zt_high", "zt_low")]
        ffn_psum, xb_ready, x1_ready = sem("ffn_psum"), sem("xb_ready"), sem("x1_ready")
        x1_bn, x1_aggr, x1_var, x1_rstd = [sem(n) for n in ("x1_bn", "x1_aggr", "x1_var", "x1_rstd")]
        v_var0, v_var, v_rstd, u_coef = sem("v_var0"), sem("v_var"), sem("v_rstd"), sem("u_coef")
        u_norm, u_weighted, u_done, u_high, u_low = [sem(n) for n in
                                                     ("u_norm", "u_weighted", "u_done", "u_high", "u_low")]

        taps_loaded = [sem(f"taps_loaded{i}") for i in range(4)]
        taps_zeroed = sem("taps_zeroed")
        y_first = sem("y_first")
        state_psum, state_scanned, state_mixed = sem("state_psum"), sem("state_scanned"), sem("state_mixed")
        state_high, state_low, state_zero = sem("state_high"), sem("state_low"), sem("state_zero")
        y_psum, y_staged = sem("y_psum"), sem("y_staged")
        y_stored = [sem(f"y_stored{b}") for b in range(BLOCKS)]

        w1_loaded, w2_loaded, fc2b_loaded = sem("w1_loaded"), sem("w2_loaded"), sem("fc2b_loaded")
        yg_loaded = sem("yg_loaded")
        r_loaded = [sem("r_loaded0"), sem("r_loaded1")]
        out_stored = [sem("out_stored0"), sem("out_stored1")]
        xm_sum, xm_bn, xm_aggr, xm_var, xm_rstd, xm_coef = [sem(n) for n in
                                                            ("xm_sum", "xm_bn", "xm_aggr", "xm_var", "xm_rstd",
                                                             "xm_coef")]
        r_sum, r_ready, z2_ready = sem("r_sum"), sem("r_ready"), sem("z2_ready")
        gt_psum, gt_high, gt_low = sem("gt_psum"), sem("gt_high"), sem("gt_low")
        fc1_psum, h_ready, h_high, h_low = sem("fc1_psum"), sem("h_ready"), sem("h_high"), sem("h_low")
        fc2_psum, x2_ready = sem("fc2_psum"), sem("x2_ready")
        x2_bn, x2_aggr, x2_var, x2_rstd, x2_coef = [sem(n) for n in
                                                    ("x2_bn", "x2_aggr", "x2_var", "x2_rstd", "x2_coef")]
        z3_ready, z3t_psum, z3t_high, z3t_low = [sem(n) for n in ("z3_ready", "z3t_psum", "z3t_high", "z3t_low")]
        x2b_ready, ffn2_psum, x3_ready = sem("x2b_ready"), sem("ffn2_psum"), sem("x3_ready")

        def each_group(eng, step):
            step(0, 0, 0)
            step(1, 0, 1)
            with eng.Fori(1, PAIRS - 1) as pair:
                step(2 * pair, pair, 0)
                step(2 * pair + 1, pair, 1)
            step(GROUPS - 2, PAIRS - 1, 0)
            step(GROUPS - 1, PAIRS - 1, 1)

        def is_first(g):
            return isinstance(g, int) and g == 0

        def is_last(g):
            return isinstance(g, int) and g == GROUPS - 1

        def rows(dram, g):
            return dram[bass.ds(g * (GT * P), GT * P), :].rearrange("(j p) c -> p j c", j=GT)

        def each_tile(eng, slot):
            def step(g, quad, q):
                for j in range(GT):
                    slot(g, quad, q, j)
            step(-1, -1, 3)
            for g in range(4):
                step(g, 0, g)
            with eng.Fori(1, QUADS - 1) as quad:
                for i in range(4):
                    step(4 * quad + i, quad, i)
            for g in range(GROUPS - 4, GROUPS + LAG):
                step(g, g // 4, g % 4)

        class Tile:

            def __init__(self, g, quad, q, j, d):
                over, self.j = divmod(j + d, GT)
                self.g = g + over
                turns, self.q = divmod(q + over, 4)
                self.quad = quad + turns
                self.n = 4 * self.g + self.j
                self.real = not isinstance(g, int) or 0 <= self.g < GROUPS

        def at_least(eng, semaphore, value):
            if not (isinstance(value, int) and value <= 0):
                eng.wait_ge(semaphore, value)

        N_SMALLS = 13
        V_STEPS = ("nx sp dt q_high q_low p_high p_low carry peaks0 bound0 e0 r0 scales0 vecs k_high k_low mixw "
                   "at0 at1 pk0 pk1 at2 pk2 pk3 pkw peaks1 e1 r1 scales1 at3 m0 m1 m2 m3 bound2 e2 r2 scales2 mhigh "
                   "mlow fc1bias low0 low1 low2 low3 peaks3 bound3 e3 r3 scales3 fc2low").split()
        V = {name: i + 1 for i, name in enumerate(V_STEPS)}
        A_STEPS = ("exp ln e_taps e_out e_in e_tile at0 at1 at2 at3 m0 m1 m2 m3 high0 high1 high2 high3 "
                   "fc2high").split()
        A = {name: i + 1 for i, name in enumerate(A_STEPS)}
        E_STEPS = "taps at0 at1 at2 at3 fc1bias m0 m1 m2 m3".split()
        E = {name: i + 1 for i, name in enumerate(E_STEPS)}

        block = ctx.enter_context(nc.Block())

        @block.sync
        def _(sp):
            for half in range(2):
                sp.dma_start(mix_s[half * NST:(half + 1) * NST, :], mixt).then_inc(smalls_loaded, 16)
                sp.dma_start(logs[half * NST:(half + 1) * NST, 64:65], log_tau).then_inc(smalls_loaded, 16)
            sp.dma_start(logs[:, 0:64], broadcast_rows(log_tau, NST)).then_inc(smalls_loaded, 16)
            sp.dma_start(logs[:, 65:66], broadcast_rows(log_dt, 1)).then_inc(smalls_loaded, 16)
            sp.dma_start(drow, dskip).then_inc(smalls_loaded, 16)
            sp.dma_start(colsb[:, 0:HC], fc1b).then_inc(smalls_loaded, 16)
            sp.dma_start(colsb[:, HC:HC + KC], n2w).then_inc(smalls_loaded, 16)
            sp.dma_start(colsb[:, HC + KC:HC + 2 * KC], n2b).then_inc(smalls_loaded, 16)
            sp.dma_start(half_bias[:, :], broadcast_rows(ffn_bias, C)).then_inc(smalls_loaded, 16)
            sp.dma_start(w1s[:, :], broadcast_rows(n1w, C)).then_inc(smalls_loaded, 16)
            sp.dma_start(b1s[:, :], broadcast_rows(n1b, C)).then_inc(smalls_loaded, 16)
            for dst, src in ((wr_sb, wr), (cos_sb, cos_t), (wi_sb, wi), (sin_sb, sin_t)):
                sp.dma_start(dst, src.rearrange("(k p) n -> p k n", p=P)).then_inc(tables_loaded, 16)
            sp.dma_start(wfull1, fc1t.rearrange("(k p) h -> p k h", p=P)).then_inc(fc1_loaded, 16)
            for i in range(4):
                sp.dma_start(xbuf[i], rows(x, i)).then_inc(x_loaded[i], 16)
            sp.wait_ge(pool_set, 2)
            sp.dma_start(taps_one[:, 0:P - 1, :].rearrange("b j n -> j b n"),
                         taps_zero[0:P - 1, :].rearrange("p (b n) -> p b n", b=OBLOCKS)).then_inc(taps_stored, 16)
            sp.wait_ge(prep_v, V["k_low"])
            sp.dma_start(taps_one[:, P - 1:TAPROWS, :].rearrange("b j n -> j b n"),
                         taps_out.rearrange("p (b n) -> p b n", b=OBLOCKS)).then_inc(taps_stored, 16)
            sp.wait_ge(prep_v, V["low3"])
            sp.dma_start(w1_dram, wsplit).then_inc(fc1_stored, 16)
            sp.dma_start(wfull, fc2t.rearrange("(h p) n -> p h n", p=P)).then_inc(fc2_loaded, 16)
            sp.wait_ge(prep_v, V["fc2low"])
            sp.dma_start(w2_dram, wsplit).then_inc(fc2_stored, 16)
            sp.wait_ge(taps_stored, 32)
            sp.dma_start(taps_dram, bass.AP(tensor=taps_one.tensor, offset=0,
                                            ap=[[0, COPIES], [1, OBLOCKS * TAPROWS * 2 * OC]]))\
              .then_inc(taps_copied, 16)

            def store(g, quad, q):
                sp.wait_ge(x1_ready, 4 * g + 4)
                sp.dma_start(rows(x1_dram, g), xbuf[q]).then_inc(x1_stored[q], 16)

            def load(g, quad, q):
                sp.wait_ge(u_norm, 4 * g)
                sp.sem_inc(sp_gate, 1)
                sp.wait_ge(x1_stored[(q - 1) % 4], 16 * ((quad if q else quad - 1) + 1))
                sp.dma_start(xbuf[(q - 1) % 4], rows(x, g + 3)).then_inc(x_loaded[(q - 1) % 4], 16)

            store(0, 0, 0)
            for g in range(1, 4):
                store(g, 0, g)
                load(g, 0, g)
            with sp.Fori(1, QUADS - 1) as quad:
                for q in range(4):
                    store(4 * quad + q, quad, q)
                    load(4 * quad + q, quad, q)
            store(GROUPS - 4, QUADS - 1, 0)
            load(GROUPS - 4, QUADS - 1, 0)
            for q in range(1, 4):
                store(GROUPS - 4 + q, QUADS - 1, q)

            def load_taps(o):
                copy, row, per = OBLOCKS * TAPROWS * 2 * OC, 2 * OC, P // 2 // COPIES
                for part, cols in ((0, P), (1, P // 2)):
                    dst = taps[part * (P // 2):(part + 1) * (P // 2), o % 4, P - cols:P, :, :]\
                        .rearrange("p t s c -> p (t s c)")
                    src = bass.AP(tensor=taps_dram.tensor, offset=(o * TAPROWS + P - 1) * row,
                                  ap=[[copy - per * row, COPIES], [-row, per], [1, cols * row]])
                    sp.dma_start(dst, src).then_inc(taps_loaded[o % 4], 16)

            sp.wait_ge(taps_copied, 16)
            load_taps(0)
            sp.wait_ge(ffn_psum, TILES)
            load_taps(1)
            sp.wait_ge(u_high, TILES)
            sp.wait_ge(u_low, TILES)
            load_taps(2)
            load_taps(3)
            for o in range(4, OBLOCKS):
                sp.wait_ge(y_psum, o - 3)
                load_taps(o)

            for i in range(4):
                sp.wait_ge(x1_stored[i], 16 * QUADS)
            sp.wait_ge(y_psum, OBLOCKS)
            sp.dma_start(rbuf[0], rows(x1_dram, 0)).then_inc(r_loaded[0], 16)
            sp.dma_start(fc2_bias, broadcast_rows(fc2b, C)).then_inc(fc2b_loaded, 16)
            for b in range(BLOCKS - 1):
                sp.wait_ge(y_stored[b], 16)
            sp.wait_ge(y_first, 16)

            def load_y(g):
                sp.dma_start(ybuf, y_dram[bass.ds(g * GT, GT), :, :].rearrange("j p c -> p j c"))\
                  .then_inc(yg_loaded, 16)

            def load_r(g, par):
                sp.dma_start(rbuf[par], rows(x1_dram, g)).then_inc(r_loaded[par], 16)

            load_y(0)
            sp.wait_ge(fc2_stored, 16)
            sp.dma_start(area(REG, REG).bitcast(F16), w2_dram).then_inc(w2_loaded, 16)
            sp.wait_ge(y_stored[BLOCKS - 1], 16)

            def step(g, pair, par):
                if not is_last(g):
                    sp.wait_ge(gt_psum, 4 * g + 4)
                    load_y(g + 1)
                    if not is_first(g):
                        sp.wait_ge(x2_ready, 4 * g)
                    load_r(g + 1, 1 - par)
                if not is_first(g):
                    sp.wait_ge(x3_ready, 4 * g)
                    sp.dma_start(rows(out, g - 1), x2buf[1 - par]).then_inc(out_stored[1 - par], 16)
            each_group(sp, step)
            sp.wait_ge(x3_ready, TILES)
            sp.dma_start(rows(out, GROUPS - 1), x2buf[1]).then_inc(out_stored[1], 16)
            for i in range(2):
                sp.wait_ge(out_stored[i], 16 * PAIRS)

        @block.gpsimd
        def _(pool):
            pool.memset(peak[:, :], 0.0).then_inc(pool_set, 1)
            pool.memset(taps_zero, 0.0).then_inc(pool_set, 1)
            pool.memset(mhalf[:, :], -0.5).then_inc(pool_set, 1)
            pool.memset(onehot, 0.0).then_inc(pool_set, 1)
            pool.memset(ident[:, :], 0.0).then_inc(pool_set, 1)
            pool.memset(carry[:, :], 1.0).then_inc(pool_set, 1)
            pool.memset(from_state[:, :, :], 0.0).then_inc(pool_set, 1)
            pool.iota(steps, [[1, P]], base=0, channel_multiplier=0, allow_small_or_imprecise_dtypes=True)\
                .then_inc(pool_set, 1)
            pool.iota(left, [[0, 1]], base=P - 1, channel_multiplier=-1, allow_small_or_imprecise_dtypes=True)\
                .then_inc(pool_set, 1)
            pool.wait_ge(pool_set, 7)
            pool.memset(flat_ring[0:1, 400:401], 1.0).then_inc(pool_set, 1)
            pool.affine_select(out=ident[:, :], in_=ident[:, :], compare_op=ALU.not_equal, fill=1.0, base=0,
                               pattern=[[-1, P]], channel_multiplier=1).then_inc(pool_set, 1)
            pool.memset(carry[:, 0:C:PER_BATCH], 0.0).then_inc(pool_set, 1)

            def reduce_peaks(i):
                pool.wait_ge(prep_v, V[f"peaks{i}" if i != 2 else "m3"])
                a, b = ((0, 4), (4, 5), (5, 9), (9, 11))[i]
                pool.partition_all_reduce(peak_all[:, a:b], peak[:, a:b], P, RMAX).then_inc(peaks_reduced, 1)

            def power(dst, src, done):
                pool.tensor_tensor(dst, src, mhalf[:, :], ALU.pow).then_inc(done, 1)

            def x_power(g):
                pool.wait_ge(x_var, g + 1)
                at_least(pool, z_ready, 4 * g)
                power(va[:, 1, :], va[:, 0, :], x_rstd)

            reduce_peaks(0)
            x_power(0)
            reduce_peaks(1)
            reduce_peaks(2)

            def slot(g, quad, q, j):
                if isinstance(g, int) and (g, j) == (0, 3):
                    reduce_peaks(3)
                t = Tile(g, quad, q, j, 0)
                if t.real:
                    pool.wait_ge(z_ready, t.n + 1)
                    pool.tensor_tensor(xbuf[q][:, j, :], xbuf[q][:, j, :], half_bias[:, :], ALU.add)\
                        .then_inc(xb_ready, 1)
                before, after = Tile(g, quad, q, j, -GT), Tile(g, quad, q, j, GT)
                if j == 0 and before.real:
                    pool.wait_ge(x1_var, before.g + 1)
                    power(va[:, 4, :], va[:, 3, :], x1_rstd)
                if j == 1:
                    if before.real:
                        pool.wait_ge(v_var, before.g + 1)
                        power(va[:, 6, :], va[:, 5, :], v_rstd)
                    if after.real and not is_first(after.g):
                        x_power(after.g)
                t = Tile(g, quad, q, j, -6)
                if t.real:
                    pool.wait_ge(u_norm, t.n + 1)
                    pool.tensor_tensor(uring[:, t.j, :], uring[:, t.j, :], w1s[:, :], ALU.mult)\
                        .then_inc(u_weighted, 1)
            pool.wait_ge(prep_v, V["vecs"])
            each_tile(pool, slot)

            pool.wait_ge(ffn_psum, TILES)
            pool.wait_ge(u_high, TILES)
            pool.wait_ge(u_low, TILES)
            pool.memset(taps[P // 2:P, :, 0:P // 2, :, :].rearrange("p r t s c -> p r (t s c)"), 0.0)\
                .then_inc(taps_zeroed, 1)

            def mix(o, i):
                pool.wait_ge(state_scanned, o + 1)
                if not (isinstance(o, int) and o < 2):
                    pool.wait_ge(state_low, o - 1)
                pool.tensor_tensor(weighted[i].rearrange("p (c t) -> p c t", c=OC),
                                   scan_out[i].rearrange("p (c t) -> p c t", c=OC),
                                   mix_s[:, bass.ds(o * OC, OC)].unsqueeze(2).to_broadcast([P, OC, TILES]),
                                   ALU.mult).then_inc(state_mixed, 1)

            mix(0, 0)
            mix(1, 1)
            with pool.Fori(1, C // OC // 2) as h:
                mix(2 * h, 0)
                mix(2 * h + 1, 1)

            def residual(g, par):
                pool.wait_ge(xm_var, g + 1)
                power(va[:, 1, :], va[:, 0, :], xm_rstd)
                for j in range(GT):
                    pool.wait_ge(r_sum, 4 * g + j + 1)
                    pool.tensor_tensor(rbuf[par][:, j, :], rbuf[par][:, j, :], fc2_bias, ALU.add)\
                        .then_inc(r_ready, 1)

            pool.wait_ge(fc2b_loaded, 16)
            residual(0, 0)

            def step(g, pair, par):
                if not is_first(g):
                    for j in range(GT):
                        pool.wait_ge(z3_ready, 4 * (g - 1) + j + 1)
                        pool.tensor_tensor(x2buf[1 - par][:, j, :], x2buf[1 - par][:, j, :], half_bias[:, :],
                                           ALU.add).then_inc(x2b_ready, 1)
                if not is_last(g):
                    pool.wait_ge(z2_ready, 4 * g + 4)
                    residual(g + 1, 1 - par)
                pool.wait_ge(x2_var, g + 1)
                power(va[:, 4, :], va[:, 3, :], x2_rstd)
            each_group(pool, step)
            for j in range(GT):
                pool.wait_ge(z3_ready, 4 * (GROUPS - 1) + j + 1)
                pool.tensor_tensor(x2buf[1][:, j, :], x2buf[1][:, j, :], half_bias[:, :], ALU.add)\
                    .then_inc(x2b_ready, 1)

        @block.scalar
        def _(act):
            act.wait_ge(prep_v, V["nx"])
            act.activation(tmp_b, tmp_a, ACT.Exp).then_inc(prep_a, 1)
            act.wait_ge(prep_a, A["exp"])
            act.activation(tmp_b, tmp_b, ACT.Ln, bias=1.0).then_inc(prep_a, 1)
            act.wait_ge(prep_v, V["dt"])
            act.wait_ge(pool_set, 9)
            act.activation(e_taps, steps, ACT.Exp, scale=neg_a[:, 64:65]).then_inc(prep_a, 1)
            act.activation(e_out, steps, ACT.Exp, scale=neg_a[:, 64:65], bias=neg_a[:, 64:65]).then_inc(prep_a, 1)
            act.activation(e_in, neg_a[:, 0:64], ACT.Exp, scale=left).then_inc(prep_a, 1)
            act.activation(e_tile, neg_a[:, 64:65], ACT.Exp, scale=float(P)).then_inc(prep_a, 1)
            for oc in range(KC):
                act.wait_ge(prep_pe, E[f"at{oc}"])
                if oc >= 2:
                    act.wait_ge(prep_v, V[f"at{oc - 2}"])
                b = 4 * (oc % 2)
                act.activation(first_sb[:, 2 * (oc % 2), :], bank(b)[:, 0:HALF], ACT.Copy)
                act.activation(first_sb[:, 2 * (oc % 2) + 1, :], bank(b + 2)[:, 0:HALF], ACT.Copy)\
                   .then_inc(prep_a, 1)
            for i in range(KC):
                act.wait_ge(prep_pe, E[f"m{i}"])
                if i >= 2:
                    act.wait_ge(prep_v, V[f"m{i - 2}"])
                act.activation(even_sb[:, i % 2, :], bank(M_BANKS[i])[:, 0:HALF], ACT.Copy).then_inc(prep_a, 1)
            act.wait_ge(prep_v, V["scales1"])
            for k in range(KC):
                act.activation(wsplit_k[:, 0, k, :], wfull1[:, k, :], ACT.Copy, scale=n2ws[:, k:k + 1])\
                   .then_inc(prep_a, 1)

            def slot(g, quad, q, j):
                if isinstance(g, int) and (g, j) == (1, 1):
                    act.wait_ge(fc1_stored, 16)
                    act.wait_ge(prep_v, V["scales3"])
                    act.activation(wsplit[:, 0:REG], wfull, ACT.Copy, scale=scale(S_W2)).then_inc(prep_a, 1)
                t = Tile(g, quad, q, j, 1)
                if t.real:
                    act.wait_ge(zt_psum, t.n + 1)
                    at_least(act, ffn_psum, t.n - 1)
                    act.activation(zt[:, t.j % 2, 0, :, :].rearrange("p k t -> p (k t)"), bank(t.j % 2), ACT.Copy)\
                       .then_inc(zt_high, 1)
                t = Tile(g, quad, q, j, 2)
                if t.real:
                    act.wait_ge(x_coef, t.g + 1)
                    at_least(act, zt_psum, t.n - 3)
                    act.activation(ring[:, t.j, :], xbuf[t.q][:, t.j, :], ACT.Identity,
                                   scale=va[:, 1, t.j:t.j + 1], bias=va[:, 2, t.j:t.j + 1]).then_inc(z_ready, 1)
                t = Tile(g, quad, q, j, -6)
                if t.real:
                    act.wait_ge(u_coef, t.g + 1)
                    at_least(act, u_low, t.n - 3)
                    act.activation(uring[:, t.j, :], xbuf[t.q][:, t.j, :], ACT.Identity,
                                   scale=va[:, 7, t.j:t.j + 1], bias=ubias[:, t.j:t.j + 1]).then_inc(u_norm, 1)
                t = Tile(g, quad, q, j, -8)
                if t.real:
                    if isinstance(t.n, int) and t.n == 0:
                        act.wait_ge(fc2_stored, 16)
                    act.wait_ge(u_done, t.n + 1)
                    act.activation(u_all[:, :, 0, :, bass.ds(t.n, 1)],
                                   uring[:, t.j, :].rearrange("p (b c o) -> p b c o", b=BLOCKS, o=1), ACT.Copy)\
                       .then_inc(u_high, 1)
            each_tile(act, slot)

            def state_part(o, i):
                act.wait_ge(state_mixed, o + 1)
                if not (isinstance(o, int) and o < 2):
                    act.wait_ge(y_psum, o - 1)
                src = weighted[i].rearrange("p (c t) -> p c t", t=PER_BATCH)[:, :, 0:PER_BATCH - 1]
                dst = state_parts[:, i, :].rearrange("p (c t) -> p c t", t=PER_BATCH)[:, :, 1:PER_BATCH]
                act.activation(dst, src, ACT.Copy).then_inc(state_high, 1)

            def stage_y(blk, o, i):
                act.wait_ge(y_psum, o + 1)
                stage = area(blk * REG, REG).rearrange("p (t c) -> p c t", c=BLK)
                act.activation(stage[:, bass.ds((o - blk * (BLK // OC)) * OC, OC), :],
                               bank(4 + i).rearrange("p (c t) -> p c t", c=OC), ACT.Copy, scale=scale(C_Y))\
                   .then_inc(y_staged, 1)

            for i in range(4):
                act.wait_ge(x1_stored[i], 16 * QUADS)
            def store_y(blk, a, b, done):
                act.wait_ge(y_staged, (blk + 1) * BLK // OC)
                stage = area(blk * REG, REG).rearrange("p (t c) -> p t c", t=TILES)
                act.dma_start(y_dram[a:b, :, blk * BLK:(blk + 1) * BLK].rearrange("t p c -> p t c"),
                              stage[:, a:b, :]).then_inc(done, 16)

            def two(blk, h):
                for i in range(2):
                    o = 2 * h + (blk * (BLK // OC) + i)
                    state_part(o + 1, 1 - i)
                    stage_y(blk, o, i)

            state_part(0, 0)
            for blk in range(BLOCKS):
                if blk == 0:
                    two(0, 0)
                with act.Fori(1 if blk == 0 else 0, BLK // OC // 2 - (1 if blk == BLOCKS - 1 else 0)) as h:
                    two(blk, h)
                if blk < BLOCKS - 1:
                    store_y(blk, 0, TILES, y_stored[blk])
                if blk == 1:
                    act.wait_ge(fc1_stored, 16)
                    act.wait_ge(y_stored[0], 16)
                    act.dma_start(area(0, REG).bitcast(F16), w1_dram).then_inc(w1_loaded, 16)
            act_last = C // OC - 2
            state_part(act_last + 1, 1)
            stage_y(BLOCKS - 1, act_last, 0)
            stage_y(BLOCKS - 1, act_last + 1, 1)
            store_y(BLOCKS - 1, 0, GT, y_first)
            store_y(BLOCKS - 1, GT, TILES, y_stored[BLOCKS - 1])

            def z2(g, j):
                act.wait_ge(xm_coef, g + 1)
                act.wait_ge(r_sum, 4 * g + j + 1)
                act.activation(ybuf[:, j, :], ybuf[:, j, :], ACT.Identity,
                               scale=va[:, 1, j:j + 1], bias=va[:, 2, j:j + 1]).then_inc(z2_ready, 1)

            def g_high(g, j):
                act.wait_ge(gt_psum, 4 * g + j + 1)
                act.activation(gt[:, 0, :, j * P:(j + 1) * P], bank(2 + j % 2).rearrange("p (k t) -> p k t", k=KC),
                               ACT.Copy).then_inc(gt_high, 1)

            def z3_norm(g, par):
                act.wait_ge(x2_coef, g + 1)
                for j in range(GT):
                    act.activation(z3[:, j, :], x2buf[par][:, j, :], ACT.Identity,
                                   scale=va[:, 4, j:j + 1], bias=va[:, 5, j:j + 1]).then_inc(z3_ready, 1)

            def z3_high(g, j):
                act.wait_ge(z3t_psum, 4 * g + j + 1)
                act.activation(z3t[:, j, 0, :, :].rearrange("p k t -> p (k t)"), bank(2 + j % 2), ACT.Copy)\
                   .then_inc(z3t_high, 1)

            for j in range(GT):
                z2(0, j)
            for j in range(GT):
                g_high(0, j)

            def step(g, pair, par):
                if not is_first(g):
                    z3_norm(g - 1, 1 - par)
                for hc in range(HC):
                    act.wait_ge(fc1_psum, HC * g + hc + 1)
                    if not (is_first(g) and hc < 4):
                        act.wait_ge(h_low, HC * g + hc - 3)
                    act.activation(h32[:, hc % 4, :],
                                   bank(hc % 2), ACT.Gelu, scale=scale(C_W1), bias=b1p[:, hc:hc + 1])\
                       .then_inc(h_ready, 1)
                    if hc in (3, 5, 7, 9) and not is_first(g):
                        z3_high(g - 1, (hc - 3) // 2)
                    if 10 <= hc < 14 and not is_last(g):
                        z2(g + 1, hc - 10)
                if not is_last(g):
                    for j in range(GT):
                        g_high(g + 1, j)
            each_group(act, step)
            z3_norm(GROUPS - 1, 1)
            for j in range(GT):
                z3_high(GROUPS - 1, j)

        @block.vector
        def _(dve):
            count = [0]

            def done(ins, name):
                count[0] += 1
                assert V[name] == count[0], name
                ins.then_inc(prep_v, 1)
                return ins

            def own(name):
                dve.wait_ge(prep_v, V[name])

            dve.wait_ge(smalls_loaded, 16 * N_SMALLS)
            done(dve.scalar_tensor_tensor(out=tmp_a, in0=logs, scalar=-1.0, in1=logs, op0=ALU.mult, op1=ALU.min),
                 "nx")
            dve.wait_ge(prep_a, A["ln"])
            done(dve.scalar_tensor_tensor(out=tmp_a, in0=logs, scalar=0.0, in1=tmp_b, op0=ALU.max, op1=ALU.add),
                 "sp")
            own("sp")
            done(dve.tensor_scalar(neg_a[:, 0:65], tmp_a[:, 0:65], tmp_a[:, 65:66], -1.0, ALU.mult, ALU.mult), "dt")
            dve.wait_ge(prep_a, A["e_tile"])
            dve.wait_ge(pool_set, 12)
            big = 32768.0
            done(dve.tensor_scalar(from_state[:, 0, :], e_out, big, None, ALU.mult), "q_high")
            own("q_high")
            done(dve.scalar_tensor_tensor(out=from_state[0:NST, 1, :], in0=e_out[0:NST, :], scalar=big,
                                          in1=from_state[0:NST, 0, :], op0=ALU.mult, op1=ALU.subtract), "q_low")
            for half in range(2):
                ins = dve.tensor_scalar(to_state[:, 0, half * NST:(half + 1) * NST], e_in, big, None, ALU.mult)
            done(ins, "p_high")
            own("p_high")
            for half in range(2):
                ins = dve.scalar_tensor_tensor(out=to_state[:, 1, half * NST:(half + 1) * NST], in0=e_in,
                                               scalar=big, in1=to_state[:, 0, half * NST:(half + 1) * NST],
                                               op0=ALU.mult, op1=ALU.subtract)
            done(ins, "p_low")
            done(dve.tensor_scalar(carry[:, :], carry[:, :], e_tile, None, ALU.mult), "carry")

            def peak_of(col, ap, parts=P, axis=AX_X):
                return dve.tensor_reduce(peak[0:parts, col:col + 1], ap, axis, ALU.max, apply_absolute_value=True)

            peak_of(0, mix_s[:, :])
            peak_of(1, drow, 1)
            peak_of(2, w1s[:, :])
            ins = peak_of(3, b1s[:, :])
            done(ins, "peaks0")
            dve.wait_ge(peaks_reduced, 1)
            dve.scalar_tensor_tensor(out=bounds[:, 0:1], in0=peak_all[:, 2:3], scalar=23.0, in1=peak_all[:, 3:4],
                                     op0=ALU.mult, op1=ALU.add)
            done(dve.scalar_tensor_tensor(out=bounds[:, 1:2], in0=peak_all[:, 0:1], scalar=1024.0,
                                          in1=peak_all[:, 1:2], op0=ALU.mult, op1=ALU.add), "bound0")

            def exponents(n, src, name):
                dve.tensor_scalar(bounds[:, 0:n], src, 2.0 ** -100, None, ALU.max).then_inc(bounds_ready, 1)
                dve.wait_ge(bounds_ready, name + 1)
                done(dve.tensor_scalar(bounds[:, 0:n].bitcast(I32), bounds[:, 0:n].bitcast(I32), 0x7F800000, None,
                                       ALU.bitwise_and), f"e{name}")
                own(f"e{name}")
                done(dve.reciprocal(bounds[:, 4:4 + n], bounds[:, 0:n]), f"r{name}")
                own(f"r{name}")

            own("bound0")
            exponents(2, bounds[:, 0:2], 0)
            dve.tensor_scalar(scale(S_U), bounds[:, 4:5], 2.0 ** 14, None, ALU.mult)
            dve.tensor_scalar(scale(S_K), bounds[:, 5:6], 2.0 ** 14, None, ALU.mult)
            dve.tensor_scalar(scale(C_MIX), bounds[:, 5:6], 2.0 ** -16, None, ALU.mult)
            done(dve.tensor_scalar(scale(C_Y), bounds[:, 0:1], bounds[:, 1:2], 2.0 ** -28, ALU.mult, ALU.mult),
                 "scales0")
            own("scales0")
            dve.tensor_scalar(half_bias[:, :], half_bias[:, :], 0.5, None, ALU.mult)
            dve.tensor_scalar(w1s[:, :], w1s[:, :], scale(S_U), None, ALU.mult)
            done(dve.tensor_scalar(b1s[:, :], b1s[:, :], scale(S_U), None, ALU.mult), "vecs")
            dve.wait_ge(prep_pe, E["taps"])
            k_psum = bank(7).rearrange("p (b c) -> p b c", c=OC)
            k_out = taps_out.rearrange("p (b s c) -> p b s c", s=2, c=OC)
            done(dve.tensor_scalar(k_out[:, :, 0, :], k_psum, scale(S_K), None, ALU.mult), "k_high")
            own("k_high")
            done(dve.scalar_tensor_tensor(out=k_out[:, :, 1, :], in0=k_psum, scalar=scale(S_K),
                                          in1=k_out[:, :, 0, :], op0=ALU.mult, op1=ALU.subtract), "k_low")
            done(dve.tensor_scalar(mix_s[:, :], mix_s[:, :], scale(C_MIX), None, ALU.mult), "mixw")

            def moments(tiles, chain, bn_done, aggr_done, var_done, var_out, g, waits, some=range(GT)):
                for j in some:
                    waits(j)
                    ins = dve.bn_stats(bn[:, chain, j, :], tiles[:, j, :])
                if GT - 1 not in some:
                    return
                ins.then_inc(bn_done, 1)
                dve.wait_ge(bn_done, g + 1)
                dve.sem_inc(gate, 1)
                for j in range(GT):
                    ins = dve.bn_aggr(mv[:, chain, j, :], bn[:, chain, j, :])
                ins.then_inc(aggr_done, 1)
                dve.wait_ge(aggr_done, g + 1)
                dve.tensor_scalar(var_out, mv[:, chain, :, 1], EPS, None, ALU.add).then_inc(var_done, 1)

            def x_moments(g, quad, q, some):
                if 0 in some:
                    dve.wait_ge(x_loaded[q], 16 * quad + 16)
                if GT - 1 in some:
                    at_least(dve, x_rstd, g)
                moments(xbuf[q], 0, x_bn, x_aggr, x_var, va[:, 0, :], g, lambda j: None, some)

            def x_shift(g):
                dve.wait_ge(x_rstd, g + 1)
                dve.scalar_tensor_tensor(out=va[:, 2, :], in0=mv[:, 0, :, 0], scalar=-1.0, in1=va[:, 1, :],
                                         op0=ALU.mult, op1=ALU.mult).then_inc(x_coef, 1)

            def a_transposed(oc):
                dve.wait_ge(prep_a, A[f"at{oc}"])
                b = 4 * (oc % 2)
                for dst, first, psum_term, sign in ((at_re, first_sb[:, 2 * (oc % 2), :], bank(b + 1), 1),
                                                    (at_im, first_sb[:, 2 * (oc % 2) + 1, :], bank(b + 3), -1)):
                    rest = dst[:, oc, C - 1:HALF - 1:-1]
                    if sign > 0:
                        dve.tensor_tensor(dst[:, oc, 0:HALF], first, psum_term[:, 0:HALF], ALU.add)
                        dve.tensor_tensor(rest, first[:, 1:HALF - 1], psum_term[:, 1:HALF - 1], ALU.subtract)
                    else:
                        dve.tensor_tensor(dst[:, oc, 0:HALF], first, psum_term[:, 0:HALF], ALU.subtract)
                        ins = dve.scalar_tensor_tensor(out=rest, in0=psum_term[:, 1:HALF - 1], scalar=-1.0,
                                                       in1=first[:, 1:HALF - 1], op0=ALU.mult, op1=ALU.subtract)
                done(ins, f"at{oc}")

            def peak_chunk(k):
                dve.wait_ge(fc1_loaded, 16)
                done(dve.tensor_reduce(peak_k[:, k:k + 1], wfull1[:, k, :], AX_X, ALU.max,
                                       apply_absolute_value=True), f"pk{k}")

            a_transposed(0)
            a_transposed(1)
            peak_chunk(0)
            peak_chunk(1)
            a_transposed(2)
            peak_chunk(2)
            peak_chunk(3)
            own("pk3")
            done(dve.tensor_tensor(peak_k[:, :], peak_k[:, :], colsb[:, HC:HC + KC], ALU.mult), "pkw")
            own("pkw")
            done(peak_of(4, peak_k[:, :]), "peaks1")
            x_moments(0, 0, 0, range(GT))
            dve.wait_ge(peaks_reduced, 2)
            exponents(1, peak_all[:, 4:5], 1)
            dve.tensor_scalar(scale(C_W1), bounds[:, 0:1], 2.0 ** -14, None, ALU.mult)
            done(dve.tensor_scalar(n2ws[:, :], colsb[:, HC:HC + KC], bounds[:, 4:5], 2.0 ** 14, ALU.mult, ALU.mult),
                 "scales1")
            a_transposed(3)
            x_shift(0)
            for i in range(KC):
                dve.wait_ge(prep_a, A[f"m{i}"])
                odd = bank(M_BANKS[i] + 1)
                dve.tensor_tensor(m_full[:, i, 0:HALF], even_sb[:, i % 2, :], odd[:, 0:HALF], ALU.add)
                dve.tensor_tensor(m_full[:, i, C - 1:HALF - 1:-1], even_sb[:, i % 2, 1:HALF - 1],
                                  odd[:, 1:HALF - 1], ALU.subtract).then_inc(m_written, 1)
                dve.wait_ge(m_written, i + 1)
                done(peak_of(5 + i, m_full[:, i, :]), f"m{i}")
            dve.wait_ge(peaks_reduced, 3)
            done(dve.tensor_reduce(bounds[:, 2:3], peak_all[:, 5:9], AX_X, ALU.max), "bound2")
            own("bound2")
            exponents(1, bounds[:, 2:3], 2)
            dve.tensor_scalar(scale(S_M), bounds[:, 4:5], 2.0 ** 14, None, ALU.mult)
            done(dve.tensor_scalar(scale(C_M), bounds[:, 0:1], 2.0 ** -14 * 0.5 / C, None, ALU.mult), "scales2")
            own("scales2")
            m_flat = m_parts[:, :, :, :].rearrange("p s k n -> p s (k n)")
            m_src = m_full.rearrange("p k n -> p (k n)")
            done(dve.tensor_scalar(m_flat[:, 0, :], m_src, scale(S_M), None, ALU.mult), "mhigh")
            own("mhigh")
            done(dve.scalar_tensor_tensor(out=m_flat[:, 1, :], in0=m_src, scalar=scale(S_M), in1=m_flat[:, 0, :],
                                          op0=ALU.mult, op1=ALU.subtract), "mlow")

            dve.wait_ge(prep_pe, E["fc1bias"])
            done(dve.tensor_tensor(b1p[:, :], bank(3)[:, 0:HC], colsb[:, 0:HC], ALU.add), "fc1bias")
            for k in range(KC):
                dve.wait_ge(prep_a, A[f"high{k}"])
                done(dve.scalar_tensor_tensor(out=wsplit_k[:, 1, k, :], in0=wfull1[:, k, :],
                                              scalar=n2ws[:, k:k + 1], in1=wsplit_k[:, 0, k, :],
                                              op0=ALU.mult, op1=ALU.subtract), f"low{k}")

            def second_layer(piece):
                if piece == 0:
                    dve.wait_ge(fc2_loaded, 16)
                if piece < 4:
                    dve.tensor_reduce(peak_k[:, piece:piece + 1], wfull[:, piece * HID:(piece + 1) * HID], AX_X,
                                      ALU.max, apply_absolute_value=True).then_inc(w2_peaks, 1)
                if piece == 3:
                    dve.wait_ge(w2_peaks, 4)
                    dve.wait_ge(prep_v, V["fc1bias"])
                    peak_of(9, peak_k[:, :])
                    done(peak_of(10, b1p[:, :]), "peaks3")
                if piece == 4:
                    dve.wait_ge(peaks_reduced, 4)
                    dve.tensor_copy(bounds[:, 2:3], peak_all[:, 9:10])
                    done(dve.scalar_tensor_tensor(out=bounds[:, 3:4], in0=peak_all[:, 4:5], scalar=float(C),
                                                  in1=peak_all[:, 10:11], op0=ALU.mult, op1=ALU.add), "bound3")
                    own("bound3")
                    exponents(2, bounds[:, 2:4], 3)
                    dve.tensor_scalar(scale(S_W2), bounds[:, 4:5], 2.0 ** 14, None, ALU.mult)
                    dve.tensor_scalar(scale(S_H), bounds[:, 5:6], 2.0 ** 14, None, ALU.mult)
                    done(dve.tensor_scalar(scale(C_2), bounds[:, 0:1], bounds[:, 1:2], 2.0 ** -28, ALU.mult,
                                           ALU.mult), "scales3")
                if piece == 5:
                    dve.wait_ge(prep_a, A["fc2high"])
                if piece >= 5:
                    a = (piece - 5) * HID
                    ins = dve.scalar_tensor_tensor(out=wsplit[:, REG + a:REG + a + HID], in0=wfull[:, a:a + HID],
                                                   scalar=scale(S_W2), in1=wsplit[:, a:a + HID],
                                                   op0=ALU.mult, op1=ALU.subtract)
                    if piece == 8:
                        done(ins, "fc2low")

            def v_variance(g):
                dve.wait_ge(x1_rstd, g + 1)
                dve.tensor_tensor(va[:, 5, :], mv[:, 1, :, 1], va[:, 4, :], ALU.mult).then_inc(v_var0, 1)
                dve.wait_ge(v_var0, 3 * g + 1)
                dve.tensor_tensor(va[:, 5, :], va[:, 5, :], va[:, 4, :], ALU.mult).then_inc(v_var0, 1)
                dve.wait_ge(v_var0, 3 * g + 2)
                dve.tensor_scalar(va[:, 5, :], va[:, 5, :], EPS, None, ALU.add).then_inc(v_var, 1)
                at = bass.ds(4 * g, GT)
                dve.tensor_copy(alpha1[:, at], va[:, 4, :])
                dve.scalar_tensor_tensor(out=beta1[:, at], in0=mv[:, 1, :, 0], scalar=-1.0, in1=va[:, 4, :],
                                         op0=ALU.mult, op1=ALU.mult).then_inc(v_var0, 1)

            def u_coefs(g):
                dve.wait_ge(v_rstd, g + 1)
                dve.wait_ge(v_var0, 3 * g + 3)
                dve.tensor_tensor(va[:, 7, :], va[:, 4, :], va[:, 6, :], ALU.mult)
                dve.tensor_tensor(ubias[:, :], beta1[:, bass.ds(4 * g, GT)], va[:, 6, :], ALU.mult)\
                   .then_inc(u_coef, 1)

            def slot(g, quad, q, j):
                before, after = Tile(g, quad, q, j, -GT), Tile(g, quad, q, j, GT)
                if j == 2:
                    if after.real and not is_first(after.g):
                        x_shift(after.g)
                    if before.real:
                        u_coefs(before.g)
                t = Tile(g, quad, q, j, 1)
                if t.real:
                    dve.wait_ge(zt_high, t.n + 1)
                    dve.tensor_tensor(zt[:, t.j % 2, 1, :, :].rearrange("p k t -> p (k t)"), bank(t.j % 2),
                                      zt[:, t.j % 2, 0, :, :].rearrange("p k t -> p (k t)"), ALU.subtract)\
                       .then_inc(zt_low, 1)
                t = Tile(g, quad, q, j, -1)
                if t.real:
                    def x1(i):
                        dve.wait_ge(ffn_psum, t.n + 1)
                        dve.wait_ge(xb_ready, t.n + 1)
                        dve.scalar_tensor_tensor(out=xbuf[t.q][:, t.j, :], in0=bank(2 + t.j % 2), scalar=scale(C_M),
                                                 in1=xbuf[t.q][:, t.j, :], op0=ALU.mult, op1=ALU.add)\
                           .then_inc(x1_ready, 1)
                        dve.wait_ge(x1_ready, t.n + 1)
                    moments(xbuf[t.q], 1, x1_bn, x1_aggr, x1_var, va[:, 3, :], t.g, x1, [t.j])
                if j == 1 and before.real:
                    v_variance(before.g)
                if j < 2 and after.real and not is_first(after.g):
                    x_moments(after.g, after.quad, after.q, [2 * j, 2 * j + 1])
                if isinstance(g, int) and g in (0, 1, 2):
                    pieces = {(0, 0): [0], (0, 1): [1], (0, 2): [2], (0, 3): [3], (1, 0): [4], (1, 1): [],
                              (1, 2): [5], (1, 3): [6], (2, 0): [7, 8]}.get((g, j), [])
                    for piece in pieces:
                        second_layer(piece)
                t = Tile(g, quad, q, j, -7)
                if t.real:
                    dve.wait_ge(u_weighted, t.n + 1)
                    dve.tensor_tensor(uring[:, t.j, :], uring[:, t.j, :], b1s[:, :], ALU.add).then_inc(u_done, 1)
                t = Tile(g, quad, q, j, -8)
                if t.real:
                    dve.wait_ge(u_high, t.n + 1)
                    at = bass.ds(t.n, 1)
                    dve.tensor_tensor(u_all[:, :, 1, :, at],
                                      uring[:, t.j, :].rearrange("p (b c o) -> p b c o", b=BLOCKS, o=1),
                                      u_all[:, :, 0, :, at], ALU.subtract).then_inc(u_low, 1)
            each_tile(dve, slot)

            firsts = state_parts[:, :, :].rearrange("p i (c t) -> p i c t", t=PER_BATCH)[:, :, :, 0:1]
            dve.memset(firsts, 0.0).then_inc(state_zero, 1)

            def scan(o, i):
                dve.wait_ge(state_psum, o + 1)
                if not (isinstance(o, int) and o < 2):
                    dve.wait_ge(state_mixed, o - 1)
                dve.tensor_tensor_scan(scan_out[i], carry[:, :], bank(i), 0.0, ALU.mult, ALU.add)\
                   .then_inc(state_scanned, 1)

            def low_part(o, i):
                dve.wait_ge(state_high, o + 1)
                src = weighted[i].rearrange("p (c t) -> p c t", t=PER_BATCH)[NST:P, :, 0:PER_BATCH - 1]
                dst = state_parts[:, i, :].rearrange("p (c t) -> p c t", t=PER_BATCH)[NST:P, :, 1:PER_BATCH]
                dve.tensor_tensor(dst, src, dst, ALU.subtract).then_inc(state_low, 1)

            scan(0, 0)
            scan(1, 1)
            low_part(0, 0)
            with dve.Fori(1, C // OC // 2) as h:
                scan(2 * h, 0)
                low_part(2 * h - 1, 1)
                scan(2 * h + 1, 1)
                low_part(2 * h, 0)
            low_part(C // OC - 1, 1)

            def mixed(g, j, pair, par):
                if j == 0:
                    dve.wait_ge(yg_loaded, 16 * g + 16)
                    dve.wait_ge(r_loaded[par], 16 * pair + 16)
                dve.scalar_tensor_tensor(out=ybuf[:, j, :], in0=rbuf[par][:, j, :],
                                         scalar=alpha1[:, bass.ds(4 * g + j, 1)], in1=ybuf[:, j, :],
                                         op0=ALU.mult, op1=ALU.add).then_inc(xm_sum, 1)
                dve.wait_ge(xm_sum, 4 * g + j + 1)
                ins = dve.bn_stats(bn[:, 0, j, :], ybuf[:, j, :])
                if j == GT - 1:
                    ins.then_inc(xm_bn, 1)
                    dve.wait_ge(xm_bn, g + 1)
                    dve.sem_inc(gate, 1)
                    for i in range(GT):
                        ins = dve.bn_aggr(mv[:, 0, i, :], bn[:, 0, i, :])
                    ins.then_inc(xm_aggr, 1)
                    dve.wait_ge(xm_aggr, g + 1)
                    dve.tensor_scalar(va[:, 0, :], mv[:, 0, :, 1], EPS, None, ALU.add).then_inc(xm_var, 1)

            def mixed_shift(g):
                dve.wait_ge(xm_rstd, g + 1)
                if not is_first(g):
                    dve.wait_ge(z2_ready, 4 * g)
                dve.scalar_tensor_tensor(out=va[:, 2, :], in0=mv[:, 0, :, 0], scalar=-1.0, in1=va[:, 1, :],
                                         op0=ALU.mult, op1=ALU.mult).then_inc(xm_coef, 1)

            def residual(g, j, par):
                dve.scalar_tensor_tensor(out=rbuf[par][:, j, :], in0=ybuf[:, j, :],
                                         scalar=beta1[:, bass.ds(4 * g + j, 1)], in1=rbuf[par][:, j, :],
                                         op0=ALU.add, op1=ALU.add).then_inc(r_sum, 1)

            def g_low(g, j):
                dve.wait_ge(gt_high, 4 * g + j + 1)
                dve.tensor_tensor(gt[:, 1, :, j * P:(j + 1) * P], bank(2 + j % 2).rearrange("p (k t) -> p k t", k=KC),
                                  gt[:, 0, :, j * P:(j + 1) * P], ALU.subtract).then_inc(gt_low, 1)

            def z3_low(g, j):
                dve.wait_ge(z3t_high, 4 * g + j + 1)
                dve.tensor_tensor(z3t[:, j, 1, :, :].rearrange("p k t -> p (k t)"), bank(2 + j % 2),
                                  z3t[:, j, 0, :, :].rearrange("p k t -> p (k t)"), ALU.subtract)\
                   .then_inc(z3t_low, 1)

            def x2_shift(g):
                dve.wait_ge(x2_rstd, g + 1)
                dve.scalar_tensor_tensor(out=va[:, 5, :], in0=mv[:, 1, :, 0], scalar=-1.0, in1=va[:, 4, :],
                                         op0=ALU.mult, op1=ALU.mult).then_inc(x2_coef, 1)

            def x3(g, j, par):
                dve.wait_ge(ffn2_psum, 4 * g + j + 1)
                dve.wait_ge(x2b_ready, 4 * g + j + 1)
                dve.scalar_tensor_tensor(out=x2buf[par][:, j, :], in0=bank(6 + j % 2), scalar=scale(C_M),
                                         in1=x2buf[par][:, j, :], op0=ALU.mult, op1=ALU.add)\
                   .then_inc(x3_ready, 1)

            for j in range(GT):
                mixed(0, j, 0, 0)
            mixed_shift(0)
            for j in range(GT):
                residual(0, j, 0)
            for j in range(GT):
                g_low(0, j)

            def step(g, pair, par):
                if not is_first(g):
                    x2_shift(g - 1)
                for hc in range(HC):
                    dve.wait_ge(h_ready, HC * g + hc + 1)
                    dve.tensor_scalar(hid[:, 0, hc, :], h32[:, hc % 4, :], scale(S_H), None, ALU.mult)\
                       .then_inc(h_high, 1)
                    dve.wait_ge(h_high, HC * g + hc + 1)
                    dve.scalar_tensor_tensor(out=hid[:, 1, hc, :], in0=h32[:, hc % 4, :], scalar=scale(S_H),
                                             in1=hid[:, 0, hc, :], op0=ALU.mult, op1=ALU.subtract)\
                       .then_inc(h_low, 1)
                    if hc in (3, 5, 7, 9) and not is_first(g):
                        z3_low(g - 1, (hc - 3) // 2)
                    if not is_last(g):
                        if 1 <= hc < 5:
                            mixed(g + 1, hc - 1, pair + par, 1 - par)
                        if hc == 6:
                            mixed_shift(g + 1)
                        if 6 <= hc < 10:
                            residual(g + 1, hc - 6, 1 - par)
                for j in range(GT):
                    if not is_last(g):
                        g_low(g + 1, j)
                    if not is_first(g):
                        x3(g - 1, j, 1 - par)

                def x2(j):
                    if j == 0 and not (isinstance(g, int) and g < 2):
                        dve.wait_ge(out_stored[par], 16 * pair)
                    dve.wait_ge(fc2_psum, 4 * g + j + 1)
                    dve.wait_ge(r_ready, 4 * g + j + 1)
                    dve.scalar_tensor_tensor(out=x2buf[par][:, j, :], in0=bank(4 + j % 2), scalar=scale(C_2),
                                             in1=rbuf[par][:, j, :], op0=ALU.mult, op1=ALU.add)\
                       .then_inc(x2_ready, 1)
                    dve.wait_ge(x2_ready, 4 * g + j + 1)
                moments(x2buf[par], 1, x2_bn, x2_aggr, x2_var, va[:, 3, :], g, x2)
            each_group(dve, step)
            x2_shift(GROUPS - 1)
            for j in range(GT):
                z3_low(GROUPS - 1, j)
            for j in range(GT):
                x3(GROUPS - 1, j, 1)

        @block.tensor
        def _(pe):
            pe.wait_ge(smalls_loaded, 16 * N_SMALLS)
            pe.wait_ge(prep_a, A["e_taps"])
            pe.wait_ge(pool_set, 12)
            pe.matmul(bank(7), e_taps[0:NST, :], mix_s[0:NST, :], start=True, stop=False)
            pe.matmul(bank(7), onehot, drow, start=False, stop=True).then_inc(prep_pe, 1)
            pe.wait_ge(tables_loaded, 16 * 4)
            for oc in range(KC):
                if oc == 1:
                    pe.wait_ge(prep_v, V["k_low"])
                if oc >= 2:
                    pe.wait_ge(prep_v, V[f"at{oc - 2}"])
                for i, (w, f) in enumerate(((wr_sb, cos_sb), (wi_sb, sin_sb), (wr_sb, sin_sb), (wi_sb, cos_sb))):
                    for k in range(KC):
                        last = pe.matmul(bank(4 * (oc % 2) + i)[:, 0:HALF], w[:, k, oc * P:(oc + 1) * P],
                                         f[:, k, :], start=(k == 0), stop=(k == KC - 1))
                last.then_inc(prep_pe, 1)
            pe.wait_ge(fc1_loaded, 16)
            pe.wait_ge(prep_v, V["at2"])
            for hc in range(HC):
                for k in range(KC):
                    last = pe.matmul(bank(3)[:, hc:hc + 1], wfull1[:, k, hc * P:(hc + 1) * P],
                                     colsb[:, HC + KC + k:HC + KC + k + 1], start=(k == 0), stop=(k == KC - 1))
            last.then_inc(prep_pe, 1)
            pe.wait_ge(prep_v, V["at3"])
            for i in range(KC):
                if i == 3:
                    pe.wait_ge(prep_v, V["m0"])
                for odd, (a, f) in enumerate(((at_re, cos_sb), (at_im, sin_sb))):
                    for k in range(KC):
                        last = pe.matmul(bank(M_BANKS[i] + odd)[:, 0:HALF], a[:, k, i * P:(i + 1) * P],
                                         f[:, k, :], start=(k == 0), stop=(k == KC - 1))
                last.then_inc(prep_pe, 1)

            PASSES = ((0, 0), (0, 1), (1, 0))

            def transposes(dst, src, done):
                for k in range(KC):
                    last = pe.transpose(dst[:, k * P:(k + 1) * P], src[:, k * P:(k + 1) * P], ident[:, :])
                last.then_inc(done, 1)

            def ffn(dst, act_parts, done):
                n = 0
                for k in range(KC):
                    for a, b in PASSES:
                        last = pe.matmul(dst, act_parts[:, a, k, :], m_parts[:, b, k, :], start=(n == 0),
                                         stop=(n == 3 * KC - 1))
                        n += 1
                last.then_inc(done, 1)

            pe.wait_ge(prep_v, V["m3"])

            def slot(g, quad, q, j):
                t = Tile(g, quad, q, j, 1)
                if t.real:
                    pe.wait_ge(z_ready, t.n + 1)
                    at_least(pe, zt_low, t.n - 1)
                    transposes(bank(t.j % 2), ring[:, t.j, :], zt_psum)
                t = Tile(g, quad, q, j, 0)
                if isinstance(t.n, int) and t.n == 0:
                    pe.wait_ge(prep_v, V["fc1bias"])
                if t.real:
                    pe.wait_ge(zt_high, t.n + 1)
                    pe.wait_ge(zt_low, t.n + 1)
                    at_least(pe, x1_ready, t.n - 1)
                    ffn(bank(2 + t.j % 2), zt[:, t.j % 2, :, :, :], ffn_psum)
            each_tile(pe, slot)

            def states(blk, o, i):
                oo = o + blk * (BLK // OC)
                if not (isinstance(oo, int) and oo < 2):
                    pe.wait_ge(state_scanned, oo - 1)
                for n, (a, b) in enumerate(PASSES):
                    off = (blk * 2 + b) * BLK * TILES
                    last = pe.matmul(bank(i), to_state[:, a, :],
                                     u_flat[:, bass.ds(o * (OC * TILES) + off, OC * TILES)],
                                     start=(n == 0), stop=(n == 2))
                last.then_inc(state_psum, 1)

            def inside(blk, o, i, buf):
                oo = o + blk * (BLK // OC)
                if not (isinstance(oo, int) and oo < 2):
                    pe.wait_ge(y_staged, oo - 1)
                for c in range(OC):
                    for n, (a, b) in enumerate(PASSES):
                        off = (blk * 2 + b) * BLK * TILES + c * TILES
                        pe.matmul(bank(4 + i)[:, c * TILES:(c + 1) * TILES], taps[:, buf, :, a, c],
                                  u_flat[:, bass.ds(o * (OC * TILES) + off, TILES)],
                                  start=(c == 0 and n == 0), stop=False, skip_group_check=True)

            def between(oo, i):
                pe.wait_ge(state_high, oo + 1)
                pe.wait_ge(state_low, oo + 1)
                pe.matmul(bank(4 + i), from_state[:, 0, :], state_parts[:, i, :], start=False, stop=False,
                          skip_group_check=True)
                pe.matmul(bank(4 + i), from_state[:, 1, :], state_parts[:, i, :], start=False, stop=True,
                          skip_group_check=True).then_inc(y_psum, 1)

            pe.wait_ge(u_high, TILES)
            pe.wait_ge(u_low, TILES)
            pe.wait_ge(state_zero, 1)
            pe.wait_ge(taps_zeroed, 1)
            states(0, 0, 0)
            states(0, 1, 1)

            def four(blk, q, n_ahead):
                for buf in range(4):
                    pe.wait_ge(taps_loaded[buf], 32 * (q + 4 * blk) + 32)
                    o, half = 4 * q + buf, buf % 2
                    inside(blk, o, half, buf)
                    if buf < n_ahead:
                        states(blk, 4 * q + (buf + 2), half)
                    elif blk < BLOCKS - 1:
                        states(blk + 1, half, half)
                    between(o + blk * (BLK // OC), half)

            for blk in range(BLOCKS):
                if blk == 0:
                    four(0, 0, 4)
                with pe.Fori(1 if blk == 0 else 0, 3) as q:
                    four(blk, q, 4)
                four(blk, 3, 2)

            def turn_z2(g, j):
                pe.wait_ge(z2_ready, 4 * g + j + 1)
                if is_first(g):
                    if j >= 2:
                        pe.wait_ge(gt_low, 4 * g + j - 1)
                elif j < 2:
                    if isinstance(g, int) and g == 1:
                        pe.wait_ge(gt_low, j + 3)
                    else:
                        pe.wait_ge(z3t_low, 4 * (g - 2) + j + 3)
                else:
                    pe.wait_ge(gt_low, 4 * g + j - 1)
                transposes(bank(2 + j % 2), ybuf[:, j, :], gt_psum)

            def turn_z3(g, j):
                pe.wait_ge(z3_ready, 4 * g + j + 1)
                if j < 2 and is_last(g):
                    pe.wait_ge(z3t_low, 4 * (g - 1) + j + 3)
                elif j < 2:
                    pe.wait_ge(gt_low, 4 * g + j + 7)
                else:
                    pe.wait_ge(z3t_low, 4 * g + j - 1)
                transposes(bank(2 + j % 2), z3[:, j, :], z3t_psum)

            def second_ffn(g, j):
                pe.wait_ge(z3t_high, 4 * g + j + 1)
                pe.wait_ge(z3t_low, 4 * g + j + 1)
                if not (is_first(g) and j < 2):
                    pe.wait_ge(x3_ready, 4 * g + j - 1)
                ffn(bank(6 + j % 2), z3t[:, j, :, :, :], ffn2_psum)

            for j in range(GT):
                turn_z2(0, j)
            pe.wait_ge(w1_loaded, 16)

            def step(g, pair, par):
                pe.wait_ge(gt_high, 4 * g + 4)
                pe.wait_ge(gt_low, 4 * g + 4)
                for hc in range(HC):
                    if not (is_first(g) and hc < 2):
                        pe.wait_ge(h_ready, HC * g + hc - 1)
                    n = 0
                    for k in range(KC):
                        for a, b in PASSES:
                            last = pe.matmul(bank(hc % 2), w1_sb[:, a, k, hc * P:(hc + 1) * P], gt[:, b, k, :],
                                             start=(n == 0), stop=(n == 3 * KC - 1))
                            n += 1
                    last.then_inc(fc1_psum, 1)
                    if hc in (3, 5, 7, 9) and not is_first(g):
                        turn_z3(g - 1, (hc - 3) // 2)
                for j in range(GT):
                    if not is_last(g):
                        turn_z2(g + 1, j)
                    if not is_first(g):
                        second_ffn(g - 1, j)
                if is_first(g):
                    pe.wait_ge(w2_loaded, 16)
                for j in range(GT):
                    if not (is_first(g) and j < 2):
                        pe.wait_ge(x2_ready, 4 * g + j - 1)
                    n = 0
                    for hc in range(HC):
                        if j == 0:
                            pe.wait_ge(h_low, HC * g + hc + 1)
                        for a, b in PASSES:
                            last = pe.matmul(bank(4 + j % 2), hid[:, a, hc, j * P:(j + 1) * P],
                                             w2_sb[:, b, hc, :], start=(n == 0), stop=(n == 3 * HC - 1))
                            n += 1
                    last.then_inc(fc2_psum, 1)
            each_group(pe, step)
            for j in range(GT):
                turn_z3(GROUPS - 1, j)
                if j >= 1:
                    second_ffn(GROUPS - 1, j - 1)
            second_ffn(GROUPS - 1, GT - 1)


def kernel(**inputs):
    import concourse.bacc as bacc
    from concourse.bass_utils import run_bass_kernel_spmd

    def get(name):
        return np.asarray(inputs["L0_" + name])

    def by_partition(v, n):
        return np.ascontiguousarray(v.reshape(n, P).T)

    turn = np.outer(np.arange(C), np.arange(C)) % C * (2 * np.pi / C)
    arrays = {
        "x": get("attn_x").reshape(TILES * P, C),
        "wr": get("ffn_w_freq_real"), "wi": get("ffn_w_freq_imag"), "ffn_bias": get("ffn_bias"),
        "fc1t": get("attn_fc1_w").T, "fc2t": get("attn_fc2_w").T,
        "fc1b": by_partition(get("attn_fc1_b"), HC), "fc2b": get("attn_fc2_b"),
        "n1w": get("attn_norm1_w"), "n1b": get("attn_norm1_b"),
        "n2w": by_partition(get("attn_norm2_w"), KC), "n2b": by_partition(get("attn_norm2_b"), KC),
        "dskip": get("attn_D").reshape(1, C), "mixt": get("attn_mix").T,
        "log_tau": get("attn_log_tau").reshape(NST, 1), "log_dt": get("attn_log_dt").reshape(1, 1),
        "cos_t": np.cos(turn[:, :HALF]).astype(np.float32), "sin_t": np.sin(turn[:, :HALF]).astype(np.float32),
    }
    nc = bacc.Bacc("TRN2", target_bir_lowering=False, num_devices=1)
    feed, aps = {}, {}
    for name, a in arrays.items():
        feed["in_" + name] = a = np.ascontiguousarray(a)
        aps[name] = nc.dram_tensor("in_" + name, a.shape, mybir.dt.from_np(a.dtype), kind="ExternalInput").ap()
    out = nc.dram_tensor("out", (TILES * P, C), F32, kind="ExternalOutput").ap()
    build(nc, out=out, **aps)
    r = run_bass_kernel_spmd(nc, [feed], core_ids=[0])
    return r.results[0]["out"].reshape(BATCH, TIME, C)
```

```python
from contextlib import ExitStack

import numpy as np

import concourse.bass as bass
from concourse import mybir

ALU = mybir.AluOpType
ACT = mybir.ActivationFunctionType
F32 = mybir.dt.float32
F16 = mybir.dt.float16
I32 = mybir.dt.int32
BF16 = mybir.dt.bfloat16
AX_X = mybir.AxisListType.X
AX_XY = mybir.AxisListType.XY
RMAX = bass.bass_isa.ReduceOp.max

P = 128
BATCH, TIME, C, HID, NST = 4, 2048, 512, 2048, 64
KC = C // P
HC = HID // P
TILES = BATCH * TIME // P
PER_BATCH = TIME // P
GT = 4
GROUPS = TILES // GT
PAIRS = GROUPS // 2
HALF = C // 2 + 1
OC = 8
OBLOCKS = C // OC
QUADS = GROUPS // 4
LAG = 2
PEAKS, SPLIT = 6, 10
BLK = 128
BLOCKS = C // BLK
TAPROWS = 2 * P - 1
COPIES = 16
EPS = 1e-5
REG = 8192


def broadcast_rows(ap, n, parts=P):
    return bass.AP(tensor=ap.tensor, offset=0, ap=[[0, parts], [1, n]])


def build(nc, x, wr, wi, ffn_bias, fc1t, fc2t, fc1b, fc2b, n1w, n1b, n2w, n2b, dskip, mixt, log_tau, log_dt,
          cos_t, sin_t, out):
    x1_dram = nc.dram_tensor("x1_scratch", (TILES * P, C), F32, kind="Internal").ap()
    y_dram = nc.dram_tensor("y_scratch", (TILES, P, C), F32, kind="Internal").ap()
    taps_one = nc.dram_tensor("taps_scratch", (OBLOCKS, TAPROWS, 2 * OC), F16, kind="Internal").ap()
    taps_dram = nc.dram_tensor("taps_copies", (COPIES, OBLOCKS * TAPROWS * 2 * OC), F16, kind="Internal").ap()
    w1_dram = nc.dram_tensor("w1_scratch", (P, 2 * KC * HID), F16, kind="Internal").ap()
    b1n_dram = nc.dram_tensor("b1n_scratch", (1, HID), F32, kind="Internal").ap()

    with ExitStack() as ctx:
        def sb(name, shape, dt):
            return ctx.enter_context(nc.sbuf_tensor(name, shape, dt))

        def sem(name):
            return ctx.enter_context(nc.semaphore(name))

        arena = sb("arena", [P, 5 * REG], F32)

        def area(start, cols):
            return arena[:, start:start + cols]

        ident = sb("ident", [P, P], F32)
        m_parts = sb("m_parts", [P, 2, KC, C], F16)
        ring = sb("ring", [P, 4, C], F32)
        taps = sb("taps", [P, 4, P, 2, OC], F16)
        half_bias = sb("half_bias", [P, C], F32)
        w1s = sb("w1s", [P, C], F32)
        b1s = sb("b1s", [P, C], F32)
        to_state = sb("to_state", [P, 2, P], F16)
        from_state = sb("from_state", [P, 2, P], F16)
        carry = sb("carry", [P, C], F32)
        mix_s = sb("mix_s", [P, C], F32)
        state_parts = sb("state_parts", [P, 2, C], F16)
        alpha1 = sb("alpha1", [P, TILES], F32)
        beta1 = sb("beta1", [P, TILES], F32)
        mv = sb("mv", [P, 2, GT, 2], F32)
        bn = sb("bn", [P, 2, GT, 6], F32)
        va = sb("va", [P, 10, GT], F32)
        mhalf = sb("mhalf", [P, GT], F32)
        peak = sb("peak", [P, 16], F32)
        peak_all = sb("peak_all", [P, 16], F32)
        peak_k = sb("peak_k", [P, KC], F32)
        n2ws = sb("n2ws", [P, KC], F32)
        sc = sb("sc", [P, 20 + HC], F32)
        bounds = sb("bounds", [P, 8], F32)
        ubias = sb("ubias", [P, GT], F32)
        b1n = sb("b1n", [P, HC], F32)
        b1p = sb("b1p", [P, HC], F32)
        colsb = sb("colsb", [P, HC + 2 * KC], F32)
        psum = ctx.enter_context(nc.psum_tensor("psum", [P, 8, 512], F32))

        xbuf = [area(i * GT * C, GT * C).rearrange("p (j c) -> p j c", j=GT) for i in range(4)]
        taps_flat = taps[:, :, :, :, :].rearrange("p r t s c -> p (r t s c)")
        one_block = P * 2 * OC
        zt = taps_flat[:, one_block:2 * one_block].rearrange("p (r s k t) -> p r s k t", r=2, s=2, k=KC)
        bias_parts = taps_flat[:, 0:C].bitcast(BF16)
        bias_rows = taps_flat[:, C:C + P].bitcast(BF16)
        bias_rest = taps_flat[:, 2 * C:4 * C].bitcast(F32)
        uring = taps_flat[:, 2 * one_block:4 * one_block].bitcast(F32).rearrange("p (r c) -> p r c", r=GT)
        u_all = area(REG, 4 * REG).bitcast(F16).rearrange("p (b s c t) -> p b s c t", b=BLOCKS, s=2, c=BLK)
        u_flat = area(REG, 4 * REG).bitcast(F16)

        taken = [REG]

        def table(*dims):
            cols = int(np.prod(dims))
            at, taken[0] = taken[0], taken[0] + cols
            return area(at, cols).rearrange("p (k n) -> p k n", k=dims[0])

        wr_sb, wi_sb, at_re, at_im, m_full = [table(KC, C) for _ in range(5)]
        cos_sb, sin_sb = table(KC, HALF), table(KC, HALF)
        first_sb = table(4, HALF)
        even_sb = table(2, HALF)
        taps_out = table(1, OBLOCKS * OC)[:, 0, :].bitcast(F16)
        taps_zero = table(1, OBLOCKS * OC)[:, 0, :].bitcast(F16)
        wfull1 = area(3 * REG, REG).rearrange("p (k h) -> p k h", k=KC)
        wsplit = area(4 * REG, REG).bitcast(F16)
        wsplit_k = wsplit.rearrange("p (s k h) -> p s k h", s=2, k=KC)
        b1n_row = area(REG, HID)[0:1, :]
        flat_ring = ring[:, :, :].rearrange("p a b -> p (a b)")
        logs = flat_ring[:, 0:66]
        tmp_a = flat_ring[:, 66:132]
        tmp_b = flat_ring[:, 132:198]
        neg_a = flat_ring[:, 198:264]
        steps = flat_ring[:, 264:392]
        left = flat_ring[:, 392:393]
        onehot = flat_ring[0:1, 400:528]
        e_taps = flat_ring[:, 528:656]
        e_out = flat_ring[:, 656:784]
        e_in = flat_ring[:, 784:848]
        e_tile = flat_ring[:, 848:849]
        drow = flat_ring[0:1, 1024:1536]

        w2_full = area(0, REG).rearrange("p (h n) -> p h n", h=HC)

        w2_peak_cols = sc[:, 20:20 + HC]

        w1_sb = area(0, REG).bitcast(F16).rearrange("p (s k h) -> p s k h", s=2, k=KC)
        w2_sb = area(REG, REG).bitcast(F16).rearrange("p (s h n) -> p s h n", s=2, h=HC)
        hid = area(2 * REG, REG).bitcast(F16).rearrange("p (s h t) -> p s h t", s=2, h=HC)
        def buffer(at):
            return area(at, GT * C).rearrange("p (j c) -> p j c", j=GT)

        at3, at4, size = 3 * REG, 4 * REG, GT * C
        rbuf = [buffer(at4), buffer(at3)]
        x2buf = [buffer(at3 + size), buffer(at3 + 2 * size)]
        ybuf = buffer(at4 + size)
        first_y, first_x1 = buffer(2 * REG), buffer(2 * REG + size)
        gt = area(at4 + 2 * size, size).bitcast(F16).rearrange("p (s k t) -> p s k t", s=2, k=KC)
        h32 = area(at4 + 3 * size, size).rearrange("p (r t) -> p r t", r=4)
        z3t = area(at3 + 3 * size, size).bitcast(F16).rearrange("p (j s k t) -> p j s k t", j=GT, s=2, k=KC)
        fc2_bias = b1s[:, :]
        z3 = ring

        def bank(i):
            return psum[:, i, :]

        def scale(i):
            return sc[:, i:i + 1]

        M_BANKS = (0, 4, 6, 0)
        S_U, S_K, S_W1, S_W2, S_H, S_M = range(6)
        C_Y, C_W1, C_2, C_M, C_MIX = range(8, 13)
        C_B = 13

        smalls_loaded = sem("smalls_loaded")
        table_loaded = [sem(f"{n}_loaded") for n in ("wr", "cos", "wi", "sin")]
        fc1_loaded = sem("fc1_loaded")
        w2_raw = [sem(f"w2_raw{i}") for i in range(8)]
        w2_high, w2_low = sem("w2_high"), sem("w2_low")
        fc1_stored, b1n_stored, b1n_loaded = sem("fc1_stored"), sem("b1n_stored"), sem("b1n_loaded")
        taps_stored, taps_copied = sem("taps_stored"), sem("taps_copied")
        pool_set = sem("pool_set")
        peaks_reduced = sem("peaks_reduced")
        prep_v = sem("prep_v")
        prep_a = sem("prep_a")
        prep_pe = sem("prep_pe")
        m_written, w2_peaks = sem("m_written"), sem("w2_peaks")
        bounds_ready, gate, sp_gate = sem("bounds_ready"), sem("gate"), sem("sp_gate")

        x_loaded = [sem(f"x_loaded{i}") for i in range(4)]
        x1_stored = [sem(f"x1_stored{i}") for i in range(4)]
        x_bn, x_aggr, x_var, x_rstd, x_coef = [sem(n) for n in ("x_bn", "x_aggr", "x_var", "x_rstd", "x_coef")]
        z_ready, zt_psum, zt_high, zt_low = [sem(n) for n in ("z_ready", "zt_psum", "zt_high", "zt_low")]
        ffn_psum, x1_ready = sem("ffn_psum"), sem("x1_ready")
        bias_ones, bias_parted = sem("bias_ones"), sem("bias_parted")
        x1_bn, x1_aggr, x1_var, x1_rstd = [sem(n) for n in ("x1_bn", "x1_aggr", "x1_var", "x1_rstd")]
        v_var0, v_var, v_rstd, u_coef = sem("v_var0"), sem("v_var"), sem("v_rstd"), sem("u_coef")
        u_norm, u_weighted, u_done, u_high, u_low = [sem(n) for n in
                                                     ("u_norm", "u_weighted", "u_done", "u_high", "u_low")]
        last_weighted, drain_weighted, u_drained = [sem(n) for n in ("last_weighted", "drain_weighted", "u_drained")]

        taps_loaded = [sem(f"taps_loaded{i}") for i in range(4)]
        taps_zeroed = sem("taps_zeroed")
        first_mixed = sem("first_mixed")
        first_loaded = [sem(f"first_loaded{j}") for j in range(GT)]
        state_psum, state_scanned, state_mixed = sem("state_psum"), sem("state_scanned"), sem("state_mixed")
        state_high, state_low, state_zero = sem("state_high"), sem("state_low"), sem("state_zero")
        y_psum, y_staged = sem("y_psum"), sem("y_staged")
        y_stored = [[sem(f"y_stored{b}_{i}") for i in range(8 if b < 2 else 1)] for b in range(BLOCKS)]

        w1_loaded, fc2b_loaded = sem("w1_loaded"), sem("fc2b_loaded")
        yg_loaded = sem("yg_loaded")
        r_loaded = [sem("r_loaded0"), sem("r_loaded1")]
        out_stored = [sem("out_stored0"), sem("out_stored1")]
        xm_sum, xm_bn, xm_aggr, xm_var, xm_rstd, xm_coef = [sem(n) for n in
                                                            ("xm_sum", "xm_bn", "xm_aggr", "xm_var", "xm_rstd",
                                                             "xm_coef")]
        r_sum, r_ready, z2_ready = sem("r_sum"), sem("r_ready"), sem("z2_ready")
        gt_psum, gt_high, gt_low = sem("gt_psum"), sem("gt_high"), sem("gt_low")
        fc1_psum, h_ready, h_high, h_low = sem("fc1_psum"), sem("h_ready"), sem("h_high"), sem("h_low")
        fc2_psum, x2_ready = sem("fc2_psum"), sem("x2_ready")
        x2_bn, x2_aggr, x2_var, x2_rstd, x2_coef = [sem(n) for n in
                                                    ("x2_bn", "x2_aggr", "x2_var", "x2_rstd", "x2_coef")]
        z3_ready, z3t_psum, z3t_high, z3t_low = [sem(n) for n in ("z3_ready", "z3t_psum", "z3t_high", "z3t_low")]
        x2b_ready, ffn2_psum, x3_ready = sem("x2b_ready"), sem("ffn2_psum"), sem("x3_ready")

        def each_group(eng, step):
            step(0, 0, 0)
            step(1, 0, 1)
            with eng.Fori(1, PAIRS - 1) as pair:
                step(2 * pair, pair, 0)
                step(2 * pair + 1, pair, 1)
            step(GROUPS - 2, PAIRS - 1, 0)
            step(GROUPS - 1, PAIRS - 1, 1)

        def is_first(g):
            return isinstance(g, int) and g == 0

        def in_drain(n):
            return isinstance(n, int) and n >= DRAIN

        def is_last(g):
            return isinstance(g, int) and g == GROUPS - 1

        def rows(dram, g):
            return dram[bass.ds(g * (GT * P), GT * P), :].rearrange("(j p) c -> p j c", j=GT)

        def each_tile(eng, slot):
            def step(g, quad, q):
                for j in range(GT):
                    slot(g, quad, q, j)
            step(-1, -1, 3)
            for g in range(4):
                step(g, 0, g)
            with eng.Fori(1, QUADS - 1) as quad:
                for i in range(4):
                    step(4 * quad + i, quad, i)
            for g in range(GROUPS - 4, GROUPS + LAG):
                step(g, g // 4, g % 4)

        X_RSTD, X_SHIFT = (1, 8), (2, 9)

        DRAIN = TILES - 7

        class Tile:

            def __init__(self, g, quad, q, j, d):
                over, self.j = divmod(j + d, GT)
                self.g = g + over
                turns, self.q = divmod(q + over, 4)
                self.quad = quad + turns
                self.n = 4 * self.g + self.j
                self.real = not isinstance(g, int) or 0 <= self.g < GROUPS

        def at_least(eng, semaphore, value):
            if not (isinstance(value, int) and value <= 0):
                eng.wait_ge(semaphore, value)

        N_SMALLS = 13
        BIAS_STEPS = 8
        V_STEPS = ("nx sp dt q_high q_low p_high p_low carry peaks0 bound0 e0 r0 scales0 vecs k_high k_low mixw "
                   "at0 at1 pk0 pk1 at2 pk2 pk3 pkw peaks1 at3 e1 r1 scales1 low0 m0 low1 m1 m2 low2 m3 bound2 e2 r2 "
                   "scales2 mhigh mlow low3 peaks3 bound3 e3 r3 scales3").split()
        V = {name: i + 1 for i, name in enumerate(V_STEPS)}
        A_STEPS = ("exp ln e_taps e_out e_in e_tile at0 at1 at2 at3 high0 high1 m0 high2 m1 high3 m2 m3 "
                   "bias").split()
        A = {name: i + 1 for i, name in enumerate(A_STEPS)}
        E_STEPS = "at0 taps at1 at2 at3 m0 m1 m2 m3 bias0 bias1 bias2 bias3".split()
        E = {name: i + 1 for i, name in enumerate(E_STEPS)}

        block = ctx.enter_context(nc.Block())

        @block.sync
        def _(sp):
            for i, (dst, src) in enumerate(((wr_sb, wr), (cos_sb, cos_t), (wi_sb, wi), (sin_sb, sin_t))):
                sp.dma_start(dst, src.rearrange("(k p) n -> p k n", p=P)).then_inc(table_loaded[i], 16)
            for half in range(2):
                sp.dma_start(mix_s[half * NST:(half + 1) * NST, :], mixt).then_inc(smalls_loaded, 16)
                sp.dma_start(logs[half * NST:(half + 1) * NST, 64:65], log_tau).then_inc(smalls_loaded, 16)
            sp.dma_start(logs[:, 0:64], broadcast_rows(log_tau, NST)).then_inc(smalls_loaded, 16)
            sp.dma_start(logs[:, 65:66], broadcast_rows(log_dt, 1)).then_inc(smalls_loaded, 16)
            sp.dma_start(drow, dskip).then_inc(smalls_loaded, 16)
            sp.dma_start(colsb[:, 0:HC], fc1b).then_inc(smalls_loaded, 16)
            sp.dma_start(colsb[:, HC:HC + KC], n2w).then_inc(smalls_loaded, 16)
            sp.dma_start(colsb[:, HC + KC:HC + 2 * KC], n2b).then_inc(smalls_loaded, 16)
            sp.dma_start(half_bias[:, :], broadcast_rows(ffn_bias, C)).then_inc(smalls_loaded, 16)
            sp.dma_start(w1s[:, :], broadcast_rows(n1w, C)).then_inc(smalls_loaded, 16)
            sp.dma_start(b1s[:, :], broadcast_rows(n1b, C)).then_inc(smalls_loaded, 16)
            sp.dma_start(wfull1, fc1t.rearrange("(k p) h -> p k h", p=P)).then_inc(fc1_loaded, 16)
            for i in range(4):
                sp.dma_start(xbuf[i], rows(x, i)).then_inc(x_loaded[i], 16)
            sp.wait_ge(pool_set, 2)
            sp.dma_start(taps_one[:, 0:P - 1, :].rearrange("b j n -> j b n"),
                         taps_zero[0:P - 1, :].rearrange("p (b n) -> p b n", b=OBLOCKS)).then_inc(taps_stored, 16)
            sp.wait_ge(prep_v, V["k_low"])
            sp.dma_start(taps_one[:, P - 1:TAPROWS, :].rearrange("b j n -> j b n"),
                         taps_out.rearrange("p (b n) -> p b n", b=OBLOCKS)).then_inc(taps_stored, 16)
            sp.wait_ge(prep_v, V["low3"])
            sp.dma_start(w1_dram, wsplit).then_inc(fc1_stored, 16)
            sp.wait_ge(prep_a, A["bias"])
            sp.dma_start(b1n_dram, b1n_row).then_inc(b1n_stored, 16)
            sp.wait_ge(b1n_stored, 16)
            sp.dma_start(b1n[:, :], b1n_dram.rearrange("o (h p) -> p (o h)", p=P),
                         allow_slow_non_contiguous=True).then_inc(b1n_loaded, 16)

            def copy_taps(i):
                some, size = COPIES // 4, OBLOCKS * TAPROWS * 2 * OC
                sp.dma_start(taps_dram[i * some:(i + 1) * some, :],
                             bass.AP(tensor=taps_one.tensor, offset=0, ap=[[0, some], [1, size]]))\
                  .then_inc(taps_copied, 16)

            def store(g, quad, q):
                sp.wait_ge(x1_ready, 4 * g + 4)
                sp.dma_start(rows(x1_dram, g), xbuf[q]).then_inc(x1_stored[q], 16)

            def load(g, quad, q):
                sp.wait_ge(u_norm, 4 * g)
                sp.sem_inc(sp_gate, 1)
                sp.wait_ge(x1_stored[(q - 1) % 4], 16 * ((quad if q else quad - 1) + 1))
                sp.dma_start(xbuf[(q - 1) % 4], rows(x, g + 3)).then_inc(x_loaded[(q - 1) % 4], 16)

            sp.wait_ge(taps_stored, 32)
            store(0, 0, 0)
            copy_taps(0)
            for g in range(1, 4):
                store(g, 0, g)
                load(g, 0, g)
                copy_taps(g)
            with sp.Fori(1, QUADS - 1) as quad:
                for q in range(4):
                    store(4 * quad + q, quad, q)
                    load(4 * quad + q, quad, q)
            store(GROUPS - 4, QUADS - 1, 0)
            load(GROUPS - 4, QUADS - 1, 0)
            for q in range(1, 4):
                store(GROUPS - 4 + q, QUADS - 1, q)

            def load_taps(o):
                copy, row, per = OBLOCKS * TAPROWS * 2 * OC, 2 * OC, P // 2 // COPIES
                for part, cols in ((0, P), (1, P // 2)):
                    dst = taps[part * (P // 2):(part + 1) * (P // 2), o % 4, P - cols:P, :, :]\
                        .rearrange("p t s c -> p (t s c)")
                    src = bass.AP(tensor=taps_dram.tensor, offset=(o * TAPROWS + P - 1) * row,
                                  ap=[[copy - per * row, COPIES], [-row, per], [1, cols * row]])
                    sp.dma_start(dst, src).then_inc(taps_loaded[o % 4], 16)

            sp.wait_ge(taps_copied, 16 * 4)
            sp.wait_ge(ffn_psum, TILES)
            load_taps(0)
            load_taps(1)
            sp.wait_ge(u_high, TILES)
            sp.wait_ge(u_low, TILES)
            load_taps(2)
            load_taps(3)
            sp.dma_start(fc2_bias, broadcast_rows(fc2b, C)).then_inc(fc2b_loaded, 16)

            def store_y(blk, i):
                at = slice(i * (TILES // 8), (i + 1) * (TILES // 8))
                stage = area(blk * REG, REG).rearrange("p (t c) -> p t c", t=TILES)
                sp.dma_start(y_dram[at, :, blk * BLK:(blk + 1) * BLK].rearrange("t p c -> p t c"),
                             stage[:, at, :]).then_inc(y_stored[blk][i if blk < 2 else 0], 16)

            def load_w2(i):
                sp.wait_ge(y_stored[0][i], 16)
                sp.dma_start(w2_full[:, 2 * i:2 * i + 2, :],
                             fc2t[2 * i * P:(2 * i + 2) * P, :].rearrange("(h p) n -> p h n", p=P))\
                  .then_inc(w2_raw[i], 16)

            def load_w1(i):
                at = slice(i * (REG // 4), (i + 1) * (REG // 4))
                sp.wait_ge(w2_low, 2 * i + 2)
                sp.dma_start(area(0, REG).bitcast(F16)[:, at], w1_dram[:, at]).then_inc(w1_loaded, 16)

            per = BLK // OC
            for o in range(4, OBLOCKS):
                sp.wait_ge(y_psum, o - 3)
                load_taps(o)
                blk, i = divmod(o - 5, per)
                if blk > 0 and i < 8:
                    if i == 0:
                        sp.wait_ge(y_staged, blk * per)
                    store_y(blk - 1, i)
                if 0 <= o - (per + 8) < 16 and o % 2 == 0:
                    load_w2((o - (per + 8)) // 2)
                if o > 3 * per and o % 2 == 0:
                    load_w1((o - 3 * per) // 2 - 1)

            for i in range(4):
                sp.wait_ge(x1_stored[i], 16 * QUADS)
            for i in range(8):
                sp.wait_ge(y_stored[1][i], 16)
            sp.wait_ge(y_stored[2][0], 16 * 8)
            for j in range(GT):
                sp.dma_start(first_x1[:, j, :], x1_dram[j * P:(j + 1) * P, :]).then_inc(first_loaded[j], 16)
                sp.dma_start(first_y[:, j, 0:C - BLK], y_dram[j, :, 0:C - BLK]).then_inc(first_loaded[j], 16)
            load_w1(7)
            sp.wait_ge(y_staged, OBLOCKS)
            for i in range(8):
                store_y(BLOCKS - 1, i)

            def load_y(g):
                sp.dma_start(ybuf, y_dram[bass.ds(g * GT, GT), :, :].rearrange("j p c -> p j c"))\
                  .then_inc(yg_loaded, 16)

            def load_r(g, par):
                sp.dma_start(rbuf[par], rows(x1_dram, g)).then_inc(r_loaded[par], 16)

            sp.wait_ge(y_stored[BLOCKS - 1][0], 16 * 8)

            def step(g, pair, par):
                if not is_last(g):
                    sp.wait_ge(gt_psum, 4 * g + 4)
                    load_y(g + 1)
                    if not is_first(g):
                        sp.wait_ge(x2_ready, 4 * g)
                    load_r(g + 1, 1 - par)
                if not is_first(g):
                    sp.wait_ge(x3_ready, 4 * g)
                    sp.dma_start(rows(out, g - 1), x2buf[1 - par]).then_inc(out_stored[1 - par], 16)
            each_group(sp, step)
            for j in range(GT):
                sp.wait_ge(x3_ready, TILES - GT + j + 1)
                at = (TILES - GT + j) * P
                sp.dma_start(out[at:at + P, :], x2buf[1][:, j, :]).then_inc(out_stored[1], 16)
            sp.wait_ge(out_stored[0], 16 * PAIRS)
            sp.wait_ge(out_stored[1], 16 * (PAIRS + GT - 1))

        @block.gpsimd
        def _(pool):
            pool.memset(peak[:, :], 0.0).then_inc(pool_set, 1)
            pool.memset(taps_zero, 0.0).then_inc(pool_set, 1)
            pool.memset(mhalf[:, :], -0.5).then_inc(pool_set, 1)
            pool.memset(onehot, 0.0).then_inc(pool_set, 1)
            pool.memset(ident[:, :], 0.0).then_inc(pool_set, 1)
            pool.memset(carry[:, :], 1.0).then_inc(pool_set, 1)
            pool.memset(from_state[:, :, :], 0.0).then_inc(pool_set, 1)
            pool.iota(steps, [[1, P]], base=0, channel_multiplier=0, allow_small_or_imprecise_dtypes=True)\
                .then_inc(pool_set, 1)
            pool.iota(left, [[0, 1]], base=P - 1, channel_multiplier=-1, allow_small_or_imprecise_dtypes=True)\
                .then_inc(pool_set, 1)
            pool.wait_ge(pool_set, 7)
            pool.memset(flat_ring[0:1, 400:401], 1.0).then_inc(pool_set, 1)
            pool.affine_select(out=ident[:, :], in_=ident[:, :], compare_op=ALU.not_equal, fill=1.0, base=0,
                               pattern=[[-1, P]], channel_multiplier=1).then_inc(pool_set, 1)
            pool.memset(carry[:, 0:C:PER_BATCH], 0.0).then_inc(pool_set, 1)

            def reduce_peaks(i):
                pool.wait_ge(prep_v, V[f"peaks{i}" if i != 2 else "m3"])
                a, b = ((0, 4), (4, 5), (5, 9), (9, 11))[i]
                pool.partition_all_reduce(peak_all[:, a:b], peak[:, a:b], P, RMAX).then_inc(peaks_reduced, 1)

            def power(dst, src, done):
                pool.tensor_tensor(dst, src, mhalf[:, :], ALU.pow).then_inc(done, 1)

            def x_power(g, q):
                pool.wait_ge(x_var, g + 1)
                at_least(pool, z_ready, 4 * (g - 1))
                power(va[:, X_RSTD[q % 2], :], va[:, 0, :], x_rstd)

            reduce_peaks(0)
            reduce_peaks(1)
            x_power(0, 0)
            reduce_peaks(2)
            pool.memset(bias_rows, 0.0).then_inc(bias_ones, 1)
            pool.wait_ge(bias_ones, 1)
            for i in range(3):
                pool.memset(bias_rows[32 * i:32 * i + 1, :], 1.0).then_inc(bias_ones, 1)
            pool.wait_ge(bias_ones, 4)
            def slot(g, quad, q, j):
                def weigh():
                    t = Tile(g, quad, q, j, -7)
                    if is_last(t.g):
                        pool.wait_ge(u_norm, t.n + 1)
                        pool.tensor_tensor(uring[:, t.j, :], uring[:, t.j, :], w1s[:, :], ALU.mult)\
                            .then_inc(last_weighted, 1)
                    elif t.real and not in_drain(t.n):
                        pool.wait_ge(u_norm, t.n + 1)
                        pool.tensor_tensor(uring[:, t.j, :], uring[:, t.j, :], w1s[:, :], ALU.mult)\
                            .then_inc(u_weighted, 1)
                        pool.wait_ge(u_weighted, t.n + 1)
                        pool.tensor_tensor(uring[:, t.j, :], uring[:, t.j, :], b1s[:, :], ALU.add).then_inc(u_done, 1)

                draining = isinstance(g, int) and g >= GROUPS
                if not draining:
                    weigh()
                before, after = Tile(g, quad, q, j, -GT), Tile(g, quad, q, j, GT)
                if j == 0 and before.real:
                    pool.wait_ge(x1_var, before.g + 1)
                    power(va[:, 4, :], va[:, 3, :], x1_rstd)
                if j == 0 and after.real and not is_first(after.g):
                    x_power(after.g, after.q)
                if j == 1 and before.real:
                    pool.wait_ge(v_var, before.g + 1)
                    power(va[:, 6, :], va[:, 5, :], v_rstd)
                if draining:
                    weigh()
            pool.wait_ge(prep_v, V["vecs"])
            each_tile(pool, slot)

            pool.wait_ge(ffn_psum, TILES)
            pool.wait_ge(last_weighted, GT)
            for half in range(2):
                if half == 1:
                    pool.wait_ge(u_high, TILES)
                    pool.wait_ge(u_low, TILES)
                pool.memset(taps[P // 2:P, 2 * half:2 * half + 2, 0:P // 2, :, :]
                            .rearrange("p r t s c -> p r (t s c)"), 0.0).then_inc(taps_zeroed, 1)
                pool.wait_ge(taps_zeroed, half + 1)

            def mix(o, i):
                pool.wait_ge(state_scanned, o + 1)
                pool.tensor_tensor(ring[:, i, :].rearrange("p (c t) -> p c t", c=OC),
                                   ring[:, i, :].rearrange("p (c t) -> p c t", c=OC),
                                   mix_s[:, bass.ds(o * OC, OC)].unsqueeze(2).to_broadcast([P, OC, TILES]),
                                   ALU.mult).then_inc(state_mixed, 1)

            with pool.Fori(0, SPLIT) as q:
                for i in range(4):
                    mix(4 * q + i, i)
            for i in range(4):
                mix(4 * SPLIT + i, i)
                if i == 0:
                    reduce_peaks(3)
            with pool.Fori(SPLIT + 1, OBLOCKS // 4) as q:
                for i in range(4):
                    mix(4 * q + i, i)

            def residual(g, par):
                pool.wait_ge(xm_var, g + 1)
                power(va[:, 1, :], va[:, 0, :], xm_rstd)
                for j in range(GT):
                    pool.wait_ge(r_sum, 4 * g + j + 1)
                    pool.tensor_tensor(rbuf[par][:, j, :], rbuf[par][:, j, :], fc2_bias, ALU.add)\
                        .then_inc(r_ready, 1)

            pool.wait_ge(fc2b_loaded, 16)
            residual(0, 0)

            def step(g, pair, par):
                if not is_first(g):
                    for j in range(GT):
                        pool.wait_ge(z3_ready, 4 * (g - 1) + j + 1)
                        pool.tensor_tensor(x2buf[1 - par][:, j, :], x2buf[1 - par][:, j, :], half_bias[:, :],
                                           ALU.add).then_inc(x2b_ready, 1)
                if not is_last(g):
                    pool.wait_ge(z2_ready, 4 * g + 4)
                    residual(g + 1, 1 - par)
                pool.wait_ge(x2_var, g + 1)
                power(va[:, 4, :], va[:, 3, :], x2_rstd)
            each_group(pool, step)
            for j in range(GT):
                pool.wait_ge(z3_ready, 4 * (GROUPS - 1) + j + 1)
                pool.tensor_tensor(x2buf[1][:, j, :], x2buf[1][:, j, :], half_bias[:, :], ALU.add)\
                    .then_inc(x2b_ready, 1)

        @block.scalar
        def _(act):
            act.wait_ge(prep_v, V["nx"])
            act.activation(tmp_b, tmp_a, ACT.Exp).then_inc(prep_a, 1)
            act.wait_ge(prep_a, A["exp"])
            act.activation(tmp_b, tmp_b, ACT.Ln, bias=1.0).then_inc(prep_a, 1)
            act.wait_ge(prep_v, V["dt"])
            act.wait_ge(pool_set, 9)
            act.activation(e_taps, steps, ACT.Exp, scale=neg_a[:, 64:65]).then_inc(prep_a, 1)
            act.activation(e_out, steps, ACT.Exp, scale=neg_a[:, 64:65], bias=neg_a[:, 64:65]).then_inc(prep_a, 1)
            act.activation(e_in, neg_a[:, 0:64], ACT.Exp, scale=left).then_inc(prep_a, 1)
            act.activation(e_tile, neg_a[:, 64:65], ACT.Exp, scale=float(P)).then_inc(prep_a, 1)
            for oc in range(KC):
                act.wait_ge(prep_pe, E[f"at{oc}"])
                if oc >= 2:
                    act.wait_ge(prep_v, V[f"at{oc - 2}"])
                b = 4 * (oc % 2)
                act.activation(first_sb[:, 2 * (oc % 2), :], bank(b)[:, 0:HALF], ACT.Copy)
                act.activation(first_sb[:, 2 * (oc % 2) + 1, :], bank(b + 2)[:, 0:HALF], ACT.Copy)\
                   .then_inc(prep_a, 1)

            def m_even(i):
                act.wait_ge(prep_pe, E[f"m{i}"])
                if i >= 2:
                    act.wait_ge(prep_v, V[f"m{i - 2}"])
                act.activation(even_sb[:, i % 2, :], bank(M_BANKS[i])[:, 0:HALF], ACT.Copy).then_inc(prep_a, 1)

            def w1_high(k):
                act.activation(wsplit_k[:, 0, k, :], wfull1[:, k, :], ACT.Copy, scale=n2ws[:, k:k + 1])\
                   .then_inc(prep_a, 1)

            act.wait_ge(prep_v, V["scales1"])
            w1_high(0)
            w1_high(1)
            m_even(0)
            w1_high(2)
            m_even(1)
            w1_high(3)
            m_even(2)
            m_even(3)

            def slot(g, quad, q, j):
                t = Tile(g, quad, q, j, 1)
                if t.real:
                    act.wait_ge(zt_psum, t.n + 1)
                    at_least(act, ffn_psum, t.n - 1)
                    act.activation(zt[:, t.j % 2, 0, :, :].rearrange("p k t -> p (k t)"), bank(t.j % 2), ACT.Copy)\
                       .then_inc(zt_high, 1)
                t = Tile(g, quad, q, j, 2)
                if t.real:
                    act.wait_ge(x_coef, t.g + 1)
                    at_least(act, zt_psum, t.n - 3)
                    act.activation(ring[:, t.j, :], xbuf[t.q][:, t.j, :], ACT.Identity,
                                   scale=va[:, X_RSTD[t.q % 2], t.j:t.j + 1],
                                   bias=va[:, X_SHIFT[t.q % 2], t.j:t.j + 1]).then_inc(z_ready, 1)
                t = Tile(g, quad, q, j, -8)
                if t.real:
                    if isinstance(t.n, int) and t.n == 0:
                        act.wait_ge(fc1_stored, 16)
                        act.wait_ge(b1n_stored, 16)
                    if in_drain(t.n):
                        act.wait_ge(u_drained, t.n - DRAIN + 1)
                    else:
                        act.wait_ge(u_done, t.n + 1)
                    act.activation(u_all[:, :, 0, :, bass.ds(t.n, 1)],
                                   uring[:, t.j, :].rearrange("p (b c o) -> p b c o", b=BLOCKS, o=1), ACT.Copy)\
                       .then_inc(u_high, 1)
                t = Tile(g, quad, q, j, -6)
                if t.real:
                    act.wait_ge(u_coef, t.g + 1)
                    at_least(act, u_low, t.n - 3)
                    act.activation(uring[:, t.j, :], xbuf[t.q][:, t.j, :], ACT.Identity,
                                   scale=va[:, 7, t.j:t.j + 1], bias=ubias[:, t.j:t.j + 1]).then_inc(u_norm, 1)
                if isinstance(g, int) and (g, j) == (1, 0):
                    act.wait_ge(prep_pe, E["bias3"])
                    act.activation(b1n_row.rearrange("o (b n) -> o b n", b=4), psum[0:1, 4:8, :], ACT.Copy)\
                       .then_inc(prep_a, 1)
            each_tile(act, slot)

            def state_part(o, i):
                act.wait_ge(state_mixed, o + 1)
                at_least(act, y_psum, o - 1)
                src = ring[:, i, :].rearrange("p (c t) -> p c t", t=PER_BATCH)[:, :, 0:PER_BATCH - 1]
                dst = state_parts[:, i % 2, :].rearrange("p (c t) -> p c t", t=PER_BATCH)[:, :, 1:PER_BATCH]
                act.activation(dst, src, ACT.Copy).then_inc(state_high, 1)

            def stage_y(blk, o, i):
                act.wait_ge(y_psum, o + 1)
                stage = area(blk * REG, REG).rearrange("p (t c) -> p c t", c=BLK)
                act.activation(stage[:, bass.ds((o - blk * (BLK // OC)) * OC, OC), :],
                               bank(4 + i).rearrange("p (c t) -> p c t", c=OC), ACT.Copy, scale=scale(C_Y))\
                   .then_inc(y_staged, 1)

            def w2_high_part(h):
                act.activation(w2_sb[:, 0, bass.ds(h, 1), :], w2_full[:, bass.ds(h, 1), :], ACT.Copy,
                               scale=scale(S_W2)).then_inc(w2_high, 1)

            def quad_of_eights(blk, q, split, last=False):
                for i in range(4):
                    if not (last and i == 3):
                        state_part(4 * q + i + 1, (i + 1) % 4)
                    stage_y(blk, 4 * q + i, i)
                    if split and q == SPLIT and i == 0:
                        act.wait_ge(prep_v, V["scales3"])
                    if split and i == 0:
                        act.wait_ge(y_stored[1][q - SPLIT], 16)
                    if split:
                        w2_high_part(4 * (q - SPLIT) + i)

            for i in range(4):
                act.wait_ge(x1_stored[i], 16 * QUADS)
            state_part(0, 0)
            quad_of_eights(0, 0, False)
            for blk, a, b in ((0, 1, 4), (1, 4, 8), (2, 8, SPLIT)):
                with act.Fori(a, b) as q:
                    quad_of_eights(blk, q, False)
            for q in range(SPLIT, SPLIT + 4):
                quad_of_eights(q // 4, q, True)
            with act.Fori(SPLIT + 4, OBLOCKS // 4 - 1) as q:
                quad_of_eights(3, q, False)
            quad_of_eights(3, OBLOCKS // 4 - 1, False, last=True)

            def z2(g, j):
                act.wait_ge(xm_coef, g + 1)
                act.wait_ge(r_sum, 4 * g + j + 1)
                y = first_y if is_first(g) else ybuf
                act.activation(y[:, j, :], y[:, j, :], ACT.Identity,
                               scale=va[:, 1, j:j + 1], bias=va[:, 2, j:j + 1]).then_inc(z2_ready, 1)

            def g_high(g, j):
                act.wait_ge(gt_psum, 4 * g + j + 1)
                act.activation(gt[:, 0, :, j * P:(j + 1) * P], bank(2 + j % 2).rearrange("p (k t) -> p k t", k=KC),
                               ACT.Copy).then_inc(gt_high, 1)

            def z3_norm(g, par, j):
                if j == 0:
                    act.wait_ge(x2_coef, g + 1)
                act.activation(z3[:, j, :], x2buf[par][:, j, :], ACT.Identity,
                               scale=va[:, 4, j:j + 1], bias=va[:, 5, j:j + 1]).then_inc(z3_ready, 1)

            def z3_high(g, j):
                act.wait_ge(z3t_psum, 4 * g + j + 1)
                act.activation(z3t[:, j, 0, :, :].rearrange("p k t -> p (k t)"), bank(2 + j % 2), ACT.Copy)\
                   .then_inc(z3t_high, 1)

            for j in range(GT):
                z2(0, j)
            for j in range(GT):
                g_high(0, j)

            def step(g, pair, par):
                for hc in range(HC):
                    act.wait_ge(fc1_psum, HC * g + hc + 1)
                    if not (is_first(g) and hc < 4):
                        act.wait_ge(h_low, HC * g + hc - 3)
                    act.activation(h32[:, hc % 4, :],
                                   bank(hc % 2), ACT.Gelu, scale=scale(C_W1), bias=b1p[:, hc:hc + 1])\
                       .then_inc(h_ready, 1)
                    if hc < GT and not is_first(g):
                        z3_norm(g - 1, 1 - par, hc)
                    if hc in (3, 5, 7, 9) and not is_first(g):
                        z3_high(g - 1, (hc - 3) // 2)
                    if 10 <= hc < 14 and not is_last(g):
                        z2(g + 1, hc - 10)
                if not is_last(g):
                    for j in range(GT):
                        g_high(g + 1, j)
            each_group(act, step)
            for j in range(GT):
                z3_norm(GROUPS - 1, 1, j)
            for j in range(GT):
                z3_high(GROUPS - 1, j)

        @block.vector
        def _(dve):
            count = [0]

            def done(ins, name):
                count[0] += 1
                assert V[name] == count[0], name
                ins.then_inc(prep_v, 1)
                return ins

            def own(name):
                dve.wait_ge(prep_v, V[name])

            dve.wait_ge(smalls_loaded, 16 * N_SMALLS)
            done(dve.scalar_tensor_tensor(out=tmp_a, in0=logs, scalar=-1.0, in1=logs, op0=ALU.mult, op1=ALU.min),
                 "nx")
            dve.wait_ge(prep_a, A["ln"])
            done(dve.scalar_tensor_tensor(out=tmp_a, in0=logs, scalar=0.0, in1=tmp_b, op0=ALU.max, op1=ALU.add),
                 "sp")
            own("sp")
            done(dve.tensor_scalar(neg_a[:, 0:65], tmp_a[:, 0:65], tmp_a[:, 65:66], -1.0, ALU.mult, ALU.mult), "dt")
            dve.wait_ge(prep_a, A["e_tile"])
            dve.wait_ge(pool_set, 12)
            big = 32768.0
            done(dve.tensor_scalar(from_state[:, 0, :], e_out, big, None, ALU.mult), "q_high")
            own("q_high")
            done(dve.scalar_tensor_tensor(out=from_state[0:NST, 1, :], in0=e_out[0:NST, :], scalar=big,
                                          in1=from_state[0:NST, 0, :], op0=ALU.mult, op1=ALU.subtract), "q_low")
            for half in range(2):
                ins = dve.tensor_scalar(to_state[:, 0, half * NST:(half + 1) * NST], e_in, big, None, ALU.mult)
            done(ins, "p_high")
            own("p_high")
            for half in range(2):
                ins = dve.scalar_tensor_tensor(out=to_state[:, 1, half * NST:(half + 1) * NST], in0=e_in,
                                               scalar=big, in1=to_state[:, 0, half * NST:(half + 1) * NST],
                                               op0=ALU.mult, op1=ALU.subtract)
            done(ins, "p_low")
            done(dve.tensor_scalar(carry[:, :], carry[:, :], e_tile, None, ALU.mult), "carry")

            def peak_of(col, ap, parts=P, axis=AX_X):
                return dve.tensor_reduce(peak[0:parts, col:col + 1], ap, axis, ALU.max, apply_absolute_value=True)

            peak_of(0, mix_s[:, :])
            peak_of(1, drow, 1)
            peak_of(2, w1s[:, :])
            ins = peak_of(3, b1s[:, :])
            done(ins, "peaks0")
            dve.wait_ge(peaks_reduced, 1)
            dve.scalar_tensor_tensor(out=bounds[:, 0:1], in0=peak_all[:, 2:3], scalar=23.0, in1=peak_all[:, 3:4],
                                     op0=ALU.mult, op1=ALU.add)
            done(dve.scalar_tensor_tensor(out=bounds[:, 1:2], in0=peak_all[:, 0:1], scalar=1024.0,
                                          in1=peak_all[:, 1:2], op0=ALU.mult, op1=ALU.add), "bound0")

            def exponents(n, src, name):
                dve.tensor_scalar(bounds[:, 0:n], src, 2.0 ** -100, None, ALU.max).then_inc(bounds_ready, 1)
                dve.wait_ge(bounds_ready, name + 1)
                done(dve.tensor_scalar(bounds[:, 0:n].bitcast(I32), bounds[:, 0:n].bitcast(I32), 0x7F800000, None,
                                       ALU.bitwise_and), f"e{name}")
                own(f"e{name}")
                done(dve.reciprocal(bounds[:, 4:4 + n], bounds[:, 0:n]), f"r{name}")
                own(f"r{name}")

            own("bound0")
            exponents(2, bounds[:, 0:2], 0)
            dve.tensor_scalar(scale(S_U), bounds[:, 4:5], 2.0 ** 14, None, ALU.mult)
            dve.tensor_scalar(scale(S_K), bounds[:, 5:6], 2.0 ** 14, None, ALU.mult)
            dve.tensor_scalar(scale(C_MIX), bounds[:, 5:6], 2.0 ** -16, None, ALU.mult)
            done(dve.tensor_scalar(scale(C_Y), bounds[:, 0:1], bounds[:, 1:2], 2.0 ** -28, ALU.mult, ALU.mult),
                 "scales0")
            own("scales0")
            dve.tensor_scalar(half_bias[:, :], half_bias[:, :], 0.5, None, ALU.mult)
            dve.tensor_scalar(w1s[:, :], w1s[:, :], scale(S_U), None, ALU.mult)
            done(dve.tensor_scalar(b1s[:, :], b1s[:, :], scale(S_U), None, ALU.mult), "vecs")
            dve.wait_ge(prep_pe, E["taps"])
            k_psum = bank(7).rearrange("p (b c) -> p b c", c=OC)
            k_out = taps_out.rearrange("p (b s c) -> p b s c", s=2, c=OC)
            done(dve.tensor_scalar(k_out[:, :, 0, :], k_psum, scale(S_K), None, ALU.mult), "k_high")
            own("k_high")
            done(dve.scalar_tensor_tensor(out=k_out[:, :, 1, :], in0=k_psum, scalar=scale(S_K),
                                          in1=k_out[:, :, 0, :], op0=ALU.mult, op1=ALU.subtract), "k_low")
            done(dve.tensor_scalar(mix_s[:, :], mix_s[:, :], scale(C_MIX), None, ALU.mult), "mixw")

            def aggregate(chain, bn_done, aggr_done, g):
                dve.wait_ge(bn_done, g + 1)
                dve.sem_inc(gate, 1)
                for j in range(GT):
                    ins = dve.bn_aggr(mv[:, chain, j, :], bn[:, chain, j, :])
                ins.then_inc(aggr_done, 1)

            def variance(chain, aggr_done, var_done, var_out, g):
                dve.wait_ge(aggr_done, g + 1)
                dve.tensor_scalar(var_out, mv[:, chain, :, 1], EPS, None, ALU.add).then_inc(var_done, 1)

            def x_stats(t, some):
                if 0 in some:
                    dve.wait_ge(x_loaded[t.q], 16 * t.quad + 16)
                for j in some:
                    ins = dve.bn_stats(bn[:, 0, j, :], xbuf[t.q][:, j, :])
                if GT - 1 in some:
                    ins.then_inc(x_bn, 1)

            def x_variance(g):
                at_least(dve, x_rstd, g)
                variance(0, x_aggr, x_var, va[:, 0, :], g)

            def x_shift(g, q):
                dve.wait_ge(x_rstd, g + 1)
                dve.scalar_tensor_tensor(out=va[:, X_SHIFT[q % 2], :], in0=mv[:, 0, :, 0], scalar=-1.0,
                                         in1=va[:, X_RSTD[q % 2], :], op0=ALU.mult, op1=ALU.mult).then_inc(x_coef, 1)

            def a_transposed(oc):
                dve.wait_ge(prep_a, A[f"at{oc}"])
                b = 4 * (oc % 2)
                for dst, first, psum_term, sign in ((at_re, first_sb[:, 2 * (oc % 2), :], bank(b + 1), 1),
                                                    (at_im, first_sb[:, 2 * (oc % 2) + 1, :], bank(b + 3), -1)):
                    rest = dst[:, oc, C - 1:HALF - 1:-1]
                    if sign > 0:
                        dve.tensor_tensor(dst[:, oc, 0:HALF], first, psum_term[:, 0:HALF], ALU.add)
                        dve.tensor_tensor(rest, first[:, 1:HALF - 1], psum_term[:, 1:HALF - 1], ALU.subtract)
                    else:
                        dve.tensor_tensor(dst[:, oc, 0:HALF], first, psum_term[:, 0:HALF], ALU.subtract)
                        ins = dve.scalar_tensor_tensor(out=rest, in0=psum_term[:, 1:HALF - 1], scalar=-1.0,
                                                       in1=first[:, 1:HALF - 1], op0=ALU.mult, op1=ALU.subtract)
                done(ins, f"at{oc}")

            def peak_chunk(k):
                dve.wait_ge(fc1_loaded, 16)
                done(dve.tensor_reduce(peak_k[:, k:k + 1], wfull1[:, k, :], AX_X, ALU.max,
                                       apply_absolute_value=True), f"pk{k}")

            a_transposed(0)
            a_transposed(1)
            peak_chunk(0)
            peak_chunk(1)
            a_transposed(2)
            peak_chunk(2)
            peak_chunk(3)
            own("pk3")
            done(dve.tensor_tensor(peak_k[:, :], peak_k[:, :], colsb[:, HC:HC + KC], ALU.mult), "pkw")
            own("pkw")
            done(peak_of(4, peak_k[:, :]), "peaks1")
            a_transposed(3)
            dve.wait_ge(peaks_reduced, 2)
            exponents(1, peak_all[:, 4:5], 1)
            dve.tensor_scalar(scale(C_W1), bounds[:, 0:1], 2.0 ** -14, None, ALU.mult)
            done(dve.tensor_scalar(n2ws[:, :], colsb[:, HC:HC + KC], bounds[:, 4:5], 2.0 ** 14, ALU.mult, ALU.mult),
                 "scales1")
            x_stats(Tile(0, 0, 0, 0, 0), range(GT))
            aggregate(0, x_bn, x_aggr, 0)
            x_variance(0)

            def m_whole(i):
                dve.wait_ge(prep_a, A[f"m{i}"])
                odd = bank(M_BANKS[i] + 1)
                dve.tensor_tensor(m_full[:, i, 0:HALF], even_sb[:, i % 2, :], odd[:, 0:HALF], ALU.add)
                dve.tensor_tensor(m_full[:, i, C - 1:HALF - 1:-1], even_sb[:, i % 2, 1:HALF - 1],
                                  odd[:, 1:HALF - 1], ALU.subtract).then_inc(m_written, 1)
                dve.wait_ge(m_written, i + 1)
                done(peak_of(5 + i, m_full[:, i, :]), f"m{i}")

            def w1_low(k):
                dve.wait_ge(prep_a, A[f"high{k}"])
                done(dve.scalar_tensor_tensor(out=wsplit_k[:, 1, k, :], in0=wfull1[:, k, :],
                                              scalar=n2ws[:, k:k + 1], in1=wsplit_k[:, 0, k, :],
                                              op0=ALU.mult, op1=ALU.subtract), f"low{k}")

            w1_low(0)
            m_whole(0)
            x_shift(0, 0)
            w1_low(1)
            m_whole(1)
            m_whole(2)
            w1_low(2)
            m_whole(3)
            dve.wait_ge(peaks_reduced, 3)
            done(dve.tensor_reduce(bounds[:, 2:3], peak_all[:, 5:9], AX_X, ALU.max), "bound2")
            own("bound2")
            exponents(1, bounds[:, 2:3], 2)
            dve.tensor_scalar(scale(S_M), bounds[:, 4:5], 2.0 ** 14, None, ALU.mult)
            dve.tensor_scalar(scale(C_B), bounds[:, 4:5], 2.0 ** 14 * 2 * C, None, ALU.mult)
            done(dve.tensor_scalar(scale(C_M), bounds[:, 0:1], 2.0 ** -14 * 0.5 / C, None, ALU.mult), "scales2")
            own("scales2")
            m_flat = m_parts[:, :, :, :].rearrange("p s k n -> p s (k n)")
            m_src = m_full.rearrange("p k n -> p (k n)")
            done(dve.tensor_scalar(m_flat[:, 0, :], m_src, scale(S_M), None, ALU.mult), "mhigh")
            own("mhigh")
            done(dve.scalar_tensor_tensor(out=m_flat[:, 1, :], in0=m_src, scalar=scale(S_M), in1=m_flat[:, 0, :],
                                          op0=ALU.mult, op1=ALU.subtract), "mlow")

            def v_variance(g, meanwhile):
                dve.wait_ge(x1_rstd, g + 1)
                dve.tensor_tensor(va[:, 5, :], mv[:, 1, :, 1], va[:, 4, :], ALU.mult).then_inc(v_var0, 1)
                at = bass.ds(4 * g, GT)
                dve.tensor_copy(alpha1[:, at], va[:, 4, :])
                dve.wait_ge(v_var0, 3 * g + 1)
                dve.tensor_tensor(va[:, 5, :], va[:, 5, :], va[:, 4, :], ALU.mult).then_inc(v_var0, 1)
                dve.scalar_tensor_tensor(out=beta1[:, at], in0=mv[:, 1, :, 0], scalar=-1.0, in1=va[:, 4, :],
                                         op0=ALU.mult, op1=ALU.mult).then_inc(v_var0, 1)
                meanwhile()
                dve.wait_ge(v_var0, 3 * g + 3)
                dve.tensor_scalar(va[:, 5, :], va[:, 5, :], EPS, None, ALU.add).then_inc(v_var, 1)

            def u_coefs(g):
                dve.wait_ge(v_rstd, g + 1)
                at_least(dve, u_norm, 4 * g)
                dve.wait_ge(v_var0, 3 * g + 3)
                dve.tensor_tensor(va[:, 7, :], va[:, 4, :], va[:, 6, :], ALU.mult)
                dve.tensor_tensor(ubias[:, :], beta1[:, bass.ds(4 * g, GT)], va[:, 6, :], ALU.mult)\
                   .then_inc(u_coef, 1)

            def zt_low_part(t):
                if t.real:
                    dve.wait_ge(zt_high, t.n + 1)
                    dve.tensor_tensor(zt[:, t.j % 2, 1, :, :].rearrange("p k t -> p (k t)"), bank(t.j % 2),
                                      zt[:, t.j % 2, 0, :, :].rearrange("p k t -> p (k t)"), ALU.subtract)\
                       .then_inc(zt_low, 1)

            def u_low_part(t):
                if t.real:
                    dve.wait_ge(u_high, t.n + 1)
                    at = bass.ds(t.n, 1)
                    dve.tensor_tensor(u_all[:, :, 1, :, at],
                                      uring[:, t.j, :].rearrange("p (b c o) -> p b c o", b=BLOCKS, o=1),
                                      u_all[:, :, 0, :, at], ALU.subtract).then_inc(u_low, 1)

            def drained(t):
                if t.real and in_drain(t.n):
                    if is_last(t.g):
                        dve.wait_ge(last_weighted, t.j + 1)
                    else:
                        dve.wait_ge(u_norm, t.n + 1)
                        dve.tensor_tensor(uring[:, t.j, :], uring[:, t.j, :], w1s[:, :], ALU.mult)\
                           .then_inc(drain_weighted, 1)
                        dve.wait_ge(drain_weighted, t.n - DRAIN + 1)
                    dve.tensor_tensor(uring[:, t.j, :], uring[:, t.j, :], b1s[:, :], ALU.add)\
                       .then_inc(u_drained, 1)

            def split_bias():
                dve.tensor_scalar(bias_rest, half_bias[:, :], scale(C_B), None, ALU.mult).then_inc(bias_parted, 1)
                steps_done = 1
                for at, n in ((slice(0, P), 1), (slice(32, 64), 1), (slice(64, P), 2)):
                    for _ in range(n):
                        if at.start:
                            dve.wait_ge(bias_parted, steps_done)
                            dve.tensor_tensor(bias_rest[at, :], bias_rest[at, :], bias_parts[at, :], ALU.subtract)\
                               .then_inc(bias_parted, 1)
                            steps_done += 1
                        dve.wait_ge(bias_parted, steps_done)
                        dve.tensor_copy(bias_parts[at, :], bias_rest[at, :]).then_inc(bias_parted, 1)
                        steps_done += 1
                assert steps_done == BIAS_STEPS

            def slot(g, quad, q, j):
                before, after, later = [Tile(g, quad, q, j, d) for d in (-GT, GT, 2 * GT)]
                t = Tile(g, quad, q, j, -1)
                if t.real:
                    dve.wait_ge(ffn_psum, t.n + 1)
                    dve.scalar_tensor_tensor(out=xbuf[t.q][:, t.j, :], in0=bank(2 + t.j % 2), scalar=scale(C_M),
                                             in1=xbuf[t.q][:, t.j, :], op0=ALU.mult, op1=ALU.add)\
                       .then_inc(x1_ready, 1)
                zt_low_part(Tile(g, quad, q, j, 1))
                if isinstance(g, int) and (g, j) == (-1, 3):
                    split_bias()
                if t.real:
                    dve.wait_ge(x1_ready, t.n + 1)
                    ins = dve.bn_stats(bn[:, 1, t.j, :], xbuf[t.q][:, t.j, :])
                    if t.j == GT - 1:
                        ins.then_inc(x1_bn, 1)
                split = Tile(g, quad, q, j, -8)
                if j == 0:
                    following = after.real and not is_first(after.g)
                    if following:
                        x_stats(after, [2, 3])
                    if before.real:
                        aggregate(1, x1_bn, x1_aggr, before.g)
                    if following:
                        aggregate(0, x_bn, x_aggr, after.g)
                    if before.real:
                        variance(1, x1_aggr, x1_var, va[:, 3, :], before.g)
                    drained(Tile(g, quad, q, j, -7))
                    u_low_part(split)
                    if following:
                        x_variance(after.g)
                elif j == 1:
                    if after.real and not is_first(after.g):
                        x_shift(after.g, after.q)
                    if before.real:
                        v_variance(before.g, lambda: u_low_part(split))
                    else:
                        u_low_part(split)
                    drained(Tile(g, quad, q, j, -7))
                else:
                    if j == 2 and before.real:
                        u_coefs(before.g)
                    drained(Tile(g, quad, q, j, -7))
                    u_low_part(split)
                    if j == 3 and later.real:
                        x_stats(later, [0, 1])
                if is_first(g) and j == 1:
                    w1_low(3)
            each_tile(dve, slot)

            firsts = state_parts[:, :, :].rearrange("p i (c t) -> p i c t", t=PER_BATCH)[:, :, :, 0:1]
            dve.memset(firsts, 0.0).then_inc(state_zero, 1)

            def scan(o, i):
                dve.wait_ge(state_psum, o + 1)
                at_least(dve, state_low, o - 3)
                dve.tensor_tensor_scan(ring[:, i, :], carry[:, :], bank(i), 0.0, ALU.mult, ALU.add)\
                   .then_inc(state_scanned, 1)

            def low_part(o, i):
                dve.wait_ge(state_high, o + 1)
                src = ring[:, i, :].rearrange("p (c t) -> p c t", t=PER_BATCH)[NST:P, :, 0:PER_BATCH - 1]
                dst = state_parts[:, i % 2, :].rearrange("p (c t) -> p c t", t=PER_BATCH)[NST:P, :, 1:PER_BATCH]
                dve.tensor_tensor(dst, src, dst, ALU.subtract).then_inc(state_low, 1)

            def w2_peak(h):
                if h % 2 == 0:
                    dve.wait_ge(w2_raw[h // 2], 16)
                dve.tensor_reduce(w2_peak_cols[:, bass.ds(h, 1)], w2_full[:, bass.ds(h, 1), :], AX_XY, ALU.max,
                                  apply_absolute_value=True).then_inc(w2_peaks, 1)

            def w2_all_peaks():
                dve.wait_ge(w2_peaks, HC + 1)
                peak_of(9, w2_peak_cols)
                done(peak_of(10, b1p[:, :]), "peaks3")

            def w2_scales():
                dve.wait_ge(peaks_reduced, 4)
                dve.tensor_copy(bounds[:, 2:3], peak_all[:, 9:10])
                done(dve.scalar_tensor_tensor(out=bounds[:, 3:4], in0=peak_all[:, 4:5], scalar=float(C),
                                              in1=peak_all[:, 10:11], op0=ALU.mult, op1=ALU.add), "bound3")
                own("bound3")
                exponents(2, bounds[:, 2:4], 3)
                dve.tensor_scalar(scale(S_W2), bounds[:, 4:5], 2.0 ** 14, None, ALU.mult)
                dve.tensor_scalar(scale(S_H), bounds[:, 5:6], 2.0 ** 14, None, ALU.mult)
                done(dve.tensor_scalar(scale(C_2), bounds[:, 0:1], bounds[:, 1:2], 2.0 ** -28, ALU.mult,
                                       ALU.mult), "scales3")
                own("scales3")

            def w2_low_part(h):
                dve.wait_ge(w2_high, h + 1)
                dve.scalar_tensor_tensor(out=w2_sb[:, 1, bass.ds(h, 1), :], in0=w2_full[:, bass.ds(h, 1), :],
                                         scalar=scale(S_W2), in1=w2_sb[:, 0, bass.ds(h, 1), :],
                                         op0=ALU.mult, op1=ALU.subtract).then_inc(w2_low, 1)

            def quad_of_eights(q, first=False):
                for i in range(4):
                    scan(4 * q + i, i)
                    if not (first and i < 2):
                        low_part(4 * q + i - 2, (i - 2) % 4)
                    if isinstance(q, int) and PEAKS <= q < PEAKS + 4 and 4 * (q - PEAKS) + i >= 2:
                        w2_peak(4 * (q - PEAKS) + i - 2)

            quad_of_eights(0, first=True)
            with dve.Fori(1, PEAKS) as q:
                quad_of_eights(q)
            dve.wait_ge(b1n_loaded, 16)
            dve.tensor_tensor(b1p[:, :], b1n[:, :], colsb[:, 0:HC], ALU.add).then_inc(w2_peaks, 1)
            for q in range(PEAKS, PEAKS + 4):
                quad_of_eights(q)
            for i in range(4):
                scan(4 * SPLIT + i, i)
                low_part(4 * SPLIT + i - 2, (i - 2) % 4)
                if i == 0:
                    w2_peak(HC - 2)
                    w2_peak(HC - 1)
                    w2_all_peaks()
                if i == 1:
                    w2_scales()
            for q in range(SPLIT + 1, SPLIT + 5):
                for i in range(4):
                    scan(4 * q + i, i)
                    low_part(4 * q + i - 2, (i - 2) % 4)
                    if i == 0:
                        dve.wait_ge(y_stored[1][4 + q - SPLIT - 1], 16)
                    w2_low_part(4 * (q - SPLIT - 1) + i)
            with dve.Fori(SPLIT + 5, OBLOCKS // 4) as q:
                quad_of_eights(q)
            low_part(OBLOCKS - 2, 2)
            low_part(OBLOCKS - 1, 3)

            def mixed(g, j, pair, par):
                y = first_y if is_first(g) else ybuf
                if is_first(g):
                    last = slice(C - BLK, C)
                    dve.scalar_tensor_tensor(out=y[:, j, last], in0=first_x1[:, j, last], scalar=alpha1[:, j:j + 1],
                                             in1=area((BLOCKS - 1) * REG + j * BLK, BLK), op0=ALU.mult,
                                             op1=ALU.add).then_inc(xm_sum, 1)
                else:
                    if j == 0:
                        dve.wait_ge(yg_loaded, 16 * g)
                        dve.wait_ge(r_loaded[par], 16 * pair + 16 * par)
                    dve.scalar_tensor_tensor(out=y[:, j, :], in0=rbuf[par][:, j, :],
                                             scalar=alpha1[:, bass.ds(4 * g + j, 1)], in1=y[:, j, :],
                                             op0=ALU.mult, op1=ALU.add).then_inc(xm_sum, 1)
                dve.wait_ge(xm_sum, 4 * g + j + 1)
                ins = dve.bn_stats(bn[:, 0, j, :], y[:, j, :])
                if j == GT - 1:
                    ins.then_inc(xm_bn, 1)
                    aggregate(0, xm_bn, xm_aggr, g)
                    variance(0, xm_aggr, xm_var, va[:, 0, :], g)

            def mixed_shift(g):
                dve.wait_ge(xm_rstd, g + 1)
                if not is_first(g):
                    dve.wait_ge(z2_ready, 4 * g)
                dve.scalar_tensor_tensor(out=va[:, 2, :], in0=mv[:, 0, :, 0], scalar=-1.0, in1=va[:, 1, :],
                                         op0=ALU.mult, op1=ALU.mult).then_inc(xm_coef, 1)

            def residual(g, j, par):
                y, x1 = (first_y, first_x1) if is_first(g) else (ybuf, rbuf[par])
                dve.scalar_tensor_tensor(out=rbuf[par][:, j, :], in0=y[:, j, :],
                                         scalar=beta1[:, bass.ds(4 * g + j, 1)], in1=x1[:, j, :],
                                         op0=ALU.add, op1=ALU.add).then_inc(r_sum, 1)

            def g_low(g, j):
                dve.wait_ge(gt_high, 4 * g + j + 1)
                dve.tensor_tensor(gt[:, 1, :, j * P:(j + 1) * P], bank(2 + j % 2).rearrange("p (k t) -> p k t", k=KC),
                                  gt[:, 0, :, j * P:(j + 1) * P], ALU.subtract).then_inc(gt_low, 1)

            def z3_low(g, j):
                dve.wait_ge(z3t_high, 4 * g + j + 1)
                dve.tensor_tensor(z3t[:, j, 1, :, :].rearrange("p k t -> p (k t)"), bank(2 + j % 2),
                                  z3t[:, j, 0, :, :].rearrange("p k t -> p (k t)"), ALU.subtract)\
                   .then_inc(z3t_low, 1)

            def x2_shift(g):
                dve.wait_ge(x2_rstd, g + 1)
                dve.scalar_tensor_tensor(out=va[:, 5, :], in0=mv[:, 1, :, 0], scalar=-1.0, in1=va[:, 4, :],
                                         op0=ALU.mult, op1=ALU.mult).then_inc(x2_coef, 1)

            def x3(g, j, par):
                dve.wait_ge(ffn2_psum, 4 * g + j + 1)
                dve.wait_ge(x2b_ready, 4 * g + j + 1)
                dve.scalar_tensor_tensor(out=x2buf[par][:, j, :], in0=bank(6 + j % 2), scalar=scale(C_M),
                                         in1=x2buf[par][:, j, :], op0=ALU.mult, op1=ALU.add)\
                   .then_inc(x3_ready, 1)

            for j in range(GT):
                dve.wait_ge(first_loaded[j], 32)
                dve.scalar_tensor_tensor(out=first_y[:, j, 0:C - BLK], in0=first_x1[:, j, 0:C - BLK],
                                         scalar=alpha1[:, j:j + 1], in1=first_y[:, j, 0:C - BLK],
                                         op0=ALU.mult, op1=ALU.add).then_inc(first_mixed, 1)
            dve.wait_ge(y_staged, OBLOCKS)
            dve.wait_ge(first_mixed, GT)
            for j in range(GT):
                mixed(0, j, 0, 0)
            mixed_shift(0)
            for j in range(GT):
                residual(0, j, 0)
            for j in range(GT):
                g_low(0, j)

            def step(g, pair, par):
                if not is_first(g):
                    x2_shift(g - 1)
                for hc in range(HC):
                    dve.wait_ge(h_ready, HC * g + hc + 1)
                    dve.tensor_scalar(hid[:, 0, hc, :], h32[:, hc % 4, :], scale(S_H), None, ALU.mult)\
                       .then_inc(h_high, 1)
                    dve.wait_ge(h_high, HC * g + hc + 1)
                    dve.scalar_tensor_tensor(out=hid[:, 1, hc, :], in0=h32[:, hc % 4, :], scalar=scale(S_H),
                                             in1=hid[:, 0, hc, :], op0=ALU.mult, op1=ALU.subtract)\
                       .then_inc(h_low, 1)
                    if hc in (3, 5, 7, 9) and not is_first(g):
                        z3_low(g - 1, (hc - 3) // 2)
                    if not is_last(g):
                        if 1 <= hc < 5:
                            mixed(g + 1, hc - 1, pair + par, 1 - par)
                        if hc == 6:
                            mixed_shift(g + 1)
                        if 6 <= hc < 10:
                            residual(g + 1, hc - 6, 1 - par)
                for j in range(GT):
                    if not is_last(g):
                        g_low(g + 1, j)
                    if not is_first(g):
                        x3(g - 1, j, 1 - par)

                if not (isinstance(g, int) and g < 2):
                    dve.wait_ge(out_stored[par], 16 * pair)
                for j in range(GT):
                    dve.wait_ge(fc2_psum, 4 * g + j + 1)
                    dve.wait_ge(r_ready, 4 * g + j + 1)
                    dve.scalar_tensor_tensor(out=x2buf[par][:, j, :], in0=bank(4 + j % 2), scalar=scale(C_2),
                                             in1=rbuf[par][:, j, :], op0=ALU.mult, op1=ALU.add)\
                       .then_inc(x2_ready, 1)
                    dve.wait_ge(x2_ready, 4 * g + j + 1)
                    ins = dve.bn_stats(bn[:, 1, j, :], x2buf[par][:, j, :])
                ins.then_inc(x2_bn, 1)
                aggregate(1, x2_bn, x2_aggr, g)
                variance(1, x2_aggr, x2_var, va[:, 3, :], g)
            each_group(dve, step)
            x2_shift(GROUPS - 1)
            for j in range(GT + 2):
                if j < GT:
                    z3_low(GROUPS - 1, j)
                if j >= 2:
                    x3(GROUPS - 1, j - 2, 1)

        @block.tensor
        def _(pe):
            for oc in range(KC):
                if oc == 1:
                    pe.wait_ge(smalls_loaded, 16 * N_SMALLS)
                    pe.wait_ge(prep_a, A["e_taps"])
                    pe.wait_ge(pool_set, 12)
                    pe.matmul(bank(7), e_taps[0:NST, :], mix_s[0:NST, :], start=True, stop=False)
                    pe.matmul(bank(7), onehot, drow, start=False, stop=True).then_inc(prep_pe, 1)
                if oc >= 2:
                    pe.wait_ge(prep_v, V[f"at{oc - 2}"])
                for i, (w, f) in enumerate(((wr_sb, cos_sb), (wi_sb, sin_sb), (wr_sb, sin_sb), (wi_sb, cos_sb))):
                    if oc == 0 and i < 2:
                        pe.wait_ge(table_loaded[2 * i], 16)
                        pe.wait_ge(table_loaded[2 * i + 1], 16)
                    if oc == 1 and i == 3:
                        pe.wait_ge(prep_v, V["k_low"])
                    for k in range(KC):
                        last = pe.matmul(bank(4 * (oc % 2) + i)[:, 0:HALF], w[:, k, oc * P:(oc + 1) * P],
                                         f[:, k, :], start=(k == 0), stop=(k == KC - 1))
                last.then_inc(prep_pe, 1)
            pe.wait_ge(fc1_loaded, 16)
            pe.wait_ge(prep_v, V["at3"])
            for i in range(KC):
                if i == 3:
                    pe.wait_ge(prep_v, V["m0"])
                for odd, (a, f) in enumerate(((at_re, cos_sb), (at_im, sin_sb))):
                    for k in range(KC):
                        last = pe.matmul(bank(M_BANKS[i] + odd)[:, 0:HALF], a[:, k, i * P:(i + 1) * P],
                                         f[:, k, :], start=(k == 0), stop=(k == KC - 1))
                last.then_inc(prep_pe, 1)

            def bias(n):
                for k in range(KC):
                    last = pe.matmul(bank(4 + n)[0:1, :], colsb[:, HC + KC + k:HC + KC + k + 1],
                                     wfull1[:, k, n * C:(n + 1) * C], start=(k == 0), stop=(k == KC - 1))
                last.then_inc(prep_pe, 1)

            pe.wait_ge(prep_v, V["m1"])
            bias(0)
            bias(1)
            PASSES = ((0, 0), (0, 1), (1, 0))

            def transposes(dst, src, done):
                for k in range(KC):
                    last = pe.transpose(dst[:, k * P:(k + 1) * P], src[:, k * P:(k + 1) * P], ident[:, :])
                last.then_inc(done, 1)

            def ffn(dst, act_parts, done, bias=False, wait_for_bias=False):
                n = 0
                for k in range(KC):
                    for a, b in PASSES:
                        last = pe.matmul(dst, act_parts[:, a, k, :], m_parts[:, b, k, :], start=(n == 0),
                                         stop=(n == 3 * KC - 1 and not bias))
                        n += 1
                if bias:
                    if wait_for_bias:
                        pe.wait_ge(bias_parted, BIAS_STEPS)
                        pe.wait_ge(bias_ones, 4)
                    last = pe.matmul(dst, bias_rows, bias_parts, start=False, stop=True)
                last.then_inc(done, 1)

            pe.wait_ge(prep_v, V["m3"])

            def slot(g, quad, q, j):
                t = Tile(g, quad, q, j, 1)
                if t.real:
                    pe.wait_ge(z_ready, t.n + 1)
                    at_least(pe, zt_low, t.n - 1)
                    transposes(bank(t.j % 2), ring[:, t.j, :], zt_psum)
                t = Tile(g, quad, q, j, 0)
                if isinstance(t.n, int) and t.n == 0:
                    pe.wait_ge(prep_v, V["mlow"])
                if t.real:
                    pe.wait_ge(zt_high, t.n + 1)
                    pe.wait_ge(zt_low, t.n + 1)
                    at_least(pe, x1_ready, t.n - 1)
                    ffn(bank(2 + t.j % 2), zt[:, t.j % 2, :, :, :], ffn_psum, bias=True,
                        wait_for_bias=isinstance(t.n, int) and t.n == 0)
                if isinstance(g, int) and g == 0 and j in (0, 1):
                    bias(2 + j)
            each_tile(pe, slot)

            per_block = BLK // OC

            def u_part(o, part, channel, n):
                blk, place = divmod(o, per_block)
                at = ((blk * 2 + part) * BLK + place * OC + channel) * TILES
                return u_flat[:, at:at + n]

            def states(o, i):
                at_least(pe, state_scanned, o - 3)
                for n, (a, b) in enumerate(PASSES):
                    last = pe.matmul(bank(i), to_state[:, a, :], u_part(o, b, 0, OC * TILES),
                                     start=(n == 0), stop=(n == 2))
                last.then_inc(state_psum, 1)

            def inside(o, i):
                at_least(pe, y_staged, o - 3)
                for c in range(OC):
                    for n, (a, b) in enumerate(PASSES):
                        pe.matmul(bank(4 + i)[:, c * TILES:(c + 1) * TILES], taps[:, i, :, a, c],
                                  u_part(o, b, c, TILES), start=(c == 0 and n == 0), stop=False,
                                  skip_group_check=True)

            def between(o, i):
                pe.wait_ge(state_high, o + 1)
                pe.wait_ge(state_low, o + 1)
                for part in range(2):
                    last = pe.matmul(bank(4 + i), from_state[:, part, :], state_parts[:, i % 2, :], start=False,
                                     stop=(part == 1), skip_group_check=True)
                last.then_inc(y_psum, 1)

            pe.wait_ge(u_high, TILES)
            pe.wait_ge(u_low, TILES)
            for o in range(3):
                states(o, o)
            pe.wait_ge(state_zero, 1)
            for o in range(OBLOCKS):
                if o + 3 < OBLOCKS:
                    states(o + 3, (o + 3) % 4)
                if o in (0, 2):
                    pe.wait_ge(taps_zeroed, 1 + o // 2)
                pe.wait_ge(taps_loaded[o % 4], 32 * (o // 4) + 32)
                inside(o, o % 4)
                between(o, o % 4)

            def turn_z2(g, j):
                pe.wait_ge(z2_ready, 4 * g + j + 1)
                if is_first(g):
                    if j >= 2:
                        pe.wait_ge(gt_low, 4 * g + j - 1)
                elif j < 2:
                    if isinstance(g, int) and g == 1:
                        pe.wait_ge(gt_low, j + 3)
                    else:
                        pe.wait_ge(z3t_low, 4 * (g - 2) + j + 3)
                else:
                    pe.wait_ge(gt_low, 4 * g + j - 1)
                transposes(bank(2 + j % 2), (first_y if is_first(g) else ybuf)[:, j, :], gt_psum)

            def turn_z3(g, j):
                pe.wait_ge(z3_ready, 4 * g + j + 1)
                if j < 2 and is_last(g):
                    pe.wait_ge(z3t_low, 4 * (g - 1) + j + 3)
                elif j < 2:
                    pe.wait_ge(gt_low, 4 * g + j + 7)
                else:
                    pe.wait_ge(z3t_low, 4 * g + j - 1)
                transposes(bank(2 + j % 2), z3[:, j, :], z3t_psum)

            def second_ffn(g, j):
                pe.wait_ge(z3t_high, 4 * g + j + 1)
                pe.wait_ge(z3t_low, 4 * g + j + 1)
                if not (is_first(g) and j < 2):
                    pe.wait_ge(x3_ready, 4 * g + j - 1)
                ffn(bank(6 + j % 2), z3t[:, j, :, :, :], ffn2_psum)

            for j in range(GT):
                turn_z2(0, j)
            pe.wait_ge(w1_loaded, 16 * 8)

            def step(g, pair, par):
                pe.wait_ge(gt_high, 4 * g + 4)
                pe.wait_ge(gt_low, 4 * g + 4)
                for hc in range(HC):
                    if not (is_first(g) and hc < 2):
                        pe.wait_ge(h_ready, HC * g + hc - 1)
                    n = 0
                    for k in range(KC):
                        for a, b in PASSES:
                            last = pe.matmul(bank(hc % 2), w1_sb[:, a, k, hc * P:(hc + 1) * P], gt[:, b, k, :],
                                             start=(n == 0), stop=(n == 3 * KC - 1))
                            n += 1
                    last.then_inc(fc1_psum, 1)
                    if hc in (3, 5, 7, 9) and not is_first(g):
                        turn_z3(g - 1, (hc - 3) // 2)
                for j in range(GT):
                    if not is_last(g):
                        turn_z2(g + 1, j)
                    if not is_first(g):
                        second_ffn(g - 1, j)
                if is_first(g):
                    pe.wait_ge(w2_low, HC)
                for j in range(GT):
                    if not (is_first(g) and j < 2):
                        pe.wait_ge(x2_ready, 4 * g + j - 1)
                    n = 0
                    for hc in range(HC):
                        if j == 0:
                            pe.wait_ge(h_low, HC * g + hc + 1)
                        for a, b in PASSES:
                            last = pe.matmul(bank(4 + j % 2), hid[:, a, hc, j * P:(j + 1) * P],
                                             w2_sb[:, b, hc, :], start=(n == 0), stop=(n == 3 * HC - 1))
                            n += 1
                    last.then_inc(fc2_psum, 1)
            each_group(pe, step)
            for j in range(GT):
                turn_z3(GROUPS - 1, j)
                if j >= 1:
                    second_ffn(GROUPS - 1, j - 1)
            second_ffn(GROUPS - 1, GT - 1)


def kernel(**inputs):
    import concourse.bacc as bacc
    from concourse.bass_utils import run_bass_kernel_spmd

    def get(name):
        return np.asarray(inputs["L0_" + name])

    def by_partition(v, n):
        return np.ascontiguousarray(v.reshape(n, P).T)

    turn = np.outer(np.arange(C), np.arange(C)) % C * (2 * np.pi / C)
    arrays = {
        "x": get("attn_x").reshape(TILES * P, C),
        "wr": get("ffn_w_freq_real"), "wi": get("ffn_w_freq_imag"), "ffn_bias": get("ffn_bias"),
        "fc1t": get("attn_fc1_w").T, "fc2t": get("attn_fc2_w").T,
        "fc1b": by_partition(get("attn_fc1_b"), HC), "fc2b": get("attn_fc2_b"),
        "n1w": get("attn_norm1_w"), "n1b": get("attn_norm1_b"),
        "n2w": by_partition(get("attn_norm2_w"), KC), "n2b": by_partition(get("attn_norm2_b"), KC),
        "dskip": get("attn_D").reshape(1, C), "mixt": get("attn_mix").T,
        "log_tau": get("attn_log_tau").reshape(NST, 1), "log_dt": get("attn_log_dt").reshape(1, 1),
        "cos_t": np.cos(turn[:, :HALF]).astype(np.float32), "sin_t": np.sin(turn[:, :HALF]).astype(np.float32),
    }
    nc = bacc.Bacc("TRN2", target_bir_lowering=False, num_devices=1)
    feed, aps = {}, {}
    for name, a in arrays.items():
        feed["in_" + name] = a = np.ascontiguousarray(a)
        aps[name] = nc.dram_tensor("in_" + name, a.shape, mybir.dt.from_np(a.dtype), kind="ExternalInput").ap()
    out = nc.dram_tensor("out", (TILES * P, C), F32, kind="ExternalOutput").ap()
    build(nc, out=out, **aps)
    r = run_bass_kernel_spmd(nc, [feed], core_ids=[0])
    return r.results[0]["out"].reshape(BATCH, TIME, C)
```
